# Optimizing a Trainium2 kernel written in Bass

```python
import numpy as np
import jax
import jax.numpy as jnp

def _softmax(x, axis=-1):
    return jax.nn.softmax(x, axis=axis)

def _gelu(x):
    return jax.nn.gelu(x, approximate=True)

def _silu(x):
    return jax.nn.silu(x)

def _sigmoid(x):
    return jax.nn.sigmoid(x)

def _layernorm(x, axis=-1, eps=1e-05):
    m = jnp.mean(x, axis=axis, keepdims=True)
    v = jnp.var(x, axis=axis, keepdims=True)
    return (x - m) / jnp.sqrt(v + eps)

def _scatter_add(tgt, idx, src, axis=0):
    return tgt.at[idx].add(src)

def _segment_sum(src, seg, n):
    return jax.ops.segment_sum(src, seg, n)
kernel_name = 'mk_sandwich_d2_jaxref_r8_0ec29f'

def setup_inputs(seed: int=0):
    np.random.seed(seed)
    _w = jnp.asarray

    def _L0_attn_setup():
        import jax, jax.numpy as jnp
        import numpy as np
        B, S, HID = (1, 256, 256)
        H = 16
        Q_LORA, KV_LORA = (96, 64)
        D_NOPE, D_ROPE, D_V = (128, 64, 128)
        D_QK = D_NOPE + D_ROPE
        THETA = 10000.0
        EPS = 1e-06

        def _rms_norm(x, w, eps=EPS):
            var = jnp.mean(x * x, axis=-1, keepdims=True)
            return x * jax.lax.rsqrt(var + eps) * w

        def _rotate_half(x):
            x1 = x[..., ::2]
            x2 = x[..., 1::2]
            return jnp.stack((-x2, x1), axis=-1).reshape(x.shape)

        def _rope_cache(seq_len, dim, theta=THETA):
            inv_freq = 1.0 / theta ** (jnp.arange(0, dim, 2, dtype=jnp.float32) / dim)
            pos = jnp.arange(seq_len, dtype=jnp.float32)
            freqs = jnp.outer(pos, inv_freq)
            emb = jnp.concatenate((freqs, freqs), -1)
            return (jnp.cos(emb), jnp.sin(emb))

        def _apply_rope(x, cos, sin):
            cos = cos[None, None]
            sin = sin[None, None]
            return x * cos + _rotate_half(x) * sin
        key = jax.random.key(seed)
        ks = jax.random.split(key, 8)
        s = lambda fin: 1.0 / np.sqrt(fin)
        return {'x': jax.random.normal(ks[0], (B, S, HID), jnp.float32), 'w_qa': jax.random.normal(ks[1], (HID, Q_LORA), jnp.float32) * s(HID), 'q_a_norm_w': jnp.ones((Q_LORA,), jnp.float32), 'w_qb': jax.random.normal(ks[2], (Q_LORA, H * D_QK), jnp.float32) * s(Q_LORA), 'w_kva': jax.random.normal(ks[3], (HID, KV_LORA + D_ROPE), jnp.float32) * s(HID), 'kv_a_norm_w': jnp.ones((KV_LORA,), jnp.float32), 'w_kvb': jax.random.normal(ks[4], (KV_LORA, H * (D_NOPE + D_V)), jnp.float32) * s(KV_LORA), 'w_o': jax.random.normal(ks[5], (H * D_V, HID), jnp.float32) * s(H * D_V)}
    _L0_attn_in = _L0_attn_setup()

    def _L0_ffn_setup():
        import jax, jax.numpy as jnp
        import numpy as np
        B, S, H = (2, 256, 256)
        E, K, F = (32, 4, 176)
        FS = 704
        EPS = 1e-06
        CAP = 128
        key = jax.random.key(seed)
        ks = jax.random.split(key, 10)
        s = 0.02
        return {'hidden_states': jax.random.normal(ks[0], (B, S, H), jnp.float32), 'w_norm': 1.0 + 0.02 * jax.random.normal(ks[1], (H,), jnp.float32), 'w_router': s * jax.random.normal(ks[2], (H, E), jnp.float32), 'w_gate': s * jax.random.normal(ks[3], (E, H, F), jnp.float32), 'w_up': s * jax.random.normal(ks[4], (E, H, F), jnp.float32), 'w_down': s * jax.random.normal(ks[5], (E, F, H), jnp.float32), 'sw_gate': s * jax.random.normal(ks[6], (H, FS), jnp.float32), 'sw_up': s * jax.random.normal(ks[7], (H, FS), jnp.float32), 'sw_down': s * jax.random.normal(ks[8], (FS, H), jnp.float32), 'w_shared_gate': s * jax.random.normal(ks[9], (H, 1), jnp.float32)}
    _L0_ffn_in = _L0_ffn_setup()

    def _L1_attn_setup():
        import jax, jax.numpy as jnp
        import numpy as np
        D_MODEL = 256
        N_HEADS = 16
        HEAD_DIM = D_MODEL // N_HEADS
        NEG_BIG = -1e+30
        key = jax.random.key(seed)
        ks = jax.random.split(key, 9)
        B, T = (2, 256)
        s_in = 1.0 / np.sqrt(D_MODEL)
        s_hd = 1.0 / np.sqrt(D_MODEL)
        return {'q_input': jax.random.normal(ks[0], (B, T, D_MODEL), dtype=jnp.float32), 'Wq': jax.random.normal(ks[1], (D_MODEL, D_MODEL), dtype=jnp.float32) * s_in, 'bq': jnp.zeros((D_MODEL,), dtype=jnp.float32), 'Wk': jax.random.normal(ks[2], (HEAD_DIM, D_MODEL), dtype=jnp.float32) * s_in, 'bk': jnp.zeros((HEAD_DIM,), dtype=jnp.float32), 'Wv': jax.random.normal(ks[3], (HEAD_DIM, D_MODEL), dtype=jnp.float32) * s_in, 'bv': jnp.zeros((HEAD_DIM,), dtype=jnp.float32), 'Wo': jax.random.normal(ks[4], (D_MODEL, D_MODEL), dtype=jnp.float32) * s_hd, 'bo': jnp.zeros((D_MODEL,), dtype=jnp.float32)}
    _L1_attn_in = _L1_attn_setup()

    def _L1_ffn_setup():
        import jax, jax.numpy as jnp
        import numpy as np
        HIDDEN = 256
        INTER = 1024
        COMPRESSION = 128.9

        def _n_ctrl(out_size, in_size):
            return max(16, int(out_size * in_size / COMPRESSION))

        def _catmull_rom_grid(n_ctrl, n_samples):
            t = np.linspace(0.0, n_ctrl - 1.0, n_samples, dtype=np.float64)
            i = np.clip(np.floor(t).astype(np.int64), 0, n_ctrl - 2)
            f = (t - i).astype(np.float32)
            idx = np.stack([np.clip(i + k, 0, n_ctrl - 1) for k in (-1, 0, 1, 2)], axis=0)
            return (jnp.asarray(idx.astype(np.int32)), jnp.asarray(f))

        def spline_reconstruct(control_points, out_size, in_size):
            n = out_size * in_size
            idx, f = _catmull_rom_grid(control_points.shape[0], n)
            p0, p1, p2, p3 = (control_points[idx[0]], control_points[idx[1]], control_points[idx[2]], control_points[idx[3]])
            f2 = f * f
            f3 = f2 * f
            w = 0.5 * (2.0 * p1 + (p2 - p0) * f + (2.0 * p0 - 5.0 * p1 + 4.0 * p2 - p3) * f2 + (3.0 * p1 - p0 - 3.0 * p2 + p3) * f3)
            return w.reshape(out_size, in_size)
        key = jax.random.key(seed)
        k0, k1, k2, k3 = jax.random.split(key, 4)
        hidden_states = jax.random.normal(k0, (4, 256, HIDDEN), dtype=jnp.float32)
        gate_cp = jax.random.normal(k1, (_n_ctrl(INTER, HIDDEN),), dtype=jnp.float32) * 0.02
        up_cp = jax.random.normal(k2, (_n_ctrl(INTER, HIDDEN),), dtype=jnp.float32) * 0.02
        down_cp = jax.random.normal(k3, (_n_ctrl(HIDDEN, INTER),), dtype=jnp.float32) * 0.02
        return {'hidden_states': hidden_states, 'gate_cp': gate_cp, 'up_cp': up_cp, 'down_cp': down_cp}
    _L1_ffn_in = _L1_ffn_setup()
    _d = {'L0_attn_x': _L0_attn_in['x'], 'L0_attn_w_qa': _L0_attn_in['w_qa'], 'L0_attn_q_a_norm_w': _L0_attn_in['q_a_norm_w'], 'L0_attn_w_qb': _L0_attn_in['w_qb'], 'L0_attn_w_kva': _L0_attn_in['w_kva'], 'L0_attn_kv_a_norm_w': _L0_attn_in['kv_a_norm_w'], 'L0_attn_w_kvb': _L0_attn_in['w_kvb'], 'L0_attn_w_o': _L0_attn_in['w_o'], 'L0_ffn_w_norm': _L0_ffn_in['w_norm'], 'L0_ffn_w_router': _L0_ffn_in['w_router'], 'L0_ffn_w_gate': _L0_ffn_in['w_gate'], 'L0_ffn_w_up': _L0_ffn_in['w_up'], 'L0_ffn_w_down': _L0_ffn_in['w_down'], 'L0_ffn_sw_gate': _L0_ffn_in['sw_gate'], 'L0_ffn_sw_up': _L0_ffn_in['sw_up'], 'L0_ffn_sw_down': _L0_ffn_in['sw_down'], 'L0_ffn_w_shared_gate': _L0_ffn_in['w_shared_gate'], 'L1_attn_Wq': _L1_attn_in['Wq'], 'L1_attn_bq': _L1_attn_in['bq'], 'L1_attn_Wk': _L1_attn_in['Wk'], 'L1_attn_bk': _L1_attn_in['bk'], 'L1_attn_Wv': _L1_attn_in['Wv'], 'L1_attn_bv': _L1_attn_in['bv'], 'L1_attn_Wo': _L1_attn_in['Wo'], 'L1_attn_bo': _L1_attn_in['bo'], 'L1_ffn_gate_cp': _L1_ffn_in['gate_cp'], 'L1_ffn_up_cp': _L1_ffn_in['up_cp'], 'L1_ffn_down_cp': _L1_ffn_in['down_cp']}
    _x0 = _d['L0_attn_x']
    _d['L0_attn_x'] = jax.random.normal(jax.random.fold_in(jax.random.key(seed), 1), (8, 256, 256), dtype=_x0.dtype)
    del _x0
    return _d

def reference(L0_attn_x, L0_attn_w_qa, L0_attn_q_a_norm_w, L0_attn_w_qb, L0_attn_w_kva, L0_attn_kv_a_norm_w, L0_attn_w_kvb, L0_attn_w_o, L0_ffn_w_norm, L0_ffn_w_router, L0_ffn_w_gate, L0_ffn_w_up, L0_ffn_w_down, L0_ffn_sw_gate, L0_ffn_sw_up, L0_ffn_sw_down, L0_ffn_w_shared_gate, L1_attn_Wq, L1_attn_bq, L1_attn_Wk, L1_attn_bk, L1_attn_Wv, L1_attn_bv, L1_attn_Wo, L1_attn_bo, L1_ffn_gate_cp, L1_ffn_up_cp, L1_ffn_down_cp):

    def _L0_attn_ref(x, w_qa, q_a_norm_w, w_qb, w_kva, kv_a_norm_w, w_kvb, w_o):
        import jax, jax.numpy as jnp
        import numpy as np
        B, S, HID = (1, 256, 256)
        H = 16
        Q_LORA, KV_LORA = (96, 64)
        D_NOPE, D_ROPE, D_V = (128, 64, 128)
        D_QK = D_NOPE + D_ROPE
        THETA = 10000.0
        EPS = 1e-06

        def _rms_norm(x, w, eps=EPS):
            var = jnp.mean(x * x, axis=-1, keepdims=True)
            return x * jax.lax.rsqrt(var + eps) * w

        def _rotate_half(x):
            x1 = x[..., ::2]
            x2 = x[..., 1::2]
            return jnp.stack((-x2, x1), axis=-1).reshape(x.shape)

        def _rope_cache(seq_len, dim, theta=THETA):
            inv_freq = 1.0 / theta ** (jnp.arange(0, dim, 2, dtype=jnp.float32) / dim)
            pos = jnp.arange(seq_len, dtype=jnp.float32)
            freqs = jnp.outer(pos, inv_freq)
            emb = jnp.concatenate((freqs, freqs), -1)
            return (jnp.cos(emb), jnp.sin(emb))

        def _apply_rope(x, cos, sin):
            cos = cos[None, None]
            sin = sin[None, None]
            return x * cos + _rotate_half(x) * sin
        b, seq, _ = x.shape
        q = _rms_norm(x @ w_qa, q_a_norm_w) @ w_qb
        q = q.reshape(b, seq, H, D_QK).transpose(0, 2, 1, 3)
        q_nope, q_rope = (q[..., :D_NOPE], q[..., D_NOPE:])
        kv = x @ w_kva
        c_kv, k_rope = (kv[..., :KV_LORA], kv[..., KV_LORA:])
        kv_up = _rms_norm(c_kv, kv_a_norm_w) @ w_kvb
        kv_up = kv_up.reshape(b, seq, H, D_NOPE + D_V).transpose(0, 2, 1, 3)
        k_nope, v = (kv_up[..., :D_NOPE], kv_up[..., D_NOPE:])
        cos, sin = _rope_cache(seq, D_ROPE)
        q_rope = _apply_rope(q_rope, cos, sin)
        k_rope = _apply_rope(k_rope[:, None], cos, sin)
        k_rope = jnp.broadcast_to(k_rope, (b, H, seq, D_ROPE))
        q_full = jnp.concatenate((q_nope, q_rope), -1)
        k_full = jnp.concatenate((k_nope, k_rope), -1)
        scale = 1.0 / np.sqrt(D_QK)
        scores = jnp.einsum('bhsd,bhtd->bhst', q_full, k_full) * scale
        mask = jnp.tril(jnp.ones((seq, seq), bool))
        scores = jnp.where(mask[None, None], scores, jnp.finfo(scores.dtype).min)
        attn = jax.nn.softmax(scores, axis=-1)
        out = jnp.einsum('bhst,bhtd->bhsd', attn, v)
        out = out.transpose(0, 2, 1, 3).reshape(b, seq, H * D_V)
        return out @ w_o

    def _L0_ffn_ref(hidden_states, w_norm, w_router, w_gate, w_up, w_down, sw_gate, sw_up, sw_down, w_shared_gate):
        import jax, jax.numpy as jnp
        import numpy as np
        B, S, H = (2, 256, 256)
        E, K, F = (32, 4, 176)
        FS = 704
        EPS = 1e-06
        CAP = 128
        inp = hidden_states
        xf = inp.astype(jnp.float32)
        var = jnp.mean(xf * xf, axis=-1, keepdims=True)
        x = (w_norm * (xf * jax.lax.rsqrt(var + EPS))).astype(inp.dtype)
        Bq, Sq, Hq = x.shape
        x = x.reshape(-1, Hq)
        T = Bq * Sq
        logits = x @ w_router
        probs = jax.nn.softmax(logits.astype(jnp.float32), axis=-1)
        w_topk, sel = jax.lax.top_k(probs, K)
        w_topk = w_topk.astype(x.dtype)
        flat_e = sel.reshape(-1)
        order = jnp.argsort(flat_e)
        sorted_e = flat_e[order]
        counts = jnp.zeros((E,), jnp.int32).at[flat_e].add(1)
        starts = jnp.cumsum(counts) - counts
        pos = jnp.arange(T * K) - starts[sorted_e]
        tok = order // K
        valid = pos < CAP
        dest = jnp.where(valid, pos, CAP)
        buf = jnp.zeros((E, CAP + 1, Hq), x.dtype).at[sorted_e, dest].set(x[tok])
        buf = buf[:, :CAP]
        g = jnp.einsum('ech,ehf->ecf', buf, w_gate)
        u = jnp.einsum('ech,ehf->ecf', buf, w_up)
        y = jnp.einsum('ecf,efh->ech', jax.nn.silu(g) * u, w_down)
        wv = w_topk.reshape(-1)[order] * valid.astype(x.dtype)
        gath = y[sorted_e, jnp.minimum(pos, CAP - 1)]
        out = jnp.zeros((T, Hq), x.dtype).at[tok].add(gath * wv[:, None])
        sh = jax.nn.silu(x @ sw_gate) * (x @ sw_up) @ sw_down
        sh = jax.nn.sigmoid(x @ w_shared_gate) * sh
        out = out + sh
        return inp + out.reshape(Bq, Sq, Hq)

    def _L1_attn_ref(q_input, Wq, bq, Wk, bk, Wv, bv, Wo, bo):
        import jax, jax.numpy as jnp
        import numpy as np
        D_MODEL = 256
        N_HEADS = 16
        HEAD_DIM = D_MODEL // N_HEADS
        NEG_BIG = -1e+30
        B, T, _ = q_input.shape
        scale = 1.0 / np.sqrt(HEAD_DIM)
        q = (q_input @ Wq.T + bq).reshape(B, T, N_HEADS, HEAD_DIM).transpose(0, 2, 1, 3)
        k = q_input @ Wk.T + bk
        v = q_input @ Wv.T + bv
        pos = jnp.arange(T)
        mask = pos[None, :] < pos[:, None]
        scores = jnp.einsum('bhtd,bsd->bhts', q, k) * scale
        scores = jnp.where(mask[None, None, :, :], scores, NEG_BIG)
        attn = jax.nn.softmax(scores, axis=-1)
        row_valid = jnp.any(mask, axis=-1)
        attn = attn * row_valid[None, None, :, None].astype(attn.dtype)
        out = jnp.einsum('bhts,bsd->bhtd', attn, v)
        out = out.transpose(0, 2, 1, 3).reshape(B, T, D_MODEL)
        out = out @ Wo.T + bo
        return out

    def _L1_ffn_ref(hidden_states, gate_cp, up_cp, down_cp):
        import jax, jax.numpy as jnp
        import numpy as np
        HIDDEN = 256
        INTER = 1024
        COMPRESSION = 128.9

        def _n_ctrl(out_size, in_size):
            return max(16, int(out_size * in_size / COMPRESSION))

        def _catmull_rom_grid(n_ctrl, n_samples):
            t = np.linspace(0.0, n_ctrl - 1.0, n_samples, dtype=np.float64)
            i = np.clip(np.floor(t).astype(np.int64), 0, n_ctrl - 2)
            f = (t - i).astype(np.float32)
            idx = np.stack([np.clip(i + k, 0, n_ctrl - 1) for k in (-1, 0, 1, 2)], axis=0)
            return (jnp.asarray(idx.astype(np.int32)), jnp.asarray(f))

        def spline_reconstruct(control_points, out_size, in_size):
            n = out_size * in_size
            idx, f = _catmull_rom_grid(control_points.shape[0], n)
            p0, p1, p2, p3 = (control_points[idx[0]], control_points[idx[1]], control_points[idx[2]], control_points[idx[3]])
            f2 = f * f
            f3 = f2 * f
            w = 0.5 * (2.0 * p1 + (p2 - p0) * f + (2.0 * p0 - 5.0 * p1 + 4.0 * p2 - p3) * f2 + (3.0 * p1 - p0 - 3.0 * p2 + p3) * f3)
            return w.reshape(out_size, in_size)
        gate_w = spline_reconstruct(gate_cp, INTER, HIDDEN)
        up_w = spline_reconstruct(up_cp, INTER, HIDDEN)
        down_w = spline_reconstruct(down_cp, HIDDEN, INTER)
        gate = jnp.einsum('bsh,ih->bsi', hidden_states, gate_w)
        up = jnp.einsum('bsh,ih->bsi', hidden_states, up_w)
        inter = jax.nn.silu(gate) * up
        return jnp.einsum('bsi,hi->bsh', inter, down_w)
    x = L0_attn_x
    x = x + _layernorm(_L0_attn_ref(_layernorm(x, axis=-1), L0_attn_w_qa, L0_attn_q_a_norm_w, L0_attn_w_qb, L0_attn_w_kva, L0_attn_kv_a_norm_w, L0_attn_w_kvb, L0_attn_w_o), axis=-1)
    x = x + _layernorm(_L0_ffn_ref(_layernorm(x, axis=-1), L0_ffn_w_norm, L0_ffn_w_router, L0_ffn_w_gate, L0_ffn_w_up, L0_ffn_w_down, L0_ffn_sw_gate, L0_ffn_sw_up, L0_ffn_sw_down, L0_ffn_w_shared_gate), axis=-1)
    x = x + _layernorm(_L1_attn_ref(_layernorm(x, axis=-1), L1_attn_Wq, L1_attn_bq, L1_attn_Wk, L1_attn_bk, L1_attn_Wv, L1_attn_bv, L1_attn_Wo, L1_attn_bo), axis=-1)
    x = x + _layernorm(_L1_ffn_ref(_layernorm(x, axis=-1), L1_ffn_gate_cp, L1_ffn_up_cp, L1_ffn_down_cp), axis=-1)
    return x

_drawn_inputs = setup_inputs


def setup_inputs(seed=0):
    import zlib

    import numpy as np

    out = dict(_drawn_inputs(seed))
    spreads = {'L0_attn_q_a_norm_w': (1.0, 0.2),
     'L0_attn_kv_a_norm_w': (1.0, 0.2),
     'L1_attn_bq': (0.0, 0.423),
     'L1_attn_bk': (0.0, 0.8),
     'L1_attn_bv': (0.0, 0.1),
     'L1_attn_bo': (0.0, 0.1)}
    factors = {'L0_ffn_w_norm': 8.0,
     'L0_ffn_w_router': 8.0,
     'L0_ffn_w_gate': 8.0,
     'L0_ffn_w_up': 8.0,
     'L0_ffn_w_down': 8.0,
     'L0_ffn_sw_gate': 8.0,
     'L0_ffn_sw_up': 8.0,
     'L0_ffn_sw_down': 8.0,
     'L0_ffn_w_shared_gate': 8.0}
    for name, (base, spread) in spreads.items():
        noise = np.random.default_rng([zlib.crc32(name.encode()), seed]).standard_normal(out[name].shape)
        drawn = base * np.exp(spread * noise) if base else spread * noise
        out[name] = jnp.asarray(drawn.astype(out[name].dtype))
    for name, factor in factors.items():
        out[name] = (out[name] * factor).astype(out[name].dtype)
    return out
```

```python
from contextlib import ExitStack

import numpy as np
import concourse.bass as bass
from concourse import mybir

F32 = mybir.dt.float32
BF16 = mybir.dt.bfloat16
I32 = mybir.dt.int32
U32 = mybir.dt.uint32
ALU = mybir.AluOpType
ACT = mybir.ActivationFunctionType
AX = mybir.AxisListType

P = 128
BATCH, SEQ, D = 8, 256, 256
TOK = BATCH * SEQ
TILES = TOK // P
KD = D // P
LN_EPS = 1e-5
RMS_EPS = 1e-6
NEG = -1e30

H0 = 16
PAIRS = H0 // 2
QL, KVL = 96, 64
NOPE, ROPE, DV = 128, 64, 128
SCALE0 = 1.0 / float(np.sqrt(NOPE + ROPE))
LAT = QL + KVL + 2 * ROPE
CAUSAL = P + SEQ

E0, TOPK, FE, FS, CAP = 32, 4, 176, 704, 128
FEC, FEK = 2, FE // 2
FSC = -(-FS // P)
FSP = FSC * P
ROW = D + E0
SLOTS = E0 * CAP
TABLE = SLOTS + TILES * E0 * P
WEXP = 2 * KD * FE + FEC * D
PREP = 2 * QL + 4 * KVL + 2 * D

H1, HD1 = 16, 16
SCALE1 = 1.0 / float(np.sqrt(HD1))
WC = 1596
IC = 8

INTER = 1024
NCTRL = 2033
SPAN = 129
ROWS = 16
ALT = 16
SPLINE = P * ROWS * SPAN


class Tally:

    def __init__(self, eng, sem):
        self.eng, self.sem, self.base, self.k, self.outer = eng, sem, 0, 0, []

    def mark(self, ins):
        ins.then_inc(self.sem, 1)
        self.k += 1

    def wait(self):
        self.eng.wait_ge(self.sem, self.base + self.k)

    def link(self, ins):
        self.mark(ins)
        self.wait()

    def hold(self):
        self.wait()
        self.mark(self.eng.nop())

    def enter(self, i, per):
        self.outer.append((self.base, self.k, per))
        self.base, self.k = self.base + self.k + i * per, 0

    def leave(self, n):
        base, k, per = self.outer.pop()
        assert self.k == per, (self.k, per)
        self.base, self.k = base, k + n * per


def build_program(nc, T, out, phases=4):
    ctx = ExitStack()
    with ctx:
        def sb(name, shape, dt=F32):
            return ctx.enter_context(nc.sbuf_tensor(name, list(shape), dt))

        def sem(name):
            return ctx.enter_context(nc.semaphore(name))

        ident = sb("ident", [P, P])
        cst = sb("cst", [P, 5, P])
        cbf = sb("cbf", [P, 5, P], BF16)
        zbf = sb("zbf", [P, 512], BF16)
        ident_bf, causal_bf, strict_bf, upper_bf, ones_bf = (cbf[:, i, :] for i in range(5))
        mhalf = sb("mhalf", [P, 4])
        vecs = sb("vecs", [P, KVL + 2])
        X = sb("X", [P, TILES, D])
        R0 = sb("R0", [P, KD * TOK])
        R1 = sb("R1", [P, TILES * D])
        R2 = sb("R2", [P, TILES * ROW])
        R3 = sb("R3", [P, PAIRS * (3 * P + D)])
        R4 = sb("R4", [P, 3 * KD * INTER])
        R5 = sb("R5", [P, 2 * WEXP])
        Y = R1[:, :].rearrange("p (t n) -> p t n", t=TILES)
        stats = sb("stats", [P, 2, 6])
        mv = sb("mv", [P, 2, 2])
        rstd = sb("rstd", [P, 2])
        lnb = sb("lnb", [P, 2, D])
        hbuf = sb("hbuf", [P, 2, D])
        hTs = sb("hTs", [P, 2, KD, P])
        sil = sb("sil", [P, 2, 512])
        sqj = sil[:, :, 0:D]
        R6 = sb("R6", [P, 2176])
        rope_q = R6[:, 0:512].rearrange("p (a t) -> p a t", a=2)
        rope_k = R6[:, 512:768].rearrange("p (t a n) -> p t a n", t=KD, a=2)
        w_lat = R6[:, 768:1344].rearrange("p (k n) -> p k n", k=KD)
        Wq = R3[0:QL, 0:PAIRS * 3 * P].rearrange("p (a k m) -> p a k m", a=PAIRS, k=3)
        Wvo = R3[:, PAIRS * 3 * P:].rearrange("p (a n) -> p a n", a=PAIRS)
        wprep = R5[:, 0:2 * PREP].rearrange("p (u n) -> p u n", u=2)
        ms = sb("ms", [P, 2, 2])
        qn = R6[:, 1344:1536].rearrange("p (u n) -> p u n", u=2)
        kst = R6[:, 1536:1920].rearrange("p (u a n) -> p u a n", u=2, a=3)
        kr2 = R6[:, 1920:2176].rearrange("p (u a n) -> p u a n", u=2, a=2)
        kTa = R0[:, 0:TOK]
        kTb = R0[:, TOK:2 * TOK]
        qlatT = R2[0:QL, 0:TOK]
        ckv = R2[:, TOK:TOK + TILES * KVL].rearrange("p (t n) -> p t n", t=TILES)
        wst = sb("wst", [QL, 2, 3, P])
        rmul = sb("rmul", [P, 2, 2, SEQ])
        qT = sb("qT", [P, 2, 2, SEQ])
        nmax = sb("nmax", [P, 2, 2, 2])
        Pr = sb("Pr", [P, 2, 2, CAUSAL])
        sums = sb("sums", [P, 2, 2, 2])
        rsum = sb("rsum", [P, 2, 2])
        PTs = sb("PTs", [P, 2, CAUSAL])
        o_sb = sb("o_sb", [P, 2, P])
        oT_sb = sb("oT_sb", [P, SEQ])
        w_rt = sb("w_rt", [P, KD, E0 + 1])
        wn_bc = sb("wn_bc", [P, D])
        sw_gu = sb("sw_gu", [P, KD, 2 * FSP])
        sw_d = sb("sw_d", [P, FSC, D])
        INP = Y
        xnT = R0[:, :].rearrange("p (k t) -> p k t", k=KD)
        XNP = R2[:, :].rearrange("p (t n) -> p t n", t=TILES)
        ROUTE = TILES * E0
        rt = R3[:, 0:6 * ROUTE].rearrange("p (a t e) -> p a t e", a=6, t=TILES)
        LG, EXPL, MSK, SLOT, INV = rt[:, 0], rt[:, 1], rt[:, 2], rt[:, 3], rt[:, 4]
        slot_c = sb("slot_c", [P, 2, TILES, E0])
        o5 = 6 * ROUTE
        PP = R3[:, o5:o5 + TILES * 40].rearrange("p (t e) -> p t e", t=TILES)
        RP = R3[:, o5 + TILES * 40:o5 + TILES * 80].rearrange("p (t e) -> p t e", t=TILES)
        MBF = sb("MBF", [P, TILES, E0], BF16)
        top8 = sb("top8", [P, TILES, 8])
        slot8 = sb("slot8", [P, TILES, 8])
        slot_i = sb("slot_i", [P, TILES, 4], I32)
        tok_i = sb("tok_i", [P, TILES], I32)
        slot_st = sb("slot_st", [P, 2, 4], I32)
        tok_st = sb("tok_st", [P, 2], I32)
        table_sb = sb("table_sb", [P, E0], I32)
        idx_st = sb("idx_st", [P, 2], I32)
        rmx = sb("rmx", [P, TILES])
        rsm = sb("rsm", [P, TILES])
        gate = sb("gate", [P, TILES])
        zer = sb("zer", [P, ROW])
        hF = sb("hF", [P, FSC, 512])
        wexp = R5[:, :].rearrange("p (u n) -> p u n", u=2)
        Xe = Pr[:, :, :, :].rearrange("p a b n -> p (a b n)")[:, 0:2 * ROW].rearrange("p (u n) -> p u n", u=2)
        XeT = rmul[:, 0, :, :].rearrange("p k (u t) -> p u k t", u=2)
        hE = qT[:, 0, :, :]
        yE = qT[:, 1, :, :]
        cpw = sb("cpw", [P, 3, ROWS + 4])
        coef = sb("coef", [P, 3, 4, ROWS + 1])
        ctmp = sb("ctmp", [P, 3, ROWS + 1])
        SP_N = ROWS * SPAN
        AL_N = ROWS * ALT
        frac = R4[:, 0:SP_N].rearrange("p (r n) -> p r n", r=ROWS)
        samp = R4[:, SP_N:2 * SP_N].rearrange("p (r n) -> p r n", r=ROWS)
        fracb = R4[:, 2 * SP_N:2 * SP_N + AL_N].rearrange("p (r n) -> p r n", r=ROWS)
        before = R4[:, 2 * SP_N + AL_N:2 * SP_N + 2 * AL_N].rearrange("p (r n) -> p r n", r=ROWS)
        sampb = R4[:, 2 * SP_N + 2 * AL_N:2 * SP_N + 3 * AL_N].rearrange("p (r n) -> p r n", r=ROWS)
        wC = R6[:, 0:WC]
        WqT = wC[:, 0:512].rearrange("p (k n) -> p k n", k=KD)
        WoT = wC[:, 512:1024].rearrange("p (k n) -> p k n", k=KD)
        WkT = wC[:, 1024:1280].rearrange("p (k n) -> p k n", k=KD)
        WvT = wC[:, 1280:1312].rearrange("p (k n) -> p k n", k=KD)
        bo_bc = wC[:, 1312:1568]
        bv_bc = wC[:, 1568:1584]
        bq, bk, row_valid = wC[:, 1584:1586], wC[:, 1586:1587], wC[:, 1587:1588]
        head_row = wC[:, 1588:1596]
        qTall = R0[:, :].rearrange("p (c t) -> p c t", c=KD)
        Kbd = R2[:, 0:2 * 8 * SEQ].rearrange("p (u j s) -> p u j s", u=2, j=8)
        kTr = R3[:, 0:TOK]
        vall = R3[:, TOK:TOK + TILES * HD1].rearrange("p (t n) -> p t n", t=TILES)
        oC = TOK + TILES * HD1
        qst = R3[:, oC:oC + 512].rearrange("p (c t) -> p c t", c=KD)
        oC_sb = R3[:, oC + 512:oC + 1024].rearrange("p (t n) -> p t n", t=2)
        oTC_sb = R3[:, oC + 1024:oC + 1536].rearrange("p (c t) -> p c t", c=KD)
        sumC = sb("sumC", [P, 2, H1])
        rsumC = sb("rsumC", [P, 2, H1])
        gateT = R4[:, 0:KD * INTER].rearrange("p (k i) -> p k i", k=KD)
        upT = R4[:, KD * INTER:2 * KD * INTER].rearrange("p (k i) -> p k i", k=KD)
        downT = R4[:, 2 * KD * INTER:].rearrange("p (f n) -> p f n", f=IC)
        wnat = R5[:, 0:2 * 3 * D].rearrange("p (u m n) -> p u m n", u=2, m=3)
        hTall = R0[:, :].rearrange("p (k t) -> p k t", k=KD)
        hFD = R2[:, 0:IC * 512].rearrange("p (f t) -> p f t", f=IC)

        bank = [ctx.enter_context(nc.psum_tensor(f"bank{i}", [P, 512], F32)) for i in range(8)]
        rows_d = nc.dram_tensor("rows_d", (TOK + CAP, ROW), F32).ap()
        acc_d = nc.dram_tensor("acc_d", (TOK + CAP, D), F32).ap()
        spline_d = nc.dram_tensor("spline_d", (3, SPLINE), F32).ap()
        table_d = nc.dram_tensor("table_d", (TABLE, 1), I32).ap()

        c_in = sem("c_in"); x_in = sem("x_in"); w_in = sem("w_in"); fin_out = sem("fin_out")
        cbf_ok = sem("cbf_ok"); z_ok = sem("z_ok"); vec_ok = sem("vec_ok")
        wp_in = [sem(f"wp_in{u}") for u in range(2)]
        wp_m = sem("wp_m"); wp_v = sem("wp_v"); wp_me = sem("wp_me"); wp_ve = sem("wp_ve"); wr_ok = sem("wr_ok")
        dch = sem("dch"); pch = sem("pch")
        h_ready = sem("h_ready"); h_tr = sem("h_tr"); hT_ok = sem("hT_ok"); lat = sem("lat")
        ms_ok = sem("ms_ok"); rs_ok = sem("rs_ok"); ckv_ok = sem("ckv_ok"); qk_ready = sem("qk_ready"); qk_tr = sem("qk_tr")
        qlatT_ok = sem("qlatT_ok"); kT_ok = sem("kT_ok")
        mv_ok = sem("mv_ok"); rstd_ok = sem("rstd_ok"); wst_ok = sem("wst_ok"); wst_free = sem("wst_free"); q_rr = sem("q_rr"); q_ab = sem("q_ab"); rmul_ok = sem("rmul_ok")
        q_rope = sem("q_rope"); q_abs = sem("q_abs")
        s_mm = [sem("s_mm_e"), sem("s_mm_o")]; max_ok = [sem("max_e"), sem("max_o")]; exp_ok = [sem("exp_e"), sem("exp_o")]
        pt_mm = [sem("pt_e"), sem("pt_o")]; pt_ok = [sem("ptc_e"), sem("ptc_o")]
        pv_mm = sem("pv_mm"); o_ok = sem("o_ok"); oT_mm = sem("oT_mm"); oT_ok = sem("oT_ok")
        y_mm = sem("y_mm"); y_ok = sem("y_ok")
        mv_n = [sem(f"mv_n{i}") for i in range(5)]; rstd_n = [sem(f"rstd_n{i}") for i in range(5)]
        hr_n = [sem(f"hr_n{i}") for i in range(5)]; tr_n = [sem(f"tr_n{i}") for i in range(5)]; hT_n = [sem(f"hT_n{i}") for i in range(5)]
        b_in = sem("b_in"); b_pool = sem("b_pool"); inp_ok = sem("inp_ok"); sq_ok = sem("sq_ok"); rms_ok = sem("rms_ok"); row_ok = sem("row_ok")
        lg_mm = sem("lg_mm"); lg_ok = sem("lg_ok"); lgs_ok = sem("lgs_ok"); lge_ok = sem("lge_ok"); mask_ok = sem("mask_ok"); rank_mm = sem("rank_mm")
        probs_ok = sem("probs_ok"); slots_ok = sem("slots_ok"); rows_out = sem("rows_out"); sc_st = sem("sc_st"); sc_out = [sem(f"sc_out{u}") for u in range(2)]
        table_in = sem("table_in"); init_out = sem("init_out")
        gu_mm = sem("gu_mm"); sil_ok = sem("sil_ok"); hf_ok = sem("hf_ok"); dn_mm = sem("dn_mm"); dn_ok = sem("dn_ok"); acc_out = sem("acc_out")
        we_in = [sem(f"we_in{u}") for u in range(2)]; idx_ok = sem("idx_ok"); xe_in = [sem(f"xe_in{u}") for u in range(2)]
        xe_tr = sem("xe_tr"); xe_ok = sem("xe_ok"); ge_mm = sem("ge_mm"); se_ok = sem("se_ok"); he_ok = sem("he_ok"); ye_mm = sem("ye_mm"); ye_ok = sem("ye_ok")
        cp_in = sem("cp_in"); cf_ok = sem("cf_ok"); samp_ok = sem("samp_ok"); spl_out = sem("spl_out"); nat_in = [sem(f"nat_in{u}") for u in range(2)]
        nat_tr = sem("nat_tr"); nat_ok = sem("nat_ok")
        qkv_mm = sem("qkv_mm"); qk1_ok = sem("qk1_ok"); v1_ok = sem("v1_ok"); qst_ok = sem("qst_ok"); kbd_ok = sem("kbd_ok")
        s1_mm = [sem("s1_mm_e"), sem("s1_mm_o")]; max1_ok = [sem("max1_e"), sem("max1_o")]; exp1_ok = [sem("exp1_e"), sem("exp1_o")]
        pt1_mm = [sem("pt1_e"), sem("pt1_o")]; pt1_ok = [sem("ptc1_e"), sem("ptc1_o")]
        pv1_mm = sem("pv1_mm"); o1_ok = sem("o1_ok"); oT1_mm = sem("oT1_mm"); oT1_ok = sem("oT1_ok"); y1_mm = sem("y1_mm"); y1_ok = sem("y1_ok")
        hk_ok = sem("hk_ok"); gu1_mm = sem("gu1_mm"); sil1_ok = sem("sil1_ok"); hf1_ok = sem("hf1_ok"); dn1_mm = sem("dn1_mm"); dn1_ok = sem("dn1_ok")
        add_out = sem("add_out"); back_in = sem("back_in"); xb_ok = sem("xb_ok")

        block = ctx.enter_context(nc.Block())




        @block.sync
        def _(sp):
            sp.dma_start(cst[:, :, :], T["cst"]).then_inc(c_in, 16)
            sp.dma_start(vecs[:, :], T["vecs"]).then_inc(c_in, 16)
            sp.dma_start(Wq[:, :, 1:3, :], T["w_rope"]).then_inc(c_in, 16)
            sp.dma_start(w_lat, T["w_lat"]).then_inc(w_in, 16)
            sp.dma_start(rope_k, T["rope_k"]).then_inc(w_in, 16)
            sp.dma_start(rope_q, T["rope_q"]).then_inc(w_in, 16)
            for u in range(2):
                sp.dma_start(wprep[:, u, :], T["wprep"][u, :, :]).then_inc(wp_in[u], 16)
            with sp.Fori(1, PAIRS // 2) as i:
                for u in range(2):
                    sp.wait_ge(wp_v, 2 * i + u - 1)
                    sp.dma_start(wprep[:, u, :], T["wprep"][bass.ds(2 * i + u, 1), :, :].rearrange("a p n -> (a p) n")).then_inc(wp_in[u], 16)

            if phases >= 2:
                for name, dst in (("w_rt", w_rt), ("wn_bc", wn_bc), ("sw_gu", sw_gu), ("sw_d", sw_d), ("slot_c", slot_c), ("tok_i", tok_i)):
                    sp.dma_start(dst[...], T[name]).then_inc(b_in, 16)
                sp.dma_start(table_d[0:SLOTS, :].rearrange("(p a) b -> p (a b)", p=P), T["spare"]).then_inc(init_out, 16)
                sp.wait_ge(z_ok, 1)
                sp.dma_start(rows_d[TOK:, :], zer[:, :]).then_inc(init_out, 16)
                sp.dma_start(acc_d[TOK:, :], zer[:, 0:D]).then_inc(init_out, 16)
                sp.wait_ge(wp_v, PAIRS)
                for u in range(2):
                    sp.dma_start(wexp[:, u, :], T["wexp"][u, :, :]).then_inc(we_in[u], 16)
                sp.dma_start(frac, T["frac"]).then_inc(cp_in, 16)
                sp.dma_start(R4[:, 2 * SP_N:2 * SP_N + 2 * AL_N].rearrange("p (a r n) -> p a r n", a=2, r=ROWS), T["fracb"]).then_inc(cp_in, 16)
                sp.dma_start(cpw[:, :, :], T["cpw"]).then_inc(cp_in, 16)
                sp.wait_ge(y_ok, BATCH)
                sp.dma_start(wC, T["wC"]).then_inc(cp_in, 16)
                sp.wait_ge(probs_ok, 1)
                sp.wait_ge(row_ok, TILES)
                sp.dma_start(rows_d[0:TOK, :].rearrange("(t p) n -> p t n", p=P), XNP).then_inc(rows_out, 16)
                def acc_store(c):
                    sp.wait_ge(dn_ok, 4 * c + 4)
                    sp.dma_start(acc_d[bass.ds(4 * P * c, 4 * P), :].rearrange("(t p) n -> p t n", p=P), INP[:, bass.ds(4 * c, 4), :]).then_inc(acc_out, 16)

                with sp.Fori(0, 3) as c:
                    sp.wait_ge(samp_ok, c + 1)
                    sp.dma_start(spline_d[bass.ds(c, 1), :].rearrange("a (p n) -> (a p) n", p=P), samp.rearrange("p r n -> p (r n)")).then_inc(spl_out, 16)
                    acc_store(c)
                acc_store(3)
                with sp.Fori(1, E0 // 2) as i:
                    for u in range(2):
                        sp.wait_ge(ye_mm, 2 * i + u - 1)
                        sp.dma_start(wexp[:, u, :], T["wexp"][bass.ds(2 * i + u, 1), :, :].rearrange("a p n -> (a p) n")).then_inc(we_in[u], 16)
                sp.wait_ge(add_out, 16 * E0)
                sp.dma_start(Y, acc_d[0:TOK, :].rearrange("(t p) n -> p t n", p=P)).then_inc(back_in, 16)
            if phases >= 3:
                def natural(j, u):
                    for m in range(2):
                        sp.dma_start(wnat[:, u, m, :], spline_d[m, bass.ds(P * D * j, P * D)].rearrange("(p n) -> p n", p=P)).then_inc(nat_in[u], 16)
                    sp.dma_start(wnat[:, u, 2, :].rearrange("p (k i) -> p k i", k=KD),
                                 spline_d[2, 0:D * INTER].rearrange("(k p j i) -> p j k i", k=KD, p=P, j=IC)[:, bass.ds(j, 1), :, :].rearrange("p a k i -> p (a k) i")).then_inc(nat_in[u], 16)

                sp.wait_ge(spl_out, 48)
                for u in range(2):
                    natural(u, u)
                with sp.Fori(1, IC // 2) as i:
                    for u in range(2):
                        sp.wait_ge(nat_tr, 2 * i + u - 1)
                        natural(2 * i + u, u)

        @block.gpsimd
        def _(pool):
            ch = Tally(pool, pch)
            ch.mark(pool.memset(zbf[:, :], 0.0))
            ch.mark(pool.memset(mhalf[:, :], -0.5))
            ch.mark(pool.memset(zer[:, :], 0.0))
            ch.wait()
            pool.nop().then_inc(z_ok, 1)
            def power(src_sem, value, out_, in_, eps, done):
                pool.wait_ge(src_sem, value)
                ch.mark(pool.nop())
                ch.link(pool.tensor_scalar(out_, in_, eps, None, ALU.add))
                pool.tensor_tensor(out_, out_, mhalf[:, 0:out_.shape[1]] if len(out_.shape) == 2 else mhalf[:, :].rearrange("p (a n) -> p a n", a=2), ALU.pow).then_inc(done, 1)

            with pool.Fori(0, BATCH) as b:
                ch.enter(b, 4)
                power(mv_ok, 2 * b + 2, rstd[:, :], mv[:, :, 1], LN_EPS, rstd_ok)
                power(ms_ok, 4 * b + 4, ms[:, :, :], ms[:, :, :], RMS_EPS, rs_ok)
            ch.leave(BATCH)
            pool.wait_ge(wr_ok, 1)
            pool.wait_ge(wp_me, PAIRS)

            def stage(g, pair, u, first=False):
                if not first:
                    pool.wait_ge(q_ab, g - 1)
                    pool.nop().then_inc(wst_free, 1)
                pool.tensor_copy(wst[:, u, :, :], Wq[:, bass.ds(pair, 1), :, :].rearrange("p a k m -> p (a k) m")).then_inc(wst_ok, 1)
                pool.wait_ge(wst_ok, g + 1)
                ch.mark(pool.nop())

            def rope_sum(g, u):
                pool.wait_ge(rmul_ok, g + 1)
                ch.link(pool.tensor_tensor(qT[64:128, u, 0, :], rmul[64:128, u, 0, :], rmul[64:128, u, 1, :], ALU.add))
                pool.tensor_tensor(qT[0:64, u, 1, :], rmul[0:64, u, 0, :], rmul[0:64, u, 1, :], ALU.add).then_inc(q_rope, 1)
                pool.wait_ge(q_rope, g + 1)
                ch.mark(pool.nop())

            stage(0, 0, 0, True)
            stage(1, 1, 1, True)
            rope_sum(0, 0)
            rope_sum(1, 1)

            STEP = 3
            def batch(b, last):
                with pool.Fori(0, 3) as i:
                    ch.enter(i, 2 * STEP)
                    for u in range(2):
                        g = 8 * b + 2 * i + u
                        stage(g + 2, 2 * i + u + 2, u)
                        rope_sum(g + 2, u)
                ch.leave(3)
                if not last:
                    for u in range(2):
                        g = 8 * b + 6 + u
                        stage(g + 2, u, u)
                        rope_sum(g + 2, u)

            with pool.Fori(0, BATCH - 1) as b:
                ch.enter(b, 8 * STEP)
                batch(b, False)
            ch.leave(BATCH - 1)
            batch(BATCH - 1, True)
            def ln_powers(i, extra=None):
                with pool.Fori(0, BATCH) as b:
                    ch.enter(b, 4 if i < 4 and i != 1 else 6 if i == 1 else 2)
                    power(mv_n[i], (4 if i < 4 else 2) * b + 2, rstd[:, :], mv[:, :, 1], LN_EPS, rstd_n[i])
                    if i < 4:
                        power(mv_n[i], 4 * b + 4, rstd[:, :], mv[:, :, 1], LN_EPS, rstd_n[i])
                    if i == 1:
                        power(sq_ok, 2 * b + 2, ms[:, :, 0], ms[:, :, 0], RMS_EPS, rms_ok)
                ch.leave(BATCH)

            if phases >= 2:
                ln_powers(1)
                pool.wait_ge(slots_ok, 1)
                pool.wait_ge(b_in, 96)
                pool.wait_ge(init_out, 48)
                ch.mark(pool.nop())
                with pool.Fori(0, BATCH) as b:
                    ch.enter(b, 2)
                    for u in range(2):
                        ch.mark(pool.nop())
                        pool.tensor_copy(slot_st[:, u, :], slot_i[:, bass.ds(2 * b + u, 1), :].rearrange("p a k -> p (a k)")).then_inc(sc_st, 1)
                        pool.tensor_copy(tok_st[:, u:u + 1], tok_i[:, bass.ds(2 * b + u, 1)]).then_inc(sc_st, 1)
                    pool.wait_ge(sc_st, 4 * b + 4)
                    pool.nop().then_inc(b_pool, 1)
                    for u in range(2):
                        for k in range(TOPK):
                            pool.indirect_dma_start(out=table_d, out_offset=bass.IndirectOffsetOnAxis(ap=slot_st[:, u, k:k + 1], axis=0),
                                                    in_=tok_st[:, u:u + 1], in_offset=None).then_inc(sc_out[u], 16)
                    for u in range(2):
                        pool.wait_ge(sc_out[u], 64 * b + 64)
                    pool.nop().then_inc(b_pool, 1)
                ch.leave(BATCH)
                pool.dma_start(table_sb[:, :], table_d[0:SLOTS, :].rearrange("(p a) b -> p (a b)", p=P)).then_inc(table_in, 16)
                pool.wait_ge(table_in, 16)
                pool.wait_ge(rows_out, 16)
                pool.wait_ge(acc_out, 64)
                ch.mark(pool.nop())

                def gather(e, u):
                    pool.tensor_copy(idx_st[:, u:u + 1], table_sb[:, bass.ds(e, 1)]).then_inc(idx_ok, 1)
                    pool.wait_ge(idx_ok, e + 1)
                    ch.mark(pool.nop())
                    pool.indirect_dma_start(out=Xe[:, u, :], out_offset=None, in_=rows_d, in_offset=bass.IndirectOffsetOnAxis(ap=idx_st[:, u:u + 1], axis=0))\
                        .then_inc(xe_in[u], 16)

                def scatter_add(e, u):
                    pool.wait_ge(ye_ok, e + 1)
                    ch.mark(pool.nop())
                    pool.indirect_dma_start(out=acc_d, out_offset=bass.IndirectOffsetOnAxis(ap=idx_st[:, u:u + 1], axis=0), in_=yE[:, u, :], in_offset=None,
                                            compute_op=ALU.add).then_inc(add_out, 16)
                    pool.wait_ge(add_out, 16 * e + 16)
                    ch.mark(pool.nop())

                gather(0, 0)
                gather(1, 1)
                with pool.Fori(0, E0 // 2 - 1) as i:
                    ch.enter(i, 6)
                    for u in range(2):
                        scatter_add(2 * i + u, u)
                        gather(2 * i + u + 2, u)
                ch.leave(E0 // 2 - 1)
                for u in range(2):
                    scatter_add(E0 - 2 + u, u)
            if phases >= 3:
                ln_powers(2)
                pool.wait_ge(qk1_ok, 3 * BATCH)
                ch.mark(pool.nop())

                def key_blocks(b):
                    pool.tensor_tensor(Kbd[:, bass.ds(b % 2, 1), :, :].rearrange("p a j s -> p (a j) s"), kTr[:, None, bass.ds(SEQ * b, SEQ)].to_broadcast([P, 8, SEQ]),
                                       head_row[:, :, None].to_broadcast([P, 8, SEQ]), ALU.mult).then_inc(kbd_ok, 1)
                    pool.wait_ge(kbd_ok, b + 1)
                    ch.mark(pool.nop())

                def queries(b, c):
                    pool.tensor_copy(qst[:, c, :], qTall[:, c, bass.ds(SEQ * b, SEQ)]).then_inc(qst_ok, 1)
                    pool.wait_ge(qst_ok, 2 * b + c + 1)
                    ch.mark(pool.nop())

                key_blocks(0)
                queries(0, 0)
                queries(0, 1)
                key_blocks(1)

                def batch(b, more):
                    for c in range(2):
                        pool.wait_ge(s1_mm[1], 8 * b + 4 * c + 4)
                        ch.mark(pool.nop())
                        queries(b + 1, c)
                    if more:
                        key_blocks(b + 2)

                with pool.Fori(0, BATCH - 2) as b:
                    ch.enter(b, 5)
                    batch(b, True)
                ch.leave(BATCH - 2)
                batch(BATCH - 2, False)
            if phases >= 4:
                ln_powers(3)
            ln_powers(4)

        @block.scalar
        def _(act):
            act.dma_start(X[:, 0:8, :], T["x"][:, 0:8, :]).then_inc(x_in, 16)
            act.dma_start(X[:, 8:16, :], T["x"][:, 8:16, :]).then_inc(x_in, 16)
            act.wait_ge(c_in, 48)
            with act.Fori(0, PAIRS // 2) as i:
                for u in range(2):
                    act.wait_ge(wp_v, 2 * i + u + 1)
                    act.activation(Wvo[:, bass.ds(2 * i + u, 1), :].rearrange("p a n -> p (a n)"), bank[2 + u][:, 0:D], ACT.Copy, scale=vecs[:, KVL:KVL + 1]).then_inc(wp_ve, 1)
            with act.Fori(0, BATCH) as b:
                for u in range(2):
                    act.wait_ge(h_tr, 2 * b + u + 1)
                    act.activation(hTs[:, u, :, :], bank[4 + u][:, 0:D].rearrange("p (k t) -> p k t", k=KD), ACT.Copy).then_inc(hT_ok, 1)
                for u in range(2):
                    act.wait_ge(lat, 2 * b + u + 1)
                    act.activation(sqj[:, u, 0:QL], bank[6 + u][:, 0:QL], ACT.Square, scale=float(QL ** -0.5), accum_out=ms[:, u, 0:1]).then_inc(ms_ok, 1)
                    act.wait_ge(ms_ok, 4 * b + 2 * u + 1)
                    act.activation(sqj[:, u, 0:KVL], bank[6 + u][:, QL:QL + KVL], ACT.Square, scale=float(KVL ** -0.5), accum_out=ms[:, u, 1:2]).then_inc(ms_ok, 1)
                for u in range(2):
                    act.wait_ge(qk_tr, 2 * b + u + 1)
                    act.activation(qlatT[:, bass.ds(2 * P * b + u * P, P)], bank[4 + u][0:QL, 0:P], ACT.Copy).then_inc(qlatT_ok, 1)

            def abs_copy(g, u):
                act.wait_ge(q_ab, g + 1)
                act.activation(qT[0:64, u, 0, :], bank[2][0:64, 0:SEQ], ACT.Copy)
                act.activation(qT[64:128, u, 1, :], bank[2][64:128, 0:SEQ], ACT.Copy).then_inc(q_abs, 1)

            def exps(g, u, e):
                act.wait_ge(max_ok[e], g + 1)
                for t, (lo, n) in enumerate(((0, P), (P, SEQ))):
                    ins = act.activation(Pr[:, u, e, lo:lo + n], bank[e][:, lo:lo + n], ACT.Exp, bias=nmax[:, u, t, e:e + 1],
                                         accum_out=sums[:, u, t, e:e + 1])
                ins.then_inc(exp_ok[e], 1)

            def pt_copy(g):
                act.wait_ge(pt_mm[0], g + 1)
                act.activation(PTs[:, 0, :], bank[4][:, 0:CAUSAL], ACT.Copy).then_inc(pt_ok[0], 1)

            abs_copy(0, 0)
            exps(0, 0, 0)
            exps(0, 0, 1)
            abs_copy(1, 1)

            def step(g, u, q_next, s_next):
                pt_copy(g)
                if s_next:
                    exps(g + 1, 1 - u, 0)
                    exps(g + 1, 1 - u, 1)
                if q_next:
                    abs_copy(g + 2, u)

            def batch(b, last):
                with act.Fori(0, 3) as i:
                    for u in range(2):
                        step(8 * b + 2 * i + u, u, True, True)
                for u in range(2):
                    step(8 * b + 6 + u, u, not last, not last or u == 0)
                act.wait_ge(y_mm, b + 1)
                act.activation(Y[:, bass.ds(2 * b, 2), :], bank[7][:, :].rearrange("p (t n) -> p t n", t=2), ACT.Copy).then_inc(y_ok, 1)

            with act.Fori(0, BATCH - 1) as b:
                batch(b, False)
            batch(BATCH - 1, True)
            def hT_copies(i, b, keep=None):
                for u in range(2):
                    act.wait_ge(tr_n[i], 2 * b + u + 1)
                    src = bank[4 + u][:, 0:D].rearrange("p (k t) -> p k t", k=KD)
                    if keep is not None:
                        act.activation(keep[:, :, bass.ds(2 * P * b + u * P, P)], src, ACT.Copy)
                    act.activation(hTs[:, u, :, :], src, ACT.Copy).then_inc(hT_n[i], 1)

            def silu_of(src, dst, sem_in, n, sem_out):
                act.wait_ge(sem_in, n)
                act.activation(dst, src, ACT.Silu).then_inc(sem_out, 1)

            if phases >= 2:
                with act.Fori(0, BATCH) as b:
                    for u in range(2):
                        act.wait_ge(inp_ok, 2 * b + u + 1)
                        act.activation(sqj[:, u, :], INP[:, bass.ds(2 * b + u, 1), :].rearrange("p a n -> p (a n)"), ACT.Square, scale=float(D ** -0.5),
                                       accum_out=ms[:, u, 0:1]).then_inc(sq_ok, 1)
                    for u in range(2):
                        act.wait_ge(hr_n[1], 2 * b + u + 1)
                        act.activation(XNP[:, bass.ds(2 * b + u, 1), 0:D].rearrange("p a n -> p (a n)"), hbuf[:, u, :], ACT.Copy).then_inc(row_ok, 1)
                    hT_copies(1, b, xnT)
                    for u in range(2):
                        act.wait_ge(lg_mm, 2 * b + u + 1)
                        act.activation(LG[:, bass.ds(2 * b + u, 1), :].rearrange("p a n -> p (a n)"), bank[6 + u][:, 0:E0], ACT.Copy)
                        act.activation(gate[:, bass.ds(2 * b + u, 1)], bank[6 + u][:, E0:E0 + 1], ACT.Copy).then_inc(lg_ok, 1)
                act.wait_ge(lgs_ok, 1)
                act.activation(EXPL, EXPL, ACT.Exp).then_inc(lge_ok, 1)
                act.activation(gate[:, :], gate[:, :], ACT.Exp, scale=-1.0).then_inc(lge_ok, 1)
                with act.Fori(0, 4) as c:
                    for f in range(FSC):
                        act.wait_ge(gu_mm, FSC * c + f + 1)
                        act.wait_ge(hf_ok, FSC * c + f + 1)
                        act.activation(sil[:, f % 2, :], bank[2 * (f % 2)][:, :], ACT.Silu).then_inc(sil_ok, 1)
                with act.Fori(0, E0 // 2) as i:
                    for u in range(2):
                        e = 2 * i + u
                        act.wait_ge(xe_tr, e + 1)
                        act.activation(XeT[:, u, :, :], bank[4][:, 0:D].rearrange("p (k t) -> p k t", k=KD), ACT.Copy).then_inc(xe_ok, 1)
                        act.wait_ge(ge_mm, e + 1)
                        act.activation(sil[0:FEK, u, 0:2 * P], bank[5 + u][0:FEK, 0:2 * P], ACT.Silu).then_inc(se_ok, 1)
            if phases >= 3:
                with act.Fori(0, BATCH) as b:
                    hT_copies(2, b)
                    act.wait_ge(nat_tr, b + 1)
                    for m, wT in enumerate((gateT, upT)):
                        act.activation(wT[:, :, bass.ds(P * b, P)], bank[7][:, m * D:(m + 1) * D].rearrange("p (k i) -> p k i", k=KD), ACT.Copy)
                    act.activation(downT[:, bass.ds(b, 1), :].rearrange("p a n -> p (a n)"), bank[6][:, 0:D], ACT.Copy).then_inc(nat_ok, 1)
                    act.wait_ge(qkv_mm, b + 1)
                    for c in range(KD):
                        act.activation(qTall[:, c, bass.ds(SEQ * b, SEQ)], bank[c][:, 0:SEQ], ACT.Identity, bias=bq[:, c:c + 1], scale=1.0).then_inc(qk1_ok, 1)
                    act.activation(kTr[:, bass.ds(SEQ * b, SEQ)], bank[2][:, 0:SEQ], ACT.Identity, bias=bk, scale=1.0).then_inc(qk1_ok, 1)

                def exps1(g, p, e):
                    act.wait_ge(max1_ok[e], g + 1)
                    for t, (lo, n) in enumerate(((0, P), (P, SEQ))):
                        ins = act.activation(Pr[:, p % 2, e, lo:lo + n], bank[e][:, lo:lo + n], ACT.Exp, bias=nmax[:, p % 2, t, e:e + 1], scale=SCALE1,
                                             accum_out=sumC[:, t, 2 * p + e:2 * p + e + 1])
                    ins.then_inc(exp1_ok[e], 1)

                def batch(b, last):
                    for p in range(8):
                        g = 8 * b + p
                        act.wait_ge(pt1_mm[0], g + 1)
                        act.activation(PTs[:, 0, :], bank[4][:, 0:CAUSAL], ACT.Copy).then_inc(pt1_ok[0], 1)
                        if p == 7:
                            act.wait_ge(o1_ok, b + 1)
                        if not (last and p == 7):
                            exps1(g + 1, (p + 1) % 8, 0)
                            exps1(g + 1, (p + 1) % 8, 1)
                    act.wait_ge(oT1_mm, b + 1)
                    act.activation(oTC_sb, bank[6][:, :].rearrange("p (c t) -> p c t", c=KD), ACT.Copy).then_inc(oT1_ok, 1)

                exps1(0, 0, 0)
                exps1(0, 0, 1)
                with act.Fori(0, BATCH - 1) as b:
                    batch(b, False)
                batch(BATCH - 1, True)
            if phases >= 4:
                with act.Fori(0, BATCH) as b:
                    for u in range(2):
                        act.wait_ge(tr_n[3], 2 * b + u + 1)
                        act.activation(hTall[:, :, bass.ds(2 * P * b + u * P, P)], bank[4 + u][:, 0:D].rearrange("p (k t) -> p k t", k=KD), ACT.Copy).then_inc(hk_ok, 1)
                with act.Fori(0, 4) as c:
                    for f in range(IC):
                        act.wait_ge(gu1_mm, IC * c + f + 1)
                        act.wait_ge(hf1_ok, IC * c + f + 1)
                        act.activation(sil[:, f % 2, :], bank[2 * (f % 2)][:, :], ACT.Silu).then_inc(sil1_ok, 1)
            act.wait_ge(xb_ok, 1)
            act.dma_start(out, X[:, :, :]).then_inc(fin_out, 16)
            act.wait_ge(fin_out, 16)

        @block.vector
        def _(dve):
            ch = Tally(dve, dch)
            dve.sem_inc(hf_ok, 2)
            dve.wait_ge(c_in, 48)
            dve.tensor_copy(cbf[:, :, :], cst[:, :, :]).then_inc(cbf_ok, 1)
            dve.tensor_copy(ident[:, :], cst[:, 0, :]).then_inc(cbf_ok, 1)
            ch.link(dve.tensor_scalar(vecs[:, KVL + 1:KVL + 2], vecs[:, KVL + 1:KVL + 2], SCALE0, None, ALU.mult))
            dve.tensor_scalar(Wq[:, :, 1:3, :].rearrange("p a k m -> p a (k m)"), Wq[:, :, 1:3, :].rearrange("p a k m -> p a (k m)"),
                              vecs[0:QL, KVL + 1:KVL + 2], None, ALU.mult).then_inc(wr_ok, 1)
            with dve.Fori(0, PAIRS // 2) as i:
                for u in range(2):
                    dve.wait_ge(wp_m, 2 * i + u + 1)
                    dve.scalar_tensor_tensor(Wq[:, bass.ds(2 * i + u, 1), 0, :].rearrange("p a (e m) -> p (a e) m", e=2),
                                             bank[u][0:QL, 0:P].rearrange("p (e m) -> p e m", e=2), vecs[0:QL, KVL + 1:KVL + 2],
                                             vecs[0:QL, None, 0:KVL].to_broadcast([QL, 2, KVL]), ALU.mult, ALU.mult).then_inc(wp_me, 1)
            dve.wait_ge(x_in, 32)
            dve.wait_ge(w_in, 48)
            with dve.Fori(0, BATCH) as b:
                ch.enter(b, 14)
                for u in range(2):
                    ch.mark(dve.bn_stats(stats[:, u, :], X[:, bass.ds(2 * b + u, 1), :].rearrange("p a n -> p (a n)")))
                ch.hold()
                for u in range(2):
                    dve.bn_aggr(mv[:, u, :], stats[:, u, :]).then_inc(mv_ok, 1)
                dve.wait_ge(rstd_ok, b + 1)
                for u in range(2):
                    dve.tensor_scalar(hbuf[:, u, :], X[:, bass.ds(2 * b + u, 1), :].rearrange("p a n -> p (a n)"), mv[:, u, 0:1], rstd[:, u:u + 1],
                                      ALU.subtract, ALU.mult).then_inc(h_ready, 1)
                dve.wait_ge(rs_ok, b + 1)
                for u in range(2):
                    psl = bank[6 + u]
                    ch.mark(dve.tensor_scalar(qn[:, u, :], psl[:, 0:QL], ms[:, u, 0:1], None, ALU.mult))
                    ch.mark(dve.tensor_tensor(kr2[:, u, :, :], psl[:, QL + KVL:LAT].rearrange("p (a n) -> p a n", a=2),
                                              rope_k[:, u, :, :], ALU.mult))
                    ch.mark(dve.tensor_scalar(kst[:, u, 0:3:2, :], psl[:, None, QL:QL + KVL].to_broadcast([P, 2, KVL]), ms[:, u, 1:2], None, ALU.mult))
                    dve.tensor_scalar(ckv[:, bass.ds(2 * b + u, 1), :].rearrange("p a n -> p (a n)"), psl[:, QL:QL + KVL], ms[:, u, 1:2], None, ALU.mult).then_inc(ckv_ok, 1)
                    ch.wait()
                    ch.mark(dve.tensor_tensor(kst[:, u, 1, :], kr2[:, u, 0, :], kr2[:, u, 1, :], ALU.add))
                    ch.wait()
                    dve.nop().then_inc(qk_ready, 1)
                for u in range(2):
                    dve.wait_ge(qk_tr, 2 * b + u + 1)
                    ch.mark(dve.tensor_copy(kTa[:, bass.ds(2 * P * b + u * P, P)], bank[u][:, P:2 * P]))
                    dve.tensor_copy(kTb[:, bass.ds(2 * P * b + u * P, P)], bank[u][:, 2 * P:3 * P]).then_inc(kT_ok, 1)
                dve.wait_ge(kT_ok, 2 * b + 2)
                ch.mark(dve.nop())
            ch.leave(BATCH)

            def rope_mul(g, u, first=False):
                dve.wait_ge(q_rr, g + 1)
                if not first:
                    dve.wait_ge(q_rope, g - 1)
                dve.tensor_tensor(rmul[:, u, :, :], bank[3][:, :].rearrange("p (k t) -> p k t", k=2), rope_q[:, :, :], ALU.mult).then_inc(rmul_ok, 1)

            def maxes(g, u, e):
                dve.wait_ge(s_mm[e], g + 1)
                for t, (lo, n) in enumerate(((0, P), (P, SEQ))):
                    ins = dve.tensor_reduce(nmax[:, u, t, e:e + 1], bank[e][:, lo:lo + n], AX.X, ALU.max, negate=True)
                ins.then_inc(max_ok[e], 1)

            def pt_copy(g):
                dve.wait_ge(pt_mm[1], g + 1)
                dve.tensor_copy(PTs[:, 1, :], bank[5][:, 0:CAUSAL]).then_inc(pt_ok[1], 1)

            def o_norm(g, u):
                dve.wait_ge(exp_ok[1], g + 1)
                ch.link(dve.reciprocal(rsum[:, :, :], sums[:, u, :, :]))
                dve.wait_ge(pv_mm, g + 1)
                dve.tensor_tensor(o_sb[:, :, :].rearrange("p t (e n) -> p (t e) n", e=2), bank[6][:, 0:SEQ].rearrange("p (c n) -> p c n", c=4),
                                  rsum[:, :, :].rearrange("p t e -> p (t e)")[:, :, None].to_broadcast([P, 4, KVL]), ALU.mult).then_inc(o_ok, 1)

            def oT_copy(g):
                dve.wait_ge(oT_mm, g + 1)
                dve.tensor_copy(oT_sb[:, :], bank[6][:, SEQ:2 * SEQ]).then_inc(oT_ok, 1)

            rope_mul(0, 0, True)
            rope_mul(1, 1, True)
            maxes(0, 0, 0)
            maxes(0, 0, 1)

            def step(g, u, q_next, s_next):
                if s_next:
                    maxes(g + 1, 1 - u, 0)
                pt_copy(g)
                if q_next:
                    rope_mul(g + 2, u)
                o_norm(g, u)
                if s_next:
                    maxes(g + 1, 1 - u, 1)
                oT_copy(g)

            STEP = 1
            def batch(b, last):
                with dve.Fori(0, 3) as i:
                    ch.enter(i, 2 * STEP)
                    for u in range(2):
                        step(8 * b + 2 * i + u, u, True, True)
                    ch.leave(3)
                for u in range(2):
                    step(8 * b + 6 + u, u, not last, not last or u == 0)

            with dve.Fori(0, BATCH - 1) as b:
                ch.enter(b, 8 * STEP)
                batch(b, False)
            ch.leave(BATCH - 1)
            batch(BATCH - 1, True)
            def tile(buf, t):
                return buf[:, bass.ds(t, 1), :].rearrange("p a n -> p (a n)")

            def moments(i, src):
                for u in range(2):
                    ch.mark(dve.bn_stats(stats[:, u, :], src(u)))
                ch.hold()
                for u in range(2):
                    dve.bn_aggr(mv[:, u, :], stats[:, u, :]).then_inc(mv_n[i], 1)

            def add_normed(i, b):
                moments(i, lambda u: tile(Y, 2 * b + u))
                dve.wait_ge(rstd_n[i], (2 * b if i < 4 else b) + 1)
                for u in range(2):
                    ch.mark(dve.tensor_scalar(lnb[:, u, :], tile(Y, 2 * b + u), mv[:, u, 0:1], rstd[:, u:u + 1], ALU.subtract, ALU.mult))
                ch.wait()
                for u in range(2):
                    ch.mark(dve.tensor_tensor(tile(X, 2 * b + u), tile(X, 2 * b + u), lnb[:, u, :], ALU.add))
                ch.hold()

            def normed(i, b, dst, done):
                moments(i, lambda u: tile(X, 2 * b + u))
                dve.wait_ge(rstd_n[i], 2 * b + 2)
                for u in range(2):
                    dve.tensor_scalar(dst(u), tile(X, 2 * b + u), mv[:, u, 0:1], rstd[:, u:u + 1], ALU.subtract, ALU.mult).then_inc(done, 1)

            dve.wait_ge(y_ok, BATCH)
            if phases >= 2:
                dve.wait_ge(b_in, 96)
                with dve.Fori(0, BATCH) as b:
                    ch.enter(b, 11)
                    add_normed(1, b)
                    normed(1, b, lambda u: tile(INP, 2 * b + u), inp_ok)
                    dve.wait_ge(inp_ok, 2 * b + 2)
                    dve.wait_ge(rms_ok, b + 1)
                    for u in range(2):
                        dve.scalar_tensor_tensor(hbuf[:, u, :], tile(INP, 2 * b + u), ms[:, u, 0:1], wn_bc[:, :], ALU.mult, ALU.mult).then_inc(hr_n[1], 1)
                    dve.wait_ge(row_ok, 2 * b + 2)
                    dve.wait_ge(tr_n[1], 2 * b + 2)
                ch.leave(BATCH)
                dve.wait_ge(lg_ok, TILES)
                bc = lambda v: v[:, :, None].to_broadcast([P, TILES, E0])
                ch.link(dve.tensor_reduce(rmx[:, :], LG, AX.X, ALU.max))
                dve.tensor_tensor(EXPL, LG, bc(rmx), ALU.subtract).then_inc(lgs_ok, 1)
                ch.mark(dve.memset(PP[:, :, E0:], -1.0))
                dve.wait_ge(lge_ok, 2)
                ch.link(dve.tensor_reduce(rsm[:, :], EXPL, AX.X, ALU.add))
                ch.mark(dve.reciprocal(rsm[:, :], rsm[:, :]))
                ch.link(dve.tensor_scalar(gate[:, :], gate[:, :], 1.0, None, ALU.add))
                ch.mark(dve.reciprocal(gate[:, :], gate[:, :]))
                ch.link(dve.tensor_tensor(PP[:, :, 0:E0], EXPL, bc(rsm), ALU.mult))
                dve.tensor_copy(XNP[:, :, D:], PP[:, :, 0:E0]).then_inc(probs_ok, 1)
                for t in range(TILES):
                    ch.mark(dve.max(top8[:, t, :], PP[:, t, 0:E0]))
                ch.wait()
                ch.link(dve.memset(top8[:, :, TOPK:], -1.0))
                for t in range(TILES):
                    ch.mark(dve.match_replace(RP[:, t, :], top8[:, t, :], PP[:, t, :], -2.0))
                ch.wait()
                dve.tensor_scalar(MBF[:, :, :], RP[:, :, 0:E0], -2.0, None, ALU.is_equal).then_inc(mask_ok, 1)
                ch.mark(dve.tensor_scalar(MSK, RP[:, :, 0:E0], -2.0, None, ALU.is_equal))
                dve.wait_ge(rank_mm, 1)
                rank = bank[0][:, :].rearrange("p (t e) -> p t e", t=TILES)
                ch.mark(dve.scalar_tensor_tensor(SLOT, rank, float(E0), slot_c[:, 0], ALU.mult, ALU.add))
                ch.link(dve.tensor_scalar(INV, rank, float(CAP), None, ALU.is_ge))
                ch.link(dve.copy_predicated(SLOT, INV.bitcast(U32), slot_c[:, 1]))
                ch.link(dve.tensor_tensor(SLOT, SLOT, MSK, ALU.mult))
                for t in range(TILES):
                    ch.mark(dve.max(slot8[:, t, :], SLOT[:, t, :]))
                ch.wait()
                dve.tensor_scalar(slot_i[:, :, :], slot8[:, :, 0:TOPK], -1.0, None, ALU.add).then_inc(slots_ok, 1)
                dve.wait_ge(cp_in, 64)
                p0, p1, p2, p3 = (cpw[:, :, k:k + ROWS + 1] for k in range(4))
                c0, c1, c2, c3 = (coef[:, :, k, :] for k in range(4))
                ch.mark(dve.tensor_copy(c0, p1))
                ch.link(dve.tensor_tensor(ctmp[:, :, :], p2, p0, ALU.subtract))
                ch.mark(dve.tensor_scalar(c1, ctmp[:, :, :], 0.5, None, ALU.mult))
                ch.mark(dve.scalar_tensor_tensor(c3, p2, -3.0, p3, ALU.mult, ALU.add))
                ch.link(dve.scalar_tensor_tensor(c2, p2, 4.0, p3, ALU.mult, ALU.subtract))
                ch.mark(dve.scalar_tensor_tensor(c3, p1, 3.0, c3, ALU.mult, ALU.add))
                ch.link(dve.scalar_tensor_tensor(c2, p1, -5.0, c2, ALU.mult, ALU.add))
                ch.mark(dve.tensor_tensor(c3, c3, p0, ALU.subtract))
                ch.link(dve.scalar_tensor_tensor(c2, p0, 2.0, c2, ALU.mult, ALU.add))
                ch.mark(dve.tensor_scalar(c3, c3, 0.5, None, ALU.mult))
                ch.link(dve.tensor_scalar(c2, c2, 0.5, None, ALU.mult))

                def spline_op(m, f):
                    for out_, t_, row, n in ((samp, frac, 1, SPAN), (sampb, fracb, 0, ALT)):
                        c = coef[:, bass.ds(m, 1), 3 - (f + 1) // 2, row:row + ROWS].rearrange("p a r -> p (a r)")[:, :, None].to_broadcast([P, ROWS, n])
                        if f == 0:
                            ch.mark(dve.tensor_tensor(out_, t_, c, ALU.mult))
                        elif f % 2:
                            ch.mark(dve.tensor_tensor(out_, out_, c, ALU.add))
                        else:
                            ch.mark(dve.tensor_tensor(out_, out_, t_, ALU.mult))
                    ch.wait()

                def shared(c, spline):
                    for f in range(FSC):
                        if spline:
                            spline_op(c, f)
                        dve.wait_ge(sil_ok, FSC * c + f + 1)
                        dve.tensor_tensor(hF[:, f, :], sil[:, f % 2, :], bank[2 * (f % 2) + 1][:, :], ALU.mult).then_inc(hf_ok, 1)
                    if spline:
                        dve.copy_predicated(samp[:, :, 0:ALT], before.bitcast(U32), sampb).then_inc(samp_ok, 1)
                    for t in range(4):
                        dve.wait_ge(dn_mm, 4 * c + t + 1)
                        dve.scalar_tensor_tensor(tile(INP, 4 * c + t), bank[4 + t % 2][:, 0:D], gate[:, bass.ds(4 * c + t, 1)], tile(INP, 4 * c + t),
                                                 ALU.mult, ALU.add).then_inc(dn_ok, 1)

                with dve.Fori(0, 3) as c:
                    ch.enter(c, 2 * FSC)
                    shared(c, True)
                    dve.wait_ge(spl_out, 16 * c + 16)
                ch.leave(3)
                shared(3, False)
                with dve.Fori(0, E0 // 2) as i:
                    for u in range(2):
                        e = 2 * i + u
                        dve.wait_ge(se_ok, e + 1)
                        dve.tensor_tensor(hE[0:FEK, u, :], sil[0:FEK, u, 0:2 * P], bank[5 + u][0:FEK, 2 * P:4 * P], ALU.mult).then_inc(he_ok, 1)
                        dve.wait_ge(ye_mm, e + 1)
                        dve.tensor_scalar(yE[:, u, :], bank[7][:, 0:D], Xe[:, u, bass.ds(D + e, 1)], None, ALU.mult).then_inc(ye_ok, 1)
                dve.wait_ge(back_in, 16)
            if phases >= 3:
                with dve.Fori(0, BATCH) as b:
                    ch.enter(b, 11)
                    add_normed(2, b)
                    normed(2, b, lambda u: hbuf[:, u, :], hr_n[2])
                    dve.wait_ge(qkv_mm, b + 1)
                    dve.tensor_tensor(vall[:, bass.ds(2 * b, 2), :], bank[3][:, 0:2 * HD1].rearrange("p (u n) -> p u n", u=2), bv_bc[:, None, :].to_broadcast([P, 2, HD1]), ALU.add)\
                        .then_inc(v1_ok, 1)
                ch.leave(BATCH)

                def maxes1(g, p, e):
                    dve.wait_ge(s1_mm[e], g + 1)
                    for t, (lo, n) in enumerate(((0, P), (P, SEQ))):
                        ch.mark(dve.tensor_reduce(nmax[:, p % 2, t, e:e + 1], bank[e][:, lo:lo + n], AX.X, ALU.max, negate=True))
                    ch.wait()
                    dve.tensor_scalar(nmax[:, p % 2, :, e], nmax[:, p % 2, :, e], SCALE1, None, ALU.mult).then_inc(max1_ok[e], 1)

                def batch(b, last):
                    for p in range(8):
                        g = 8 * b + p
                        more = not (last and p == 7)
                        if more:
                            maxes1(g + 1, (p + 1) % 8, 0)
                        dve.wait_ge(pt1_mm[1], g + 1)
                        dve.tensor_copy(PTs[:, 1, :], bank[5][:, 0:CAUSAL]).then_inc(pt1_ok[1], 1)
                        if more:
                            maxes1(g + 1, (p + 1) % 8, 1)
                    dve.wait_ge(exp1_ok[1], 8 * b + 8)
                    ch.link(dve.reciprocal(rsumC[:, :, :], sumC[:, :, :]))
                    ch.link(dve.tensor_scalar(rsumC[:, 0, :], rsumC[:, 0, :], row_valid, None, ALU.mult))
                    dve.wait_ge(pv1_mm, 8 * b + 8)
                    dve.tensor_tensor(oC_sb.rearrange("p t (h n) -> p (t h) n", n=HD1), bank[6][:, :].rearrange("p (c n) -> p c n", n=HD1),
                                      rsumC[:, :, :].rearrange("p t h -> p (t h)")[:, :, None].to_broadcast([P, 2 * H1, HD1]), ALU.mult).then_inc(o1_ok, 1)
                    dve.wait_ge(y1_mm, b + 1)
                    dve.tensor_tensor(Y[:, bass.ds(2 * b, 2), :], bank[7][:, :].rearrange("p (t n) -> p t n", t=2), bo_bc[:, None, :].to_broadcast([P, 2, D]), ALU.add)\
                        .then_inc(y1_ok, 1)

                maxes1(0, 0, 0)
                maxes1(0, 0, 1)
                with dve.Fori(0, BATCH - 1) as b:
                    ch.enter(b, 34)
                    batch(b, False)
                ch.leave(BATCH - 1)
                batch(BATCH - 1, True)
                dve.wait_ge(y1_ok, BATCH)
            if phases >= 4:
                dve.sem_inc(hf1_ok, 2)
                with dve.Fori(0, BATCH) as b:
                    ch.enter(b, 11)
                    add_normed(3, b)
                    normed(3, b, lambda u: hbuf[:, u, :], hr_n[3])
                    dve.wait_ge(tr_n[3], 2 * b + 2)
                ch.leave(BATCH)
                with dve.Fori(0, 4) as c:
                    for f in range(IC):
                        dve.wait_ge(sil1_ok, IC * c + f + 1)
                        dve.tensor_tensor(hFD[:, f, :], sil[:, f % 2, :], bank[2 * (f % 2) + 1][:, :], ALU.mult).then_inc(hf1_ok, 1)
                    for t in range(4):
                        dve.wait_ge(dn1_mm, 4 * c + t + 1)
                        dve.tensor_copy(tile(Y, 4 * c + t), bank[4 + t % 2][:, 0:D]).then_inc(dn1_ok, 1)
                dve.wait_ge(dn1_ok, TILES)
            with dve.Fori(0, BATCH) as b:
                ch.enter(b, 8)
                add_normed(4, b)
            ch.leave(BATCH)
            dve.nop().then_inc(xb_ok, 1)

        @block.tensor
        def _(pe):
            pe.wait_ge(cbf_ok, 2)
            with pe.Fori(0, PAIRS // 2) as i:
                for u in range(2):
                    pe.wait_ge(wp_in[u], 16 * i + 16)
                    w = wprep[:, u, :]
                    wn, wk = w[:, 0:2 * QL], w[:, 2 * QL:2 * QL + 2 * KVL]
                    wv, wo = w[:, 2 * QL + 2 * KVL:2 * QL + 4 * KVL], w[:, 2 * QL + 4 * KVL:]
                    for e in range(2):
                        ins = pe.matmul(bank[u][0:QL, e * KVL:(e + 1) * KVL], wn[:, e * QL:(e + 1) * QL], wk[:, e * KVL:(e + 1) * KVL], start=True, stop=True)
                    ins.then_inc(wp_m, 1)
                    for e in range(2):
                        ins = pe.matmul(bank[2 + u][e * 64:e * 64 + 64, 0:D], wv[:, e * KVL:(e + 1) * KVL], wo[:, e * D:(e + 1) * D], start=True, stop=True)
                    ins.then_inc(wp_v, 1)
                    pe.wait_ge(wp_me, 2 * i + u + 1)
                    pe.wait_ge(wp_ve, 2 * i + u + 1)
            pe.wait_ge(w_in, 48)
            with pe.Fori(0, BATCH) as b:
                for u in range(2):
                    pe.wait_ge(h_ready, 2 * b + u + 1)
                    for k in range(KD):
                        ins = pe.transpose(bank[4 + u][:, k * P:(k + 1) * P], hbuf[:, u, k * P:(k + 1) * P], ident[:, :])
                    ins.then_inc(h_tr, 1)
                for u in range(2):
                    pe.wait_ge(hT_ok, 2 * b + u + 1)
                    for k in range(KD):
                        ins = pe.matmul(bank[6 + u][:, 0:LAT], hTs[:, u, k, :], w_lat[:, k, :], start=(k == 0), stop=(k == KD - 1))
                    ins.then_inc(lat, 1)
                for u in range(2):
                    pe.wait_ge(qk_ready, 2 * b + u + 1)
                    pe.transpose(bank[4 + u][0:QL, 0:P], qn[:, u, :], ident[:, :])
                    pe.transpose(bank[u][:, P:2 * P], kst[:, u, 0:2, :].rearrange("p a n -> p (a n)"), ident[:, :])
                    pe.transpose(bank[u][:, 2 * P:3 * P], kst[:, u, 1:3, :].rearrange("p a n -> p (a n)"), ident[:, :]).then_inc(qk_tr, 1)
                pe.wait_ge(kT_ok, 2 * b + 2)
                pe.wait_ge(qlatT_ok, 2 * b + 2)
                pe.wait_ge(ckv_ok, 2 * b + 2)

            def q_rope_mm(g, b, u, first=False):
                pe.wait_ge(wst_ok, g + 1)
                if not first:
                    pe.wait_ge(rmul_ok, g)
                for k in (1, 2):
                    ins = pe.matmul(bank[3][:, (k - 1) * SEQ:k * SEQ], wst[:, u, k, :], qlatT[:, bass.ds(SEQ * b, SEQ)], start=True, stop=True)
                ins.then_inc(q_rr, 1)

            def q_abs_mm(g, b, u, first=False):
                if not first:
                    pe.wait_ge(q_abs, g)
                pe.matmul(bank[2][:, 0:SEQ], wst[:, u, 0, :], qlatT[:, bass.ds(SEQ * b, SEQ)], start=True, stop=True).then_inc(q_ab, 1)

            def scores(g, b, u, e, first=False):
                pe.wait_ge(q_rope, g + 1)
                pe.wait_ge(q_abs, g + 1)
                if not first:
                    pe.wait_ge(exp_ok[e], g)
                kT = (kTa, kTb)[e]
                for lo, n in ((0, P), (P, SEQ)):
                    pe.matmul(bank[e][:, lo:lo + n], qT[:, u, e, lo:lo + P], kT[:, bass.ds(SEQ * b, n)], start=True, stop=False)
                    ins = pe.matmul(bank[e][:, lo + n - P:lo + n], ident_bf, causal_bf, start=False, stop=True)
                ins.then_inc(s_mm[e], 1)

            def pt(g, u, e):
                pe.wait_ge(exp_ok[e], g + 1)
                for c in range(3):
                    ins = pe.transpose(bank[4 + e][:, c * P:(c + 1) * P], Pr[:, u, e, c * P:(c + 1) * P], ident[:, :])
                ins.then_inc(pt_mm[e], 1)

            def pv(g, b):
                for e in range(2):
                    pe.wait_ge(pt_ok[e], g + 1)
                    o0 = bank[6][:, e * KVL:(e + 1) * KVL]
                    o1 = bank[6][:, P + e * KVL:P + (e + 1) * KVL]
                    v0 = ckv[:, bass.ds(2 * b, 1), :].rearrange("p a n -> p (a n)")
                    v1 = ckv[:, bass.ds(2 * b + 1, 1), :].rearrange("p a n -> p (a n)")
                    pe.matmul(o0, PTs[:, e, 0:P], v0, start=True, stop=True)
                    pe.matmul(o1, PTs[:, e, P:2 * P], v0, start=True, stop=False)
                    ins = pe.matmul(o1, PTs[:, e, 2 * P:3 * P], v1, start=False, stop=True)
                ins.then_inc(pv_mm, 1)

            def oT(g):
                pe.wait_ge(o_ok, g + 1)
                for t in range(2):
                    ins = pe.transpose(bank[6][:, SEQ + t * P:SEQ + (t + 1) * P], o_sb[:, t, :], ident[:, :])
                ins.then_inc(oT_mm, 1)

            def proj(g, pair, done=False):
                pe.wait_ge(oT_ok, g + 1)
                for t in range(2):
                    ins = pe.matmul(bank[7][:, t * D:(t + 1) * D], oT_sb[:, t * P:(t + 1) * P], Wvo[:, bass.ds(pair, 1), :].rearrange("p a n -> p (a n)"),
                                    start=False, stop=done, skip_group_check=True)
                if done:
                    ins.then_inc(y_mm, 1)

            pe.wait_ge(z_ok, 1)
            for g in range(2):
                q_rope_mm(g, 0, g, g == 0)
                q_abs_mm(g, 0, g, g == 0)
            scores(0, 0, 0, 0, True)
            scores(0, 0, 0, 1, True)

            def step(g, b, pair, u, bs, bq, firsts=False):
                if bs is not None:
                    scores(g + 1, bs, 1 - u, 0)
                pt(g, u, 0)
                pt(g, u, 1)
                if bq is not None:
                    q_rope_mm(g + 2, bq, u)
                pv(g, b)
                if bs is not None:
                    scores(g + 1, bs, 1 - u, 1)
                oT(g)
                if bq is not None:
                    q_abs_mm(g + 2, bq, u)
                proj(g, pair, done=firsts)

            def batch(b, last):
                pe.matmul(bank[7][:, :], zbf[:, 0:P], zbf[:, :], start=True, stop=False, skip_group_check=True)
                with pe.Fori(0, 3) as i:
                    for u in range(2):
                        step(8 * b + 2 * i + u, b, 2 * i + u, u, b, b)
                step(8 * b + 6, b, 6, 0, b, None if last else b + 1)
                step(8 * b + 7, b, 7, 1, None if last else b + 1, None if last else b + 1, True)

            with pe.Fori(0, BATCH - 1) as b:
                batch(b, False)
                pe.wait_ge(y_ok, b + 1)
            batch(BATCH - 1, True)
            def transposes(i, b):
                for u in range(2):
                    pe.wait_ge(hr_n[i], 2 * b + u + 1)
                    for k in range(KD):
                        ins = pe.transpose(bank[4 + u][:, k * P:(k + 1) * P], hbuf[:, u, k * P:(k + 1) * P], ident[:, :])
                    ins.then_inc(tr_n[i], 1)

            if phases >= 2:
                pe.wait_ge(b_in, 96)
                with pe.Fori(0, BATCH) as b:
                    transposes(1, b)
                    for u in range(2):
                        pe.wait_ge(hT_n[1], 2 * b + u + 1)
                        for k in range(KD):
                            ins = pe.matmul(bank[6 + u][:, 0:E0 + 1], hTs[:, u, k, :], w_rt[:, k, :], start=(k == 0), stop=(k == KD - 1))
                        ins.then_inc(lg_mm, 1)
                    pe.wait_ge(lg_ok, 2 * b + 2)
                pe.wait_ge(mask_ok, 1)
                rank = bank[0]
                pe.matmul(rank[:, :], upper_bf, MBF[:, :, :].rearrange("p t e -> p (t e)"), start=True, stop=False)
                for t in range(TILES - 1):
                    n = TILES - 1 - t
                    ins = pe.matmul(rank[:, (t + 1) * E0:].rearrange("p (a e) -> p a e", a=n), ones_bf, MBF[:, t, None, :].to_broadcast([P, n, E0]),
                                    start=False, stop=(t == TILES - 2))
                ins.then_inc(rank_mm, 1)
                pe.wait_ge(slots_ok, 1)
                with pe.Fori(0, 4) as c:
                    for f in range(FSC):
                        pe.wait_ge(hf_ok, FSC * c + f + 1)
                        for j in range(2):
                            for k in range(KD):
                                ins = pe.matmul(bank[2 * (f % 2) + j][:, :], sw_gu[:, k, j * FSP + f * P:j * FSP + (f + 1) * P], xnT[:, k, bass.ds(512 * c, 512)],
                                                start=(k == 0), stop=(k == KD - 1))
                        ins.then_inc(gu_mm, 1)
                    pe.wait_ge(hf_ok, FSC * c + FSC + 2)
                    for t in range(4):
                        if t >= 2:
                            pe.wait_ge(dn_ok, 4 * c + t - 1)
                        for f in range(FSC):
                            ins = pe.matmul(bank[4 + t % 2][:, 0:D], hF[:, f, t * P:(t + 1) * P], sw_d[:, f, :], start=(f == 0), stop=(f == FSC - 1))
                        ins.then_inc(dn_mm, 1)
                    pe.wait_ge(dn_ok, 4 * c + 4)
                with pe.Fori(0, E0 // 2) as i:
                    for u in range(2):
                        e = 2 * i + u
                        wg, wd = wexp[:, u, 0:2 * KD * FE].rearrange("p (j k n) -> p j k n", j=2, k=KD), wexp[:, u, 2 * KD * FE:].rearrange("p (f n) -> p f n", f=FEC)
                        pe.wait_ge(xe_in[u], 16 * i + 16)
                        for k in range(KD):
                            ins = pe.transpose(bank[4][:, k * P:(k + 1) * P], Xe[:, u, k * P:(k + 1) * P], ident[:, :])
                        ins.then_inc(xe_tr, 1)
                        pe.wait_ge(xe_ok, e + 1)
                        pe.wait_ge(we_in[u], 16 * i + 16)
                        for j in range(2):
                            for f in range(FEC):
                                for k in range(KD):
                                    ins = pe.matmul(bank[5 + u][0:FEK, (2 * j + f) * P:(2 * j + f + 1) * P], wg[:, j, k, f * FEK:(f + 1) * FEK], XeT[:, u, k, :],
                                                    start=(k == 0), stop=(k == KD - 1))
                        ins.then_inc(ge_mm, 1)
                        pe.wait_ge(he_ok, e + 1)
                        for f in range(FEC):
                            ins = pe.matmul(bank[7][:, 0:D], hE[0:FEK, u, f * P:(f + 1) * P], wd[0:FEK, f, :], start=(f == 0), stop=(f == FEC - 1))
                        ins.then_inc(ye_mm, 1)
                        pe.wait_ge(ye_ok, e + 1)


            if phases >= 3:
                pe.wait_ge(cp_in, 64)
                with pe.Fori(0, BATCH // 2) as i:
                    for v in range(2):
                        b = 2 * i + v
                        transposes(2, b)
                        pe.wait_ge(nat_in[v], 48 * i + 48)
                        for m in range(3):
                            for k in range(KD):
                                dst = bank[7][:, (2 * m + k) * P:(2 * m + k + 1) * P] if m < 2 else bank[6][:, k * P:(k + 1) * P]
                                ins = pe.transpose(dst, wnat[:, v, m, k * P:(k + 1) * P], ident[:, :])
                        ins.then_inc(nat_tr, 1)
                        pe.wait_ge(hT_n[2], 2 * b + 2)
                        for c in range(KD):
                            for k in range(KD):
                                pe.matmul(bank[c][:, 0:SEQ], WqT[:, k, c * P:(c + 1) * P], hTs[:, :, k, :], start=(k == 0), stop=(k == KD - 1))
                        for k in range(KD):
                            pe.matmul(bank[2][:, 0:SEQ], WkT[:, k, :], hTs[:, :, k, :], start=(k == 0), stop=(k == KD - 1))
                        for u in range(2):
                            for k in range(KD):
                                ins = pe.matmul(bank[3][:, u * HD1:(u + 1) * HD1], hTs[:, u, k, :], WvT[:, k, :], start=(k == 0), stop=(k == KD - 1))
                        ins.then_inc(qkv_mm, 1)
                        pe.wait_ge(qk1_ok, 3 * b + 3)
                        pe.wait_ge(v1_ok, b + 1)
                        pe.wait_ge(nat_ok, b + 1)

                def scores1(g, b, p, e, first=False):
                    if e == 0 and p % 4 == 0:
                        pe.wait_ge(kbd_ok, b + 1)
                        pe.wait_ge(qst_ok, 2 * b + p // 4 + 1)
                    if not first:
                        pe.wait_ge(exp1_ok[e], g)
                    for lo, n in ((0, P), (P, SEQ)):
                        pe.matmul(bank[e][:, lo:lo + n], qst[:, p // 4, lo:lo + P], Kbd[:, bass.ds(b % 2, 1), 2 * (p % 4) + e, 0:n].rearrange("p a s -> p (a s)"), start=True, stop=False)
                        ins = pe.matmul(bank[e][:, lo + n - P:lo + n], ident_bf, strict_bf, start=False, stop=True)
                    ins.then_inc(s1_mm[e], 1)

                def pt1(g, p, e):
                    pe.wait_ge(exp1_ok[e], g + 1)
                    for c in range(3):
                        ins = pe.transpose(bank[4 + e][:, c * P:(c + 1) * P], Pr[:, p % 2, e, c * P:(c + 1) * P], ident[:, :])
                    ins.then_inc(pt1_mm[e], 1)

                def pv1(g, b, p):
                    v0, v1 = (vall[:, bass.ds(2 * b + t, 1), :].rearrange("p a n -> p (a n)") for t in range(2))
                    for e in range(2):
                        pe.wait_ge(pt1_ok[e], g + 1)
                        at = (2 * p + e) * HD1
                        o0, o1 = bank[6][:, at:at + HD1], bank[6][:, D + at:D + at + HD1]
                        pe.matmul(o0, PTs[:, e, 0:P], v0, start=True, stop=True)
                        pe.matmul(o1, PTs[:, e, P:2 * P], v0, start=True, stop=False)
                        ins = pe.matmul(o1, PTs[:, e, 2 * P:3 * P], v1, start=False, stop=True)
                    ins.then_inc(pv1_mm, 1)

                def batch(b, last):
                    for p in range(8):
                        g = 8 * b + p
                        more = not (last and p == 7)
                        nb = b + 1 if p == 7 else b
                        if more:
                            scores1(g + 1, nb, (p + 1) % 8, 0)
                        pt1(g, p, 0)
                        pt1(g, p, 1)
                        if more:
                            scores1(g + 1, nb, (p + 1) % 8, 1)
                        pv1(g, b, p)
                    pe.wait_ge(o1_ok, b + 1)
                    for c in range(KD):
                        for t in range(2):
                            ins = pe.transpose(bank[6][:, c * SEQ + t * P:c * SEQ + (t + 1) * P], oC_sb[:, t, c * P:(c + 1) * P], ident[:, :])
                    ins.then_inc(oT1_mm, 1)
                    pe.wait_ge(oT1_ok, b + 1)
                    for t in range(2):
                        for c in range(KD):
                            ins = pe.matmul(bank[7][:, t * D:(t + 1) * D], oTC_sb[:, c, t * P:(t + 1) * P], WoT[:, c, :], start=(c == 0), stop=(c == KD - 1))
                    ins.then_inc(y1_mm, 1)
                    pe.wait_ge(y1_ok, b + 1)

                scores1(0, 0, 0, 0, True)
                scores1(0, 0, 0, 1, True)
                with pe.Fori(0, BATCH - 1) as b:
                    batch(b, False)
                batch(BATCH - 1, True)
            if phases >= 4:
                with pe.Fori(0, BATCH) as b:
                    transposes(3, b)
                    pe.wait_ge(hk_ok, 2 * b + 2)
                with pe.Fori(0, 4) as c:
                    for f in range(IC):
                        pe.wait_ge(hf1_ok, IC * c + f + 1)
                        for j, wT in enumerate((gateT, upT)):
                            for k in range(KD):
                                ins = pe.matmul(bank[2 * (f % 2) + j][:, :], wT[:, k, f * P:(f + 1) * P], hTall[:, k, bass.ds(512 * c, 512)], start=(k == 0), stop=(k == KD - 1))
                        ins.then_inc(gu1_mm, 1)
                    pe.wait_ge(hf1_ok, IC * c + IC + 2)
                    for t in range(4):
                        if t >= 2:
                            pe.wait_ge(dn1_ok, 4 * c + t - 1)
                        for f in range(IC):
                            ins = pe.matmul(bank[4 + t % 2][:, 0:D], hFD[:, f, t * P:(t + 1) * P], downT[:, f, :], start=(f == 0), stop=(f == IC - 1))
                        ins.then_inc(dn1_mm, 1)
                    pe.wait_ge(dn1_ok, 4 * c + 4)


def layouts(inputs):
    a = {k: np.ascontiguousarray(v) for k, v in inputs.items()}
    f = np.float32
    d = {}
    d["x"] = a["L0_attn_x"].reshape(TILES, P, D).transpose(1, 0, 2)
    r = np.arange(P)
    tri = r[:, None] - r[None, :]
    d["cst"] = np.stack([np.eye(P), np.where(tri >= 0, 0.0, NEG), np.where(tri > 0, 0.0, NEG), np.where(tri < 0, 1.0, 0.0), np.ones((P, P))], 1).astype(f)
    inv = (1.0 / np.float32(10000.0) ** (np.arange(0, ROPE, 2, dtype=f) / f(ROPE))).astype(f)
    ang = np.outer(np.arange(SEQ, dtype=f), inv).astype(f)
    ang = np.concatenate([ang, ang], -1)
    cos, sin = np.cos(ang).astype(f), np.sin(ang).astype(f)
    sin = sin * np.where(np.arange(ROPE) % 2 == 0, -1, 1).astype(f)
    d["rope_q"] = np.stack([np.tile(cos.T, (2, 1)), np.tile(sin.T, (2, 1))], 1)
    d["rope_k"] = np.stack([cos, sin], 1).reshape(KD, P, 2, ROPE).transpose(1, 0, 2, 3)
    swap = np.arange(ROPE) ^ 1
    kva = a["L0_attn_w_kva"]
    d["w_lat"] = np.concatenate([a["L0_attn_w_qa"], kva, kva[:, KVL:][:, swap]], 1).reshape(KD, P, LAT).transpose(1, 0, 2)
    vecs = np.zeros((P, KVL + 2), f)
    vecs[:, 0:KVL] = a["L0_attn_kv_a_norm_w"][None]
    vecs[:, KVL] = np.tile(a["L0_attn_kv_a_norm_w"], 2)
    vecs[:QL, KVL + 1] = a["L0_attn_q_a_norm_w"]
    d["vecs"] = vecs
    wqb = a["L0_attn_w_qb"].reshape(QL, PAIRS, 2, NOPE + ROPE)
    rp = wqb[:, :, ::-1, NOPE:]
    d["w_rope"] = np.stack([rp, rp[..., swap]], 2).reshape(QL, PAIRS, 2, P)
    wkvb = a["L0_attn_w_kvb"].reshape(KVL, PAIRS, 2, NOPE + DV)
    wo = a["L0_attn_w_o"].reshape(PAIRS, 2, DV, D)
    d["wprep"] = np.concatenate([
        wqb[..., :NOPE].transpose(1, 3, 2, 0).reshape(PAIRS, P, 2 * QL),
        wkvb[..., :NOPE].transpose(1, 3, 2, 0).reshape(PAIRS, P, 2 * KVL),
        wkvb[..., NOPE:].transpose(1, 3, 2, 0).reshape(PAIRS, P, 2 * KVL),
        wo.transpose(0, 2, 1, 3).reshape(PAIRS, P, 2 * D)], 2)
    d["w_rt"] = np.concatenate([a["L0_ffn_w_router"], a["L0_ffn_w_shared_gate"]], 1).reshape(KD, P, E0 + 1).transpose(1, 0, 2)
    d["wn_bc"] = np.tile(a["L0_ffn_w_norm"][None], (P, 1))
    swg = np.zeros((D, 2, FSP), f)
    swg[:, 0, :FS], swg[:, 1, :FS] = a["L0_ffn_sw_gate"], a["L0_ffn_sw_up"]
    d["sw_gu"] = swg.reshape(KD, P, 2 * FSP).transpose(1, 0, 2)
    swd = np.zeros((FSC * P, D), f)
    swd[:FS] = a["L0_ffn_sw_down"]
    d["sw_d"] = swd.reshape(FSC, P, D).transpose(1, 0, 2)
    t, e, p = np.arange(TILES), np.arange(E0), np.arange(P)
    spare = SLOTS + (t[None, :, None] * E0 + e[None, None, :]) * P + p[:, None, None]
    d["slot_c"] = np.stack([np.broadcast_to(e[None, None] + 1, spare.shape), spare + 1], 1).astype(f)
    d["tok_i"] = (t[None, :] * P + p[:, None]).astype(np.int32)
    d["spare"] = np.tile((TOK + p)[:, None], (1, E0)).astype(np.int32)
    gu = np.stack([a["L0_ffn_w_gate"], a["L0_ffn_w_up"]], 1).reshape(E0, 2, KD, P, FE).transpose(0, 3, 1, 2, 4).reshape(E0, P, 2 * KD * FE)
    dn = np.zeros((E0, P, FEC, D), f)
    dn[:, :FEK] = a["L0_ffn_w_down"].reshape(E0, FEC, FEK, D).transpose(0, 2, 1, 3)
    d["wexp"] = np.concatenate([gu, dn.reshape(E0, P, FEC * D)], 2)
    n = np.arange(P * ROWS * SPAN).reshape(P * ROWS, SPAN)
    pos = np.linspace(0.0, NCTRL - 1.0, INTER * D, dtype=np.float64)
    pos = np.concatenate([pos, np.full(n.size - pos.size, pos[-1])])[n]
    cell = np.clip(np.floor(pos).astype(np.int64), 0, NCTRL - 2)
    row = np.arange(P * ROWS)[:, None]
    real = n < INTER * D
    assert np.all((cell == row) | (cell == row - 1) | ~real) and np.all((cell == row)[:, ALT:] | ~real[:, ALT:])
    own = np.where(cell == row, pos - row, 0.0).astype(f)
    was = np.where((cell == row - 1) & real, pos - (row - 1), 0.0).astype(f)[:, :ALT]
    d["frac"] = own.reshape(P, ROWS, SPAN)
    d["fracb"] = np.stack([was.reshape(P, ROWS, ALT), ((cell == row - 1) & real)[:, :ALT].astype(f).reshape(P, ROWS, ALT)], 1)
    at = np.clip(ROWS * p[:, None] - 2 + np.arange(ROWS + 4)[None], 0, NCTRL - 1)
    d["cpw"] = np.stack([a[k][at] for k in ("L1_ffn_gate_cp", "L1_ffn_up_cp", "L1_ffn_down_cp")], 1)
    split = lambda w: w.T.reshape(KD, P, -1).transpose(1, 0, 2).reshape(P, -1)
    bc = lambda v: np.tile(v[None], (P, 1))
    d["wC"] = np.concatenate([
        split(a["L1_attn_Wq"]), split(a["L1_attn_Wo"]), split(np.tile(a["L1_attn_Wk"], (8, 1))), split(a["L1_attn_Wv"]), bc(a["L1_attn_bo"]), bc(a["L1_attn_bv"]),
        a["L1_attn_bq"].reshape(KD, P).T, np.tile(a["L1_attn_bk"], 8)[:, None], (p[:, None] > 0).astype(f), (p[:, None] // HD1 == np.arange(8)[None]).astype(f)], 1)
    return {k: np.ascontiguousarray(v) for k, v in d.items()}


def kernel(**inputs):
    import concourse.bacc as bacc
    from concourse.bass_utils import run_bass_kernel_spmd

    nc = bacc.Bacc("TRN2", target_bir_lowering=False, num_devices=1)
    arrays = layouts(inputs)
    T = {k: nc.dram_tensor(f"in_{k}", v.shape, mybir.dt.from_np(v.dtype), kind="ExternalInput").ap() for k, v in arrays.items()}
    out = nc.dram_tensor("out_x", (P, TILES, D), F32, kind="ExternalOutput").ap()
    build_program(nc, T, out, 4)
    r = run_bass_kernel_spmd(nc, [{f"in_{k}": v for k, v in arrays.items()}], core_ids=[0])
    return r.results[0]["out_x"].transpose(1, 0, 2).reshape(BATCH, SEQ, D)
```

```python
from contextlib import ExitStack

import numpy as np
import concourse.bass as bass
from concourse import mybir

F32 = mybir.dt.float32
BF16 = mybir.dt.bfloat16
I32 = mybir.dt.int32
U32 = mybir.dt.uint32
ALU = mybir.AluOpType
ACT = mybir.ActivationFunctionType
AX = mybir.AxisListType

P = 128
BATCH, SEQ, D = 8, 256, 256
TOK = BATCH * SEQ
TILES = TOK // P
QT = 4
QN = TILES // QT
KD = D // P
LN_EPS = 1e-5
RMS_EPS = 1e-6
NEG = -1e30

H0 = 16
PAIRS = H0 // 2
QL, KVL = 96, 64
NOPE, ROPE, DV = 128, 64, 128
SCALE0 = 1.0 / float(np.sqrt(NOPE + ROPE))
LAT = QL + KVL + 2 * ROPE
CAUSAL = P + SEQ

E0, TOPK, FE, FS, CAP = 32, 4, 176, 704, 128
FEC, FEK = 2, FE // 2
FSC = -(-FS // P)
FSP = FSC * P
ROW = D + E0
SLOTS = E0 * CAP
TABLE = SLOTS + TILES * E0 * P
WEXP = 2 * KD * FE + FEC * D
PREP = 2 * QL + 4 * KVL + 2 * D

H1, HD1 = 16, 16
SCALE1 = 1.0 / float(np.sqrt(HD1))
WC = 1596
IC = 8

INTER = 1024
NCTRL = 2033
SPAN = 129
ROWS = 16
ALT = 16
SPLINE = P * ROWS * SPAN


class Tally:

    def __init__(self, eng, sem):
        self.eng, self.sem, self.base, self.k, self.outer = eng, sem, 0, 0, []

    def mark(self, ins):
        ins.then_inc(self.sem, 1)
        self.k += 1

    def wait(self):
        self.eng.wait_ge(self.sem, self.base + self.k)

    def link(self, ins):
        self.mark(ins)
        self.wait()

    def hold(self):
        self.wait()
        self.mark(self.eng.nop())

    def enter(self, i, per):
        self.outer.append((self.base, self.k, per))
        self.base, self.k = self.base + self.k + i * per, 0

    def leave(self, n):
        base, k, per = self.outer.pop()
        assert self.k == per, (self.k, per)
        self.base, self.k = base, k + n * per


def build_program(nc, T, out, phases=4):
    ctx = ExitStack()
    with ctx:
        def sb(name, shape, dt=F32):
            return ctx.enter_context(nc.sbuf_tensor(name, list(shape), dt))

        def sem(name):
            return ctx.enter_context(nc.semaphore(name))

        ident = sb("ident", [P, P])
        cst = sb("cst", [P, 5, P])
        cbf = sb("cbf", [P, 5, P], BF16)
        zbf = sb("zbf", [P, 512], BF16)
        ident_bf, causal_bf, strict_bf, upper_bf, ones_bf = (cbf[:, i, :] for i in range(5))
        mhalf = sb("mhalf", [P, 4])
        vecs = sb("vecs", [P, KVL + 2])
        X = sb("X", [P, TILES, D])
        R0 = sb("R0", [P, KD * TOK])
        R1 = sb("R1", [P, TILES * D])
        R2 = sb("R2", [P, TILES * ROW])
        R3 = sb("R3", [P, PAIRS * (3 * P + D)])
        R4 = sb("R4", [P, 3 * KD * INTER])
        R5 = sb("R5", [P, 2 * PREP])
        Y = R1[:, :].rearrange("p (t n) -> p t n", t=TILES)
        stats = sb("stats", [P, 2, 2, QT, 6])
        mv = sb("mv", [P, 2, TILES, 2])
        norm = sb("norm", [P, 2, TILES, 2])
        rms = sb("rms", [P, TILES])
        hbuf = sb("hbuf", [P, QT, D])
        sil = sb("sil", [P, 2, 512])
        R6 = sb("R6", [P, 2176])
        rope_q = R6[:, 0:512].rearrange("p (a t) -> p a t", a=2)
        rope_k = R6[:, 512:768].rearrange("p (t a n) -> p t a n", t=KD, a=2)
        w_lat = R6[:, 768:1344].rearrange("p (k n) -> p k n", k=KD)
        Wq = R3[0:QL, 0:PAIRS * 3 * P].rearrange("p (a k m) -> p a k m", a=PAIRS, k=3)
        Wvo = R3[:, PAIRS * 3 * P:].rearrange("p (a n) -> p a n", a=PAIRS)
        wprep = R5[:, 0:2 * PREP].rearrange("p (u n) -> p u n", u=2)
        ms = sb("ms", [P, TILES, 2])
        LATS = R4[:, 0:TILES * LAT].rearrange("p (t n) -> p t n", t=TILES)
        sq_q = R1[:, 0:TILES * QL].rearrange("p (t n) -> p t n", t=TILES)
        sq_kv = R1[:, TILES * QL:TILES * (QL + KVL)].rearrange("p (t n) -> p t n", t=TILES)
        qn = R1[:, 0:2 * QT * QL].rearrange("p (v u n) -> p v u n", v=2, u=QT)
        oK = 2 * QT * QL
        kst = R1[:, oK:oK + 2 * QT * 3 * KVL].rearrange("p (v u a n) -> p v u a n", v=2, u=QT, a=3)
        oK2 = oK + 2 * QT * 3 * KVL
        kr2 = R1[:, oK2:oK2 + 2 * QT * 2 * ROPE].rearrange("p (v u a n) -> p v u a n", v=2, u=QT, a=2)
        kTa = R0[:, 0:TOK]
        kTb = R0[:, TOK:2 * TOK]
        qlatT = R2[0:QL, 0:TOK]
        ckv = R2[:, TOK:TOK + TILES * KVL].rearrange("p (t n) -> p t n", t=TILES)
        wst = sb("wst", [QL, 2, 3, P])
        rmul = sb("rmul", [P, 2, 2, SEQ])
        qT = sb("qT", [P, 2, 2, SEQ])
        hTs = rmul[:, :, :, :].rearrange("p a b n -> p (a b n)").rearrange("p (k t) -> p k t", k=KD)
        nmax = sb("nmax", [P, 2, 2, 2])
        Pr = sb("Pr", [P, 2, 2, CAUSAL])
        sums = sb("sums", [P, 2, 2, 2])
        rsum = sb("rsum", [P, 2, 2])
        PTs = sb("PTs", [P, 2, CAUSAL])
        o_sb = sb("o_sb", [P, 2, P])
        oT_sb = sb("oT_sb", [P, SEQ])
        w_rt = sb("w_rt", [P, KD, E0 + 1])
        wn_bc = sb("wn_bc", [P, D])
        sw_gu = sb("sw_gu", [P, KD, 2 * FSP])
        sw_d = sb("sw_d", [P, FSC, D])
        INP = Y
        xnT = R0[:, :].rearrange("p (k t) -> p k t", k=KD)
        XNP = R2[:, :].rearrange("p (t n) -> p t n", t=TILES)
        ROUTE = TILES * E0
        rt = R3[:, 0:6 * ROUTE].rearrange("p (a t e) -> p a t e", a=6, t=TILES)
        LG, EXPL, MSK, SLOT, INV = rt[:, 0], rt[:, 1], rt[:, 2], rt[:, 3], rt[:, 4]
        slot_c = sb("slot_c", [P, 2, TILES, E0])
        o5 = 6 * ROUTE
        PP = R3[:, o5:o5 + TILES * 40].rearrange("p (t e) -> p t e", t=TILES)
        RP = R3[:, o5 + TILES * 40:o5 + TILES * 80].rearrange("p (t e) -> p t e", t=TILES)
        MBF = sb("MBF", [P, TILES, E0], BF16)
        top8 = sb("top8", [P, TILES, 8])
        slot8 = sb("slot8", [P, TILES, 8])
        slot_i = sb("slot_i", [P, TILES, 4], I32)
        tok_i = sb("tok_i", [P, TILES], I32)
        slot_st = sb("slot_st", [P, 2, 4], I32)
        tok_st = sb("tok_st", [P, 2], I32)
        table_sb = sb("table_sb", [P, E0], I32)
        idx_st = sb("idx_st", [P, 4], I32)
        add_idx = sb("add_idx", [P, 2], I32)
        rmx = sb("rmx", [P, TILES])
        rsm = sb("rsm", [P, TILES])
        gate = sb("gate", [P, TILES])
        zer = sb("zer", [P, ROW])
        hF = sb("hF", [P, FSC, 512])
        wexp = R3[:, 0:4 * WEXP].rearrange("p (u n) -> p u n", u=4)
        Xe = Pr[:, :, :, :].rearrange("p a b n -> p (a b n)")[:, 0:4 * ROW].rearrange("p (u n) -> p u n", u=4)
        XeT = rmul[:, 0, :, :].rearrange("p k (u t) -> p u k t", u=2)
        gE = sil[:, :, 0:FE]
        hE = sil[:, :, FE:2 * FE]
        hET = qT[:, 0, :, :]
        yE = qT[:, 1, :, :]
        cpw = sb("cpw", [P, 3, ROWS + 4])
        coef = sb("coef", [P, 3, 4, ROWS + 1])
        ctmp = sb("ctmp", [P, 3, ROWS + 1])
        SP_N = ROWS * SPAN
        AL_N = ROWS * ALT
        frac = R4[:, 0:SP_N].rearrange("p (r n) -> p r n", r=ROWS)
        samp = R4[:, SP_N:2 * SP_N].rearrange("p (r n) -> p r n", r=ROWS)
        fracb = R4[:, 2 * SP_N:2 * SP_N + AL_N].rearrange("p (r n) -> p r n", r=ROWS)
        before = R4[:, 2 * SP_N + AL_N:2 * SP_N + 2 * AL_N].rearrange("p (r n) -> p r n", r=ROWS)
        sampb = R4[:, 2 * SP_N + 2 * AL_N:2 * SP_N + 3 * AL_N].rearrange("p (r n) -> p r n", r=ROWS)
        wC = R6[:, 0:WC]
        WqT = wC[:, 0:512].rearrange("p (k n) -> p k n", k=KD)
        WoT = wC[:, 512:1024].rearrange("p (k n) -> p k n", k=KD)
        WkT = wC[:, 1024:1280].rearrange("p (k n) -> p k n", k=KD)
        WvT = wC[:, 1280:1312].rearrange("p (k n) -> p k n", k=KD)
        bo_bc = wC[:, 1312:1568]
        bv_bc = wC[:, 1568:1584]
        bq, bk, row_valid = wC[:, 1584:1586], wC[:, 1586:1587], wC[:, 1587:1588]
        head_row = wC[:, 1588:1596]
        qTall = R0[:, :].rearrange("p (c t) -> p c t", c=KD)
        Kbd = R2[:, 0:2 * 8 * SEQ].rearrange("p (u j s) -> p u j s", u=2, j=8)
        kTr = R3[:, 0:TOK]
        vall = R3[:, TOK:TOK + TILES * HD1].rearrange("p (t n) -> p t n", t=TILES)
        oC = TOK + TILES * HD1
        qst = R3[:, oC:oC + 512].rearrange("p (c t) -> p c t", c=KD)
        oC_sb = R3[:, oC + 512:oC + 1024].rearrange("p (t n) -> p t n", t=2)
        oTC_sb = R3[:, oC + 1024:oC + 1536].rearrange("p (c t) -> p c t", c=KD)
        PTc = (PTs, R5[:, 0:2 * CAUSAL].rearrange("p (e n) -> p e n", e=2))
        sumC = sb("sumC", [P, 2, H1])
        rsumC = sb("rsumC", [P, 2, H1])
        gateT = R4[:, 0:KD * INTER].rearrange("p (k i) -> p k i", k=KD)
        upT = R4[:, KD * INTER:2 * KD * INTER].rearrange("p (k i) -> p k i", k=KD)
        downT = R4[:, 2 * KD * INTER:].rearrange("p (f n) -> p f n", f=IC)
        wnat = R5[:, 0:3 * D].rearrange("p (m n) -> p m n", m=3)
        hTall = R0[:, :].rearrange("p (k t) -> p k t", k=KD)
        hFD = R2[:, 0:IC * 512].rearrange("p (f t) -> p f t", f=IC)

        bank = [ctx.enter_context(nc.psum_tensor(f"bank{i}", [P, 512], F32)) for i in range(8)]
        rows_d = nc.dram_tensor("rows_d", (TOK + CAP, ROW), F32).ap()
        acc_d = nc.dram_tensor("acc_d", (TOK + CAP, D), F32).ap()
        spline_d = nc.dram_tensor("spline_d", (3, SPLINE), F32).ap()
        table_d = nc.dram_tensor("table_d", (TABLE, 1), I32).ap()

        c_in = sem("c_in"); x_in = sem("x_in"); w_in = sem("w_in"); fin_out = sem("fin_out")
        cbf_ok = sem("cbf_ok"); z_ok = sem("z_ok"); vec_ok = sem("vec_ok")
        wp_in = [sem(f"wp_in{u}") for u in range(2)]
        wp_m = sem("wp_m"); wp_v = sem("wp_v"); wp_me = sem("wp_me"); wp_ve = sem("wp_ve"); wr_ok = sem("wr_ok")
        dch = sem("dch"); pch = sem("pch")
        lat = sem("lat"); lat_ok = sem("lat_ok")
        ms_ok = sem("ms_ok"); msr_ok = sem("msr_ok"); rs_ok = sem("rs_ok"); ckv_ok = sem("ckv_ok"); qk_ready = sem("qk_ready"); qk_tr = sem("qk_tr"); kT_ok = sem("kT_ok")
        wst_ok = sem("wst_ok"); wst_free = sem("wst_free"); q_rr = sem("q_rr"); q_ab = sem("q_ab"); rmul_ok = sem("rmul_ok")
        q_rope = sem("q_rope"); q_abs = sem("q_abs")
        s_mm = [sem("s_mm_e"), sem("s_mm_o")]; max_ok = [sem("max_e"), sem("max_o")]; exp_ok = [sem("exp_e"), sem("exp_o")]
        pt_mm = [sem("pt_e"), sem("pt_o")]; pt_ok = [sem("ptc_e"), sem("ptc_o")]
        pv_mm = sem("pv_mm"); o_ok = sem("o_ok"); oT_mm = sem("oT_mm"); oT_ok = sem("oT_ok")
        y_mm = sem("y_mm"); y_ok = sem("y_ok")
        mvy, ny, lny, mvx, nx, h_n, tr_n, hT_n = (sem(n) for n in ("mvy", "ny", "lny", "mvx", "nx", "h_n", "tr_n", "hT_n"))
        b_in = sem("b_in"); b_pool = sem("b_pool"); inp_ok = sem("inp_ok"); rms_ok = sem("rms_ok"); row_ok = sem("row_ok"); xnT_ok = sem("xnT_ok")
        lg_mm = sem("lg_mm"); lg_ok = sem("lg_ok"); lgs_ok = sem("lgs_ok"); lge_ok = sem("lge_ok"); mask_ok = sem("mask_ok"); rank_mm = sem("rank_mm")
        probs_ok = sem("probs_ok"); slots_ok = sem("slots_ok"); rows_out = sem("rows_out"); sc_st = sem("sc_st"); sc_out = [sem(f"sc_out{u}") for u in range(2)]
        table_in = sem("table_in"); init_out = sem("init_out")
        gu_mm = sem("gu_mm"); sil_ok = sem("sil_ok"); hf_ok = sem("hf_ok"); dn_mm = sem("dn_mm"); dn_ok = sem("dn_ok"); acc_out = sem("acc_out"); added = sem("added")
        we_in = [sem(f"we_in{u}") for u in range(4)]; idx_ok = sem("idx_ok"); adx_ok = sem("adx_ok"); xe_in = [sem(f"xe_in{u}") for u in range(4)]
        xe_tr = sem("xe_tr"); xe_ok = sem("xe_ok"); ge_mm = sem("ge_mm"); se_ok = sem("se_ok"); he_ok = sem("he_ok"); he_tr = sem("he_tr"); heT_ok = sem("heT_ok"); ye_mm = sem("ye_mm"); ye_ok = sem("ye_ok")
        cp_in = sem("cp_in"); cf_ok = sem("cf_ok"); samp_ok = sem("samp_ok"); spl_out = sem("spl_out"); nat_in = sem("nat_in")
        qkv_mm = sem("qkv_mm"); bq_ok = sem("bq_ok"); rs1_ok = sem("rs1_ok"); qk1_ok = sem("qk1_ok"); v1_ok = sem("v1_ok"); qst_ok = sem("qst_ok"); kbd_ok = sem("kbd_ok")
        s1_mm = [sem("s1_mm_e"), sem("s1_mm_o")]; max1_ok = [sem("max1_e"), sem("max1_o")]; exp1_ok = [sem("exp1_e"), sem("exp1_o")]
        pt1_mm = [sem("pt1_e"), sem("pt1_o")]; pt1_ok = [sem("ptc1_e"), sem("ptc1_o")]
        pv1_mm = sem("pv1_mm"); o1_ok = sem("o1_ok"); oT1_mm = sem("oT1_mm"); oT1_ok = sem("oT1_ok"); y1_mm = sem("y1_mm"); y1_ok = sem("y1_ok")
        gu1_mm = sem("gu1_mm"); sil1_ok = sem("sil1_ok"); hf1_ok = sem("hf1_ok"); dn1_mm = sem("dn1_mm"); dn1_ok = sem("dn1_ok")
        add_out = sem("add_out"); back_in = sem("back_in"); xb_ok = sem("xb_ok")

        latent_banks = ((4, 5, 6), (7, 0, 1))

        block = ctx.enter_context(nc.Block())

        @block.sync
        def _(sp):
            sp.dma_start(cst[:, :, :], T["cst"]).then_inc(c_in, 16)
            sp.dma_start(vecs[:, :], T["vecs"]).then_inc(c_in, 16)
            sp.dma_start(Wq[:, :, 1:3, :], T["w_rope"]).then_inc(c_in, 16)
            sp.dma_start(rope_k, T["rope_k"]).then_inc(w_in, 16)
            sp.dma_start(rope_q, T["rope_q"]).then_inc(w_in, 16)
            for u in range(2):
                sp.dma_start(wprep[:, u, :], T["wprep"][u, :, :]).then_inc(wp_in[u], 16)
            with sp.Fori(1, PAIRS // 2) as i:
                for u in range(2):
                    sp.wait_ge(wp_v, 2 * i + u - 1)
                    sp.dma_start(wprep[:, u, :], T["wprep"][bass.ds(2 * i + u, 1), :, :].rearrange("a p n -> (a p) n")).then_inc(wp_in[u], 16)

            if phases >= 2:
                for name, dst in (("w_rt", w_rt), ("wn_bc", wn_bc), ("sw_gu", sw_gu), ("sw_d", sw_d), ("slot_c", slot_c), ("tok_i", tok_i)):
                    sp.dma_start(dst[...], T[name]).then_inc(b_in, 16)
                sp.dma_start(table_d[0:SLOTS, :].rearrange("(p a) b -> p (a b)", p=P), T["spare"]).then_inc(init_out, 16)
                sp.wait_ge(z_ok, 1)
                sp.dma_start(rows_d[TOK:, :], zer[:, :]).then_inc(init_out, 16)
                sp.dma_start(acc_d[TOK:, :], zer[:, 0:D]).then_inc(init_out, 16)
                sp.wait_ge(qk_ready, QN)
                sp.wait_ge(ckv_ok, QN)
                sp.dma_start(frac, T["frac"]).then_inc(cp_in, 16)
                sp.dma_start(R4[:, 2 * SP_N:2 * SP_N + 2 * AL_N].rearrange("p (a r n) -> p a r n", a=2, r=ROWS), T["fracb"]).then_inc(cp_in, 16)
                sp.dma_start(cpw[:, :, :], T["cpw"]).then_inc(cp_in, 16)
                sp.wait_ge(y_ok, BATCH)
                sp.dma_start(wC, T["wC"]).then_inc(cp_in, 16)
                sp.wait_ge(probs_ok, 1)
                sp.wait_ge(row_ok, QN)
                sp.dma_start(rows_d[0:TOK, :].rearrange("(t p) n -> p t n", p=P), XNP).then_inc(rows_out, 16)
                sp.wait_ge(slots_ok, 1)
                for u in range(4):
                    sp.dma_start(wexp[:, u, :], T["wexp"][u, :, :]).then_inc(we_in[u], 16)
                def acc_store(c):
                    sp.wait_ge(dn_ok, 4 * c + 4)
                    sp.dma_start(acc_d[bass.ds(4 * P * c, 4 * P), :].rearrange("(t p) n -> p t n", p=P), INP[:, bass.ds(4 * c, 4), :]).then_inc(acc_out, 16)

                with sp.Fori(0, 3) as c:
                    sp.wait_ge(samp_ok, c + 1)
                    sp.dma_start(spline_d[bass.ds(c, 1), :].rearrange("a (p n) -> (a p) n", p=P), samp.rearrange("p r n -> p (r n)")).then_inc(spl_out, 16)
                    acc_store(c)
                acc_store(3)

                def natural(j):
                    for m in range(2):
                        sp.dma_start(wnat[:, m, :], spline_d[m, bass.ds(P * D * j, P * D)].rearrange("(p n) -> p n", p=P)).then_inc(nat_in, 16)
                    sp.dma_start(wnat[:, 2, :].rearrange("p (k i) -> p k i", k=KD),
                                 spline_d[2, 0:D * INTER].rearrange("(k p j i) -> p j k i", k=KD, p=P, j=IC)[:, bass.ds(j, 1), :, :].rearrange("p a k i -> p (a k) i")).then_inc(nat_in, 16)

                sp.wait_ge(spl_out, 48)
                natural(0)
                with sp.Fori(1, E0 // 4) as i:
                    for u in range(4):
                        sp.wait_ge(ye_mm, 4 * i + u - 3)
                        sp.dma_start(wexp[:, u, :], T["wexp"][bass.ds(4 * i + u, 1), :, :].rearrange("a p n -> (a p) n")).then_inc(we_in[u], 16)
                        if u == 3:
                            natural(i)
                sp.wait_ge(add_out, 16 * E0)
                sp.dma_start(Y, acc_d[0:TOK, :].rearrange("(t p) n -> p t n", p=P)).then_inc(back_in, 16)
        @block.gpsimd
        def _(pool):
            ch = Tally(pool, pch)
            ch.mark(pool.memset(zbf[:, :], 0.0))
            ch.mark(pool.memset(mhalf[:, :], -0.5))
            ch.mark(pool.memset(zer[:, :], 0.0))
            ch.wait()
            pool.nop().then_inc(z_ok, 1)

            def roots(k, i, after=None):
                src_sem, done = ((mvy, ny), (mvx, nx))[k]
                for q in range(QN):
                    quarter = bass.ds(QT * q, QT)
                    inv, off = norm[:, k, quarter, 0], norm[:, k, quarter, 1]
                    pool.wait_ge(src_sem, QN * (i if k else i - 1) + q + 1)
                    ch.mark(pool.nop())
                    ch.mark(pool.tensor_scalar(off, mv[:, k, quarter, 0], -1.0, None, ALU.mult))
                    ch.link(pool.tensor_scalar(inv, mv[:, k, quarter, 1], LN_EPS, None, ALU.add))
                    ch.link(pool.tensor_tensor(inv, inv, mhalf[:, :], ALU.pow))
                    pool.tensor_tensor(off, off, inv, ALU.mult).then_inc(done, 1)
                    if after is not None:
                        after(quarter, inv)

            def ln_roots(i):
                roots(0, i)
                if i < 4:
                    roots(1, i)

            roots(1, 0)
            pool.wait_ge(msr_ok, 1)
            ch.link(pool.tensor_scalar(ms[:, :, :], ms[:, :, :], RMS_EPS, None, ALU.add))
            pool.tensor_tensor(ms[:, :, :], ms[:, :, :], mhalf[:, None, 0:2].to_broadcast([P, TILES, 2]), ALU.pow).then_inc(rs_ok, 1)
            with pool.Fori(0, QN) as q:
                quarter = bass.ds(QT * q, QT)
                pool.wait_ge(rs_ok, 1)
                pool.tensor_tensor(ckv[:, quarter, :], LATS[:, quarter, QL:QL + KVL], ms[:, quarter, 1, None].to_broadcast([P, QT, KVL]), ALU.mult).then_inc(ckv_ok, 1)
            pool.wait_ge(wr_ok, 1)
            pool.wait_ge(wp_me, PAIRS + 2)

            def stage(g, pair, u, first=False):
                if not first:
                    pool.wait_ge(q_ab, g - 1)
                    pool.nop().then_inc(wst_free, 1)
                pool.tensor_copy(wst[:, u, :, :], Wq[:, bass.ds(pair, 1), :, :].rearrange("p a k m -> p (a k) m")).then_inc(wst_ok, 1)
                pool.wait_ge(wst_ok, g + 1)
                ch.mark(pool.nop())

            def rope_sum(g, u):
                pool.wait_ge(rmul_ok, g + 1)
                ch.link(pool.tensor_tensor(qT[64:128, u, 0, :], rmul[64:128, u, 0, :], rmul[64:128, u, 1, :], ALU.add))
                pool.tensor_tensor(qT[0:64, u, 1, :], rmul[0:64, u, 0, :], rmul[0:64, u, 1, :], ALU.add).then_inc(q_rope, 1)
                pool.wait_ge(q_rope, g + 1)
                ch.mark(pool.nop())

            stage(0, 0, 0, True)
            stage(1, 1, 1, True)
            rope_sum(0, 0)
            rope_sum(1, 1)

            STEP = 3
            def batch(b, last):
                with pool.Fori(0, 3) as i:
                    ch.enter(i, 2 * STEP)
                    for u in range(2):
                        g = 8 * b + 2 * i + u
                        stage(g + 2, 2 * i + u + 2, u)
                        rope_sum(g + 2, u)
                ch.leave(3)
                if not last:
                    for u in range(2):
                        g = 8 * b + 6 + u
                        stage(g + 2, u, u)
                        rope_sum(g + 2, u)

            with pool.Fori(0, BATCH - 1) as b:
                ch.enter(b, 8 * STEP)
                batch(b, False)
            ch.leave(BATCH - 1)
            batch(BATCH - 1, True)
            if phases >= 2:
                roots(0, 1)

                def rms_root(quarter, inv):
                    w = rms[:, quarter]
                    ch.wait()
                    ch.link(pool.tensor_tensor(w, mv[:, 1, quarter, 1], inv, ALU.mult))
                    ch.link(pool.tensor_tensor(w, w, inv, ALU.mult))
                    ch.link(pool.tensor_scalar(w, w, RMS_EPS, None, ALU.add))
                    pool.tensor_tensor(w, w, mhalf[:, :], ALU.pow).then_inc(rms_ok, 1)

                roots(1, 1, rms_root)
                pool.wait_ge(slots_ok, 1)
                pool.wait_ge(b_in, 96)
                pool.wait_ge(init_out, 48)
                ch.mark(pool.nop())
                with pool.Fori(0, BATCH) as b:
                    ch.enter(b, 2)
                    for u in range(2):
                        ch.mark(pool.nop())
                        pool.tensor_copy(slot_st[:, u, :], slot_i[:, bass.ds(2 * b + u, 1), :].rearrange("p a k -> p (a k)")).then_inc(sc_st, 1)
                        pool.tensor_copy(tok_st[:, u:u + 1], tok_i[:, bass.ds(2 * b + u, 1)]).then_inc(sc_st, 1)
                    pool.wait_ge(sc_st, 4 * b + 4)
                    pool.nop().then_inc(b_pool, 1)
                    for u in range(2):
                        for k in range(TOPK):
                            pool.indirect_dma_start(out=table_d, out_offset=bass.IndirectOffsetOnAxis(ap=slot_st[:, u, k:k + 1], axis=0),
                                                    in_=tok_st[:, u:u + 1], in_offset=None).then_inc(sc_out[u], 16)
                    for u in range(2):
                        pool.wait_ge(sc_out[u], 64 * b + 64)
                    pool.nop().then_inc(b_pool, 1)
                ch.leave(BATCH)
                pool.dma_start(table_sb[:, :], table_d[0:SLOTS, :].rearrange("(p a) b -> p (a b)", p=P)).then_inc(table_in, 16)
                pool.wait_ge(table_in, 16)
                pool.wait_ge(rows_out, 16)
                ch.mark(pool.nop())

                def gather(e, u):
                    pool.tensor_copy(idx_st[:, u:u + 1], table_sb[:, bass.ds(e, 1)]).then_inc(idx_ok, 1)
                    pool.wait_ge(idx_ok, e + 1)
                    ch.mark(pool.nop())
                    pool.indirect_dma_start(out=Xe[:, u, :], out_offset=None, in_=rows_d, in_offset=bass.IndirectOffsetOnAxis(ap=idx_st[:, u:u + 1], axis=0))\
                        .then_inc(xe_in[u], 16)

                def step(e, u, more):
                    pool.wait_ge(add_out, 16 * e)
                    pool.nop().then_inc(added, 1)
                    pool.tensor_copy(add_idx[:, u % 2:u % 2 + 1], table_sb[:, bass.ds(e, 1)]).then_inc(adx_ok, 1)
                    pool.wait_ge(adx_ok, e + 1)
                    pool.wait_ge(ye_ok, e + 1)
                    ch.mark(pool.nop())
                    pool.indirect_dma_start(out=acc_d, out_offset=bass.IndirectOffsetOnAxis(ap=add_idx[:, u % 2:u % 2 + 1], axis=0), in_=yE[:, u % 2, :], in_offset=None,
                                            compute_op=ALU.add).then_inc(add_out, 16)
                    if more:
                        ch.mark(pool.nop())
                        gather(e + 4, u)

                for e in range(4):
                    gather(e, e)
                pool.wait_ge(acc_out, 64)
                ch.mark(pool.nop())
                with pool.Fori(0, E0 // 4 - 1) as i:
                    ch.enter(i, 12)
                    for u in range(4):
                        step(4 * i + u, u, True)
                ch.leave(E0 // 4 - 1)
                for u in range(4):
                    step(E0 - 4 + u, u, False)
            if phases >= 3:
                ln_roots(2)
                pool.wait_ge(qk1_ok, QN)
                ch.mark(pool.nop())

                def key_blocks(b):
                    pool.tensor_tensor(Kbd[:, bass.ds(b % 2, 1), :, :].rearrange("p a j s -> p (a j) s"), kTr[:, None, bass.ds(SEQ * b, SEQ)].to_broadcast([P, 8, SEQ]),
                                       head_row[:, :, None].to_broadcast([P, 8, SEQ]), ALU.mult).then_inc(kbd_ok, 1)
                    pool.wait_ge(kbd_ok, b + 1)
                    ch.mark(pool.nop())

                def queries(b, c):
                    pool.tensor_copy(qst[:, c, :], qTall[:, c, bass.ds(SEQ * b, SEQ)]).then_inc(qst_ok, 1)
                    pool.wait_ge(qst_ok, 2 * b + c + 1)
                    ch.mark(pool.nop())

                key_blocks(0)
                queries(0, 0)
                queries(0, 1)
                key_blocks(1)

                def batch(b, more):
                    for c in range(2):
                        pool.wait_ge(s1_mm[1], 8 * b + 4 * c + 4)
                        ch.mark(pool.nop())
                        queries(b + 1, c)
                    if more:
                        key_blocks(b + 2)

                with pool.Fori(0, BATCH - 2) as b:
                    ch.enter(b, 5)
                    batch(b, True)
                ch.leave(BATCH - 2)
                batch(BATCH - 2, False)
            if phases >= 4:
                ln_roots(3)
            ln_roots(4)

        @block.scalar
        def _(act):
            act.dma_start(X[:, 0:8, :], T["x"][:, 0:8, :]).then_inc(x_in, 16)
            act.dma_start(X[:, 8:16, :], T["x"][:, 8:16, :]).then_inc(x_in, 16)
            act.dma_start(w_lat, T["w_lat"]).then_inc(w_in, 16)

            def tile(buf, t):
                return buf[:, bass.ds(t, 1), :].rearrange("p a n -> p (a n)")

            def scaled(k, t, dst, src):
                return act.activation(dst, src, ACT.Identity, scale=norm[:, k, bass.ds(t, 1), 0], bias=norm[:, k, bass.ds(t, 1), 1])

            def output_norms(i):
                with act.Fori(0, QN) as q:
                    act.wait_ge(ny, QN * (i - 1) + q + 1)
                    for u in range(QT):
                        ins = scaled(0, QT * q + u, tile(Y, QT * q + u), tile(Y, QT * q + u))
                    ins.then_inc(lny, 1)

            def x_norms(i, q):
                act.wait_ge(nx, QN * i + q + 1)
                act.wait_ge(tr_n, TILES * i + QT * q)
                for u in range(QT):
                    scaled(1, QT * q + u, hbuf[:, u, :], tile(X, QT * q + u)).then_inc(h_n, 1)

            with act.Fori(0, QN) as q:
                x_norms(0, q)
                for u in range(QT):
                    act.wait_ge(lat, QT * q + u + 1)
                    act.activation(tile(LATS, QT * q + u), bank[4 + u][:, 0:LAT], ACT.Copy).then_inc(lat_ok, 1)
            act.wait_ge(lat_ok, TILES)
            act.activation(sq_q, LATS[:, :, 0:QL], ACT.Square, scale=float(QL ** -0.5)).then_inc(ms_ok, 1)
            act.activation(sq_kv, LATS[:, :, QL:QL + KVL], ACT.Square, scale=float(KVL ** -0.5)).then_inc(ms_ok, 1)
            act.wait_ge(c_in, 48)
            with act.Fori(0, PAIRS // 2) as i:
                for u in range(2):
                    act.wait_ge(wp_v, 2 * i + u + 1)
                    act.activation(Wvo[:, bass.ds(2 * i + u, 1), :].rearrange("p a n -> p (a n)"), bank[2 + u][:, 0:D], ACT.Copy, scale=vecs[:, KVL:KVL + 1]).then_inc(wp_ve, 1)
            with act.Fori(0, QN // 2) as i:
                for v in range(2):
                    q = 2 * i + v
                    act.wait_ge(qk_tr, q + 1)
                    for dst, src in zip((qlatT, kTa, kTb), latent_banks[v]):
                        ins = act.activation(dst[:, bass.ds(QT * P * q, QT * P)], bank[src][0:dst.shape[0], :], ACT.Copy)
                    ins.then_inc(kT_ok, 1)

            def abs_copy(g, u):
                act.wait_ge(q_ab, g + 1)
                act.activation(qT[0:64, u, 0, :], bank[2][0:64, 0:SEQ], ACT.Copy)
                act.activation(qT[64:128, u, 1, :], bank[2][64:128, 0:SEQ], ACT.Copy).then_inc(q_abs, 1)

            def exps(g, u, e):
                act.wait_ge(max_ok[e], g + 1)
                for t, (lo, n) in enumerate(((0, P), (P, SEQ))):
                    ins = act.activation(Pr[:, u, e, lo:lo + n], bank[e][:, lo:lo + n], ACT.Exp, bias=nmax[:, u, t, e:e + 1],
                                         accum_out=sums[:, u, t, e:e + 1])
                ins.then_inc(exp_ok[e], 1)

            def pt_copy(g):
                act.wait_ge(pt_mm[0], g + 1)
                act.activation(PTs[:, 0, :], bank[4][:, 0:CAUSAL], ACT.Copy).then_inc(pt_ok[0], 1)

            abs_copy(0, 0)
            exps(0, 0, 0)
            exps(0, 0, 1)
            abs_copy(1, 1)

            def y_copy(b):
                act.wait_ge(y_mm, b + 1)
                act.activation(Y[:, bass.ds(2 * b, 2), :], bank[7][:, :].rearrange("p (t n) -> p t n", t=2), ACT.Copy).then_inc(y_ok, 1)

            def step(g, u, q_next=True, s_next=True, y_of=None):
                pt_copy(g)
                if s_next:
                    exps(g + 1, 1 - u, 0)
                if q_next:
                    abs_copy(g + 2, u)
                if y_of is not None:
                    y_copy(y_of)
                if s_next:
                    exps(g + 1, 1 - u, 1)

            def batch(b, first=False, last=False):
                step(8 * b, 0, y_of=None if first else b - 1)
                step(8 * b + 1, 1)
                with act.Fori(1, 3) as i:
                    for u in range(2):
                        step(8 * b + 2 * i + u, u)
                for u in range(2):
                    step(8 * b + 6 + u, u, not last, not last or u == 0)

            batch(0, first=True)
            with act.Fori(1, BATCH - 1) as b:
                batch(b)
            batch(BATCH - 1, last=True)
            y_copy(BATCH - 1)
            if phases >= 2:
                output_norms(1)
                with act.Fori(0, QN) as q:
                    act.wait_ge(nx, QN * 1 + q + 1)
                    for u in range(QT):
                        ins = scaled(1, QT * q + u, tile(INP, QT * q + u), tile(X, QT * q + u))
                    ins.then_inc(inp_ok, 1)
                    act.wait_ge(h_n, TILES * 1 + QT * q + QT)
                    act.activation(XNP[:, bass.ds(QT * q, QT), 0:D], hbuf[:, :, :], ACT.Copy).then_inc(row_ok, 1)
                    for v in range(2):
                        act.wait_ge(hT_n, 2 * QN + 2 * q + v + 1)
                        act.activation(xnT[:, :, bass.ds(QT * P * q + v * SEQ, SEQ)], hTs[:, :, v * SEQ:(v + 1) * SEQ], ACT.Copy).then_inc(xnT_ok, 1)
                    act.wait_ge(lg_mm, q + 1)
                    lg = bank[4][:, 0:QT * (E0 + 1)].rearrange("p (u n) -> p u n", u=QT)
                    act.activation(LG[:, bass.ds(QT * q, QT), :], lg[:, :, 0:E0], ACT.Copy)
                    act.activation(gate[:, bass.ds(QT * q, QT)], lg[:, :, E0], ACT.Copy).then_inc(lg_ok, 1)
                act.wait_ge(lgs_ok, 1)
                act.activation(EXPL, EXPL, ACT.Exp).then_inc(lge_ok, 1)
                act.activation(gate[:, :], gate[:, :], ACT.Exp, scale=-1.0).then_inc(lge_ok, 1)
                with act.Fori(0, 4) as c:
                    for f in range(FSC):
                        act.wait_ge(gu_mm, FSC * c + f + 1)
                        act.wait_ge(hf_ok, FSC * c + f + 1)
                        act.activation(sil[:, f % 2, :], bank[2 * (f % 2)][:, :], ACT.Silu).then_inc(sil_ok, 1)
                def xe_copy(e, u):
                    act.wait_ge(xe_tr, e + 1)
                    act.activation(XeT[:, u % 2, :, :], bank[u % 2][:, 0:D].rearrange("p (k t) -> p k t", k=KD), ACT.Copy).then_inc(xe_ok, 1)

                def gate_silu(e, u):
                    act.wait_ge(ge_mm, e + 1)
                    act.activation(gE[:, u % 2, :], bank[2 + u % 2][:, 0:FE], ACT.Silu).then_inc(se_ok, 1)

                def step(e, u, more=True):
                    if more or u < 3:
                        gate_silu(e + 1, u + 1)
                    if more or u < 2:
                        xe_copy(e + 2, u)

                xe_copy(0, 0)
                xe_copy(1, 1)
                gate_silu(0, 0)
                with act.Fori(0, E0 // 4 - 1) as i:
                    for u in range(4):
                        step(4 * i + u, u)
                for u in range(4):
                    step(E0 - 4 + u, u, False)
            if phases >= 3:
                output_norms(2)
                with act.Fori(0, QN) as q:
                    x_norms(2, q)
                    act.wait_ge(bq_ok, 1)
                    act.wait_ge(qkv_mm, q + 1)
                    for c in range(KD):
                        act.activation(qTall[:, c, bass.ds(QT * P * q, QT * P)], bank[4 + c][:, :], ACT.Identity, bias=bq[:, c:c + 1], scale=SCALE1)
                    act.activation(kTr[:, bass.ds(QT * P * q, QT * P)], bank[6][:, :], ACT.Identity, bias=bk, scale=1.0).then_inc(qk1_ok, 1)

                def exps1(g, p, e):
                    act.wait_ge(max1_ok[e], g + 1)
                    for t, (lo, n) in enumerate(((0, P), (P, SEQ))):
                        ins = act.activation(Pr[:, p % 2, e, lo:lo + n], bank[2 * (p % 2) + e][:, lo:lo + n], ACT.Exp, bias=nmax[:, p % 2, t, e:e + 1],
                                             accum_out=sumC[:, t, 2 * p + e:2 * p + e + 1])
                    ins.then_inc(exp1_ok[e], 1)

                def step(b, p, more=True, before=True):
                    g = 8 * b + p
                    if before and p == 3:
                        act.wait_ge(oT1_mm, b)
                        act.activation(oTC_sb, bank[7][:, :].rearrange("p (c t) -> p c t", c=KD), ACT.Copy).then_inc(oT1_ok, 1)
                    if more:
                        if p == 7:
                            act.wait_ge(rs1_ok, b + 1)
                        exps1(g + 1, (p + 1) % 8, 0)
                    act.wait_ge(pt1_mm[0], g + 1)
                    act.activation(PTc[p % 2][:, 0, :], bank[4][:, 0:CAUSAL], ACT.Copy).then_inc(pt1_ok[0], 1)
                    if more:
                        exps1(g + 1, (p + 1) % 8, 1)

                exps1(0, 0, 0)
                exps1(0, 0, 1)
                for p in range(8):
                    step(0, p, before=False)
                with act.Fori(1, BATCH - 1) as b:
                    for p in range(8):
                        step(b, p)
                for p in range(8):
                    step(BATCH - 1, p, more=p < 7)
                act.wait_ge(oT1_mm, BATCH)
                act.activation(oTC_sb, bank[7][:, :].rearrange("p (c t) -> p c t", c=KD), ACT.Copy).then_inc(oT1_ok, 1)
            if phases >= 4:
                output_norms(3)
                with act.Fori(0, QN) as q:
                    x_norms(3, q)
                with act.Fori(0, 4) as c:
                    for f in range(IC):
                        act.wait_ge(gu1_mm, IC * c + f + 1)
                        act.wait_ge(hf1_ok, IC * c + f + 1)
                        act.activation(sil[:, f % 2, :], bank[2 * (f % 2)][:, :], ACT.Silu).then_inc(sil1_ok, 1)
            output_norms(4)
            with act.Fori(0, QN) as q:
                act.wait_ge(xb_ok, q + 1)
                act.dma_start(out[:, bass.ds(QT * q, QT), :], X[:, bass.ds(QT * q, QT), :]).then_inc(fin_out, 16)
            act.wait_ge(fin_out, 16 * QN)

        @block.vector
        def _(dve):
            ch = Tally(dve, dch)
            dve.sem_inc(hf_ok, 2)
            dve.wait_ge(c_in, 48)
            dve.tensor_copy(cbf[:, :, :], cst[:, :, :]).then_inc(cbf_ok, 1)
            dve.tensor_copy(ident[:, :], cst[:, 0, :]).then_inc(cbf_ok, 1)
            ch.link(dve.tensor_scalar(vecs[:, KVL + 1:KVL + 2], vecs[:, KVL + 1:KVL + 2], SCALE0, None, ALU.mult))
            dve.tensor_scalar(Wq[:, :, 1:3, :].rearrange("p a k m -> p a (k m)"), Wq[:, :, 1:3, :].rearrange("p a k m -> p a (k m)"),
                              vecs[0:QL, KVL + 1:KVL + 2], None, ALU.mult).then_inc(wr_ok, 1)
            dve.sem_inc(wp_me, 2)
            dve.sem_inc(wp_ve, 2)

            def tile(buf, t):
                return buf[:, bass.ds(t, 1), :].rearrange("p a n -> p (a n)")

            def moments(k, i, q, src):
                done, n = (mvy, QN * (i - 1) + q) if k == 0 else (mvx, QN * i + q)
                if n >= 2:
                    dve.wait_ge(done, n - 1)
                st = stats[:, k, n % 2]
                for u in range(QT):
                    ch.mark(dve.bn_stats(st[:, u, :], src[:, QT * q + u, :]))
                ch.wait()
                for u in range(QT):
                    ins = dve.bn_aggr(mv[:, k, QT * q + u, :], st[:, u, :])
                ins.then_inc(done, 1)

            def output_moments(i):
                for q in range(QN):
                    moments(0, i, q, Y)

            def add_quarter(i, q):
                dve.wait_ge(lny, QN * (i - 1) + q + 1)
                quarter = bass.ds(QT * q, QT)
                ch.mark(dve.tensor_tensor(X[:, quarter, :], X[:, quarter, :], Y[:, quarter, :], ALU.add))

            def add_outputs(i):
                output_moments(i)
                for q in range(QN):
                    add_quarter(i, q)
                    ch.wait()
                    moments(1, i, q, X)

            def hT_copies(i, q, keep=None):
                for v in range(2):
                    dve.wait_ge(tr_n, TILES * i + QT * q + 2 * v + 2)
                    dst = hTs[:, :, v * SEQ:(v + 1) * SEQ] if keep is None else keep[:, :, bass.ds(QT * P * q + v * SEQ, SEQ)]
                    dve.tensor_copy(dst.rearrange("p k (u t) -> p k u t", u=2), bank[v][:, :].rearrange("p (u k t) -> p k u t", u=2, k=KD)).then_inc(hT_n, 1)

            dve.wait_ge(x_in, 32)
            for q in range(QN):
                moments(1, 0, q, X)
            with dve.Fori(0, QN) as q:
                dve.wait_ge(lat, QT * q)
                hT_copies(0, q)
            dve.wait_ge(ms_ok, 1)
            dve.tensor_reduce(ms[:, :, 0], sq_q, AX.X, ALU.add)
            dve.wait_ge(ms_ok, 2)
            dve.tensor_reduce(ms[:, :, 1], sq_kv, AX.X, ALU.add).then_inc(msr_ok, 1)
            with dve.Fori(0, PAIRS // 2) as i:
                for u in range(2):
                    dve.wait_ge(wp_m, 2 * i + u + 1)
                    dve.scalar_tensor_tensor(Wq[:, bass.ds(2 * i + u, 1), 0, :].rearrange("p a (e m) -> p (a e) m", e=2),
                                             bank[u][0:QL, 0:P].rearrange("p (e m) -> p e m", e=2), vecs[0:QL, KVL + 1:KVL + 2],
                                             vecs[0:QL, None, 0:KVL].to_broadcast([QL, 2, KVL]), ALU.mult, ALU.mult).then_inc(wp_me, 1)
            dve.wait_ge(w_in, 48)
            dve.wait_ge(rs_ok, 1)
            with dve.Fori(0, QN // 2) as i:
                ch.enter(i, 6)
                for v in range(2):
                    q = 2 * i + v
                    quarter = bass.ds(QT * q, QT)
                    dve.wait_ge(qk_tr, 2 * i)
                    lats = LATS[:, quarter, :]
                    ch.mark(dve.tensor_tensor(qn[:, v], lats[:, :, 0:QL], ms[:, quarter, 0, None].to_broadcast([P, QT, QL]), ALU.mult))
                    for t in range(2):
                        at = bass.ds(QT * q + 2 * t, 2)
                        ins = dve.tensor_tensor(kr2[:, v, 2 * t:2 * t + 2], LATS[:, at, QL + KVL:LAT].rearrange("p u (a n) -> p u a n", a=2), rope_k, ALU.mult)
                    ch.mark(ins)
                    for a in (0, 2):
                        ins = dve.tensor_tensor(kst[:, v, :, a, :], lats[:, :, QL:QL + KVL], ms[:, quarter, 1, None].to_broadcast([P, QT, KVL]), ALU.mult)
                    ch.mark(ins)
                    ch.wait()
                    dve.tensor_tensor(kst[:, v, :, 1, :], kr2[:, v, :, 0, :], kr2[:, v, :, 1, :], ALU.add).then_inc(qk_ready, 1)
            ch.leave(QN // 2)

            def rope_mul(g, u, first=False):
                dve.wait_ge(q_rr, g + 1)
                if not first:
                    dve.wait_ge(q_rope, g - 1)
                dve.tensor_tensor(rmul[:, u, :, :], bank[3][:, :].rearrange("p (k t) -> p k t", k=2), rope_q[:, :, :], ALU.mult).then_inc(rmul_ok, 1)

            def maxes(g, u, e):
                dve.wait_ge(s_mm[e], g + 1)
                for t, (lo, n) in enumerate(((0, P), (P, SEQ))):
                    ins = dve.tensor_reduce(nmax[:, u, t, e:e + 1], bank[e][:, lo:lo + n], AX.X, ALU.max, negate=True)
                ins.then_inc(max_ok[e], 1)

            def pt_copy(g):
                dve.wait_ge(pt_mm[1], g + 1)
                dve.tensor_copy(PTs[:, 1, :], bank[5][:, 0:CAUSAL]).then_inc(pt_ok[1], 1)

            def o_norm(g, u):
                dve.wait_ge(exp_ok[1], g + 1)
                ch.link(dve.reciprocal(rsum[:, :, :], sums[:, u, :, :]))
                dve.wait_ge(pv_mm, g + 1)
                dve.tensor_tensor(o_sb[:, :, :].rearrange("p t (e n) -> p (t e) n", e=2), bank[6][:, 0:SEQ].rearrange("p (c n) -> p c n", c=4),
                                  rsum[:, :, :].rearrange("p t e -> p (t e)")[:, :, None].to_broadcast([P, 4, KVL]), ALU.mult).then_inc(o_ok, 1)

            def oT_copy(g):
                dve.wait_ge(oT_mm, g + 1)
                dve.tensor_copy(oT_sb[:, :], bank[6][:, SEQ:2 * SEQ]).then_inc(oT_ok, 1)

            rope_mul(0, 0, True)
            rope_mul(1, 1, True)
            maxes(0, 0, 0)
            maxes(0, 0, 1)

            def step(g, u, q_next=True, s_next=True, first=False):
                if s_next:
                    maxes(g + 1, 1 - u, 0)
                if not first:
                    oT_copy(g - 1)
                pt_copy(g)
                if q_next:
                    rope_mul(g + 2, u)
                if s_next:
                    maxes(g + 1, 1 - u, 1)
                o_norm(g, u)

            step(0, 0, first=True)
            step(1, 1)
            with dve.Fori(1, PAIRS * BATCH // 2 - 1) as i:
                ch.enter(i - 1, 2)
                for u in range(2):
                    step(2 * i + u, u)
            ch.leave(PAIRS * BATCH // 2 - 2)
            step(PAIRS * BATCH - 2, 0, q_next=False)
            step(PAIRS * BATCH - 1, 1, q_next=False, s_next=False)
            oT_copy(PAIRS * BATCH - 1)
            dve.wait_ge(y_ok, BATCH)
            if phases >= 2:
                dve.wait_ge(b_in, 96)
                add_outputs(1)
                with dve.Fori(0, QN) as q:
                    dve.wait_ge(rms_ok, q + 1)
                    dve.wait_ge(inp_ok, q + 1)
                    dve.wait_ge(row_ok, q)
                    dve.wait_ge(tr_n, TILES * 1 + QT * q)
                    for u in range(QT):
                        t = QT * q + u
                        dve.scalar_tensor_tensor(hbuf[:, u, :], tile(INP, t), rms[:, bass.ds(t, 1)], wn_bc[:, :], ALU.mult, ALU.mult).then_inc(h_n, 1)
                    dve.wait_ge(lg_mm, q)
                    dve.wait_ge(xnT_ok, 2 * q)
                    hT_copies(1, q)
                dve.wait_ge(lg_ok, QN)
                bc = lambda v: v[:, :, None].to_broadcast([P, TILES, E0])
                ch.link(dve.tensor_reduce(rmx[:, :], LG, AX.X, ALU.max))
                dve.tensor_tensor(EXPL, LG, bc(rmx), ALU.subtract).then_inc(lgs_ok, 1)
                ch.mark(dve.memset(PP[:, :, E0:], -1.0))
                dve.wait_ge(lge_ok, 2)
                ch.link(dve.tensor_reduce(rsm[:, :], EXPL, AX.X, ALU.add))
                ch.mark(dve.reciprocal(rsm[:, :], rsm[:, :]))
                ch.link(dve.tensor_scalar(gate[:, :], gate[:, :], 1.0, None, ALU.add))
                ch.mark(dve.reciprocal(gate[:, :], gate[:, :]))
                ch.link(dve.tensor_tensor(PP[:, :, 0:E0], EXPL, bc(rsm), ALU.mult))
                dve.tensor_copy(XNP[:, :, D:], PP[:, :, 0:E0]).then_inc(probs_ok, 1)
                for t in range(TILES):
                    ch.mark(dve.max(top8[:, t, :], PP[:, t, 0:E0]))
                ch.wait()
                ch.link(dve.memset(top8[:, :, TOPK:], -1.0))
                for t in range(TILES):
                    ch.mark(dve.match_replace(RP[:, t, :], top8[:, t, :], PP[:, t, :], -2.0))
                ch.wait()
                dve.tensor_scalar(MBF[:, :, :], RP[:, :, 0:E0], -2.0, None, ALU.is_equal).then_inc(mask_ok, 1)
                ch.mark(dve.tensor_scalar(MSK, RP[:, :, 0:E0], -2.0, None, ALU.is_equal))
                dve.wait_ge(rank_mm, 1)
                rank = bank[0][:, :].rearrange("p (t e) -> p t e", t=TILES)
                ch.mark(dve.scalar_tensor_tensor(SLOT, rank, float(E0), slot_c[:, 0], ALU.mult, ALU.add))
                ch.link(dve.tensor_scalar(INV, rank, float(CAP), None, ALU.is_ge))
                ch.link(dve.copy_predicated(SLOT, INV.bitcast(U32), slot_c[:, 1]))
                ch.link(dve.tensor_tensor(SLOT, SLOT, MSK, ALU.mult))
                for t in range(TILES):
                    ch.mark(dve.max(slot8[:, t, :], SLOT[:, t, :]))
                ch.wait()
                dve.tensor_scalar(slot_i[:, :, :], slot8[:, :, 0:TOPK], -1.0, None, ALU.add).then_inc(slots_ok, 1)
                dve.wait_ge(cp_in, 64)
                dve.tensor_scalar(bq, bq, SCALE1, None, ALU.mult).then_inc(bq_ok, 1)
                p0, p1, p2, p3 = (cpw[:, :, k:k + ROWS + 1] for k in range(4))
                c0, c1, c2, c3 = (coef[:, :, k, :] for k in range(4))
                ch.mark(dve.tensor_copy(c0, p1))
                ch.link(dve.tensor_tensor(ctmp[:, :, :], p2, p0, ALU.subtract))
                ch.mark(dve.tensor_scalar(c1, ctmp[:, :, :], 0.5, None, ALU.mult))
                ch.mark(dve.scalar_tensor_tensor(c3, p2, -3.0, p3, ALU.mult, ALU.add))
                ch.link(dve.scalar_tensor_tensor(c2, p2, 4.0, p3, ALU.mult, ALU.subtract))
                ch.mark(dve.scalar_tensor_tensor(c3, p1, 3.0, c3, ALU.mult, ALU.add))
                ch.link(dve.scalar_tensor_tensor(c2, p1, -5.0, c2, ALU.mult, ALU.add))
                ch.mark(dve.tensor_tensor(c3, c3, p0, ALU.subtract))
                ch.link(dve.scalar_tensor_tensor(c2, p0, 2.0, c2, ALU.mult, ALU.add))
                ch.mark(dve.tensor_scalar(c3, c3, 0.5, None, ALU.mult))
                ch.link(dve.tensor_scalar(c2, c2, 0.5, None, ALU.mult))

                def spline_op(m, f):
                    for out_, t_, row, n in ((samp, frac, 1, SPAN), (sampb, fracb, 0, ALT)):
                        c = coef[:, bass.ds(m, 1), 3 - (f + 1) // 2, row:row + ROWS].rearrange("p a r -> p (a r)")[:, :, None].to_broadcast([P, ROWS, n])
                        if f == 0:
                            ch.mark(dve.tensor_tensor(out_, t_, c, ALU.mult))
                        elif f % 2:
                            ch.mark(dve.tensor_tensor(out_, out_, c, ALU.add))
                        else:
                            ch.mark(dve.tensor_tensor(out_, out_, t_, ALU.mult))
                    ch.wait()

                def shared(c, spline):
                    for f in range(FSC):
                        if spline:
                            spline_op(c, f)
                        dve.wait_ge(sil_ok, FSC * c + f + 1)
                        dve.tensor_tensor(hF[:, f, :], sil[:, f % 2, :], bank[2 * (f % 2) + 1][:, :], ALU.mult).then_inc(hf_ok, 1)
                    if spline:
                        dve.copy_predicated(samp[:, :, 0:ALT], before.bitcast(U32), sampb).then_inc(samp_ok, 1)
                    for t in range(4):
                        dve.wait_ge(dn_mm, 4 * c + t + 1)
                        dve.scalar_tensor_tensor(tile(INP, 4 * c + t), bank[4 + t % 2][:, 0:D], gate[:, bass.ds(4 * c + t, 1)], tile(INP, 4 * c + t),
                                                 ALU.mult, ALU.add).then_inc(dn_ok, 1)

                with dve.Fori(0, 3) as c:
                    ch.enter(c, 2 * FSC)
                    shared(c, True)
                    dve.wait_ge(spl_out, 16 * c + 16)
                ch.leave(3)
                shared(3, False)

                def hidden(e, u):
                    dve.wait_ge(se_ok, e + 1)
                    dve.tensor_tensor(hE[:, u % 2, :], gE[:, u % 2, :], bank[2 + u % 2][:, FE:2 * FE], ALU.mult).then_inc(he_ok, 1)

                def step(e, u, j, more=True):
                    if more or u < 3:
                        hidden(e + 1, u + 1)
                    dve.wait_ge(he_tr, e + 1)
                    b = bank[4 + u % 2]
                    if u < 2:
                        dve.tensor_copy((gateT, upT)[u][:, :, bass.ds(P * j, P)], b[:, D:2 * D].rearrange("p (k i) -> p k i", k=KD))
                    elif u == 2:
                        dve.tensor_copy(tile(downT, j), b[:, D:2 * D])
                    dve.tensor_copy(hET[0:FEK, u % 2, :], b[0:FEK, 0:FEC * P]).then_inc(heT_ok, 1)
                    dve.wait_ge(ye_mm, e + 1)
                    dve.wait_ge(added, e)
                    dve.tensor_scalar(yE[:, u % 2, :], bank[6 + u % 2][:, 0:D], Xe[:, u, bass.ds(D + e, 1)], None, ALU.mult).then_inc(ye_ok, 1)

                hidden(0, 0)
                with dve.Fori(0, E0 // 4 - 1) as i:
                    for u in range(4):
                        step(4 * i + u, u, i)
                for u in range(4):
                    step(E0 - 4 + u, u, E0 // 4 - 1, False)
                dve.wait_ge(back_in, 16)
            if phases >= 3:
                add_outputs(2)
                with dve.Fori(0, QN) as q:
                    dve.wait_ge(qkv_mm, q)
                    hT_copies(2, q)
                    dve.wait_ge(qkv_mm, q + 1)
                    dve.tensor_tensor(vall[:, bass.ds(QT * q, QT), :], bank[7][:, 0:QT * HD1].rearrange("p (u n) -> p u n", u=QT), bv_bc[:, None, :].to_broadcast([P, QT, HD1]),
                                      ALU.add).then_inc(v1_ok, 1)

                def maxes1(g, p, e):
                    dve.wait_ge(s1_mm[e], g + 1)
                    for t, (lo, n) in enumerate(((0, P), (P, SEQ))):
                        ins = dve.tensor_reduce(nmax[:, p % 2, t, e:e + 1], bank[2 * (p % 2) + e][:, lo:lo + n], AX.X, ALU.max, negate=True)
                    ins.then_inc(max1_ok[e], 1)

                def o_norm1(b):
                    dve.wait_ge(pv1_mm, 8 * b + 8)
                    dve.tensor_tensor(oC_sb.rearrange("p t (h n) -> p (t h) n", n=HD1), bank[6][:, :].rearrange("p (c n) -> p c n", n=HD1),
                                      rsumC[:, :, :].rearrange("p t h -> p (t h)")[:, :, None].to_broadcast([P, 2 * H1, HD1]), ALU.mult).then_inc(o1_ok, 1)

                def y_add(b):
                    dve.wait_ge(y1_mm, b + 1)
                    dve.tensor_tensor(Y[:, bass.ds(2 * b, 2), :], bank[7][:, :].rearrange("p (t n) -> p t n", t=2), bo_bc[:, None, :].to_broadcast([P, 2, D]), ALU.add)\
                        .then_inc(y1_ok, 1)

                def step(b, p, more=True, before=True):
                    g = 8 * b + p
                    if before and p == 1:
                        o_norm1(b - 1)
                    if before and p == 5:
                        y_add(b - 1)
                    if p == 7:
                        dve.wait_ge(exp1_ok[1], g + 1)
                        ch.link(dve.reciprocal(rsumC[:, :, :], sumC[:, :, :]))
                        ch.link(dve.tensor_scalar(rsumC[:, 0, :], rsumC[:, 0, :], row_valid, None, ALU.mult))
                        dve.nop().then_inc(rs1_ok, 1)
                    if more:
                        maxes1(g + 1, (p + 1) % 8, 0)
                        maxes1(g + 1, (p + 1) % 8, 1)
                    dve.wait_ge(pt1_mm[1], g + 1)
                    dve.tensor_copy(PTc[p % 2][:, 1, :], bank[5][:, 0:CAUSAL]).then_inc(pt1_ok[1], 1)

                maxes1(0, 0, 0)
                maxes1(0, 0, 1)
                for p in range(8):
                    step(0, p, before=False)
                with dve.Fori(1, BATCH - 1) as b:
                    ch.enter(b - 1, 2)
                    for p in range(8):
                        step(b, p)
                ch.leave(BATCH - 2)
                for p in range(8):
                    step(BATCH - 1, p, more=p < 7)
                o_norm1(BATCH - 1)
                y_add(BATCH - 1)
                dve.wait_ge(y1_ok, BATCH)
            if phases >= 4:
                dve.sem_inc(hf1_ok, 2)
                add_outputs(3)
                with dve.Fori(0, QN) as q:
                    hT_copies(3, q, hTall)
                with dve.Fori(0, 4) as c:
                    for f in range(IC):
                        dve.wait_ge(sil1_ok, IC * c + f + 1)
                        dve.tensor_tensor(hFD[:, f, :], sil[:, f % 2, :], bank[2 * (f % 2) + 1][:, :], ALU.mult).then_inc(hf1_ok, 1)
                    for t in range(4):
                        dve.wait_ge(dn1_mm, 4 * c + t + 1)
                        dve.tensor_copy(tile(Y, 4 * c + t), bank[4 + t % 2][:, 0:D]).then_inc(dn1_ok, 1)
                dve.wait_ge(dn1_ok, TILES)
            output_moments(4)
            with dve.Fori(0, QN) as q:
                ch.enter(q, 2)
                add_quarter(4, q)
                ch.wait()
                dve.nop().then_inc(xb_ok, 1)
                ch.mark(dve.nop())
            ch.leave(QN)

        @block.tensor
        def _(pe):
            def transposes(i, q):
                pe.wait_ge(hT_n, 2 * QN * i + 2 * q)
                for u in range(QT):
                    pe.wait_ge(h_n, TILES * i + QT * q + u + 1)
                    for k in range(KD):
                        at = (u % 2) * D + k * P
                        ins = pe.transpose(bank[u // 2][:, at:at + P], hbuf[:, u, k * P:(k + 1) * P], ident[:, :])
                    ins.then_inc(tr_n, 1)

            pe.wait_ge(cbf_ok, 2)
            with pe.Fori(0, QN) as q:
                transposes(0, q)
                pe.wait_ge(w_in, 48)
                pe.wait_ge(lat_ok, QT * q)
                for u in range(QT):
                    pe.wait_ge(hT_n, 2 * q + u // 2 + 1)
                    for k in range(KD):
                        ins = pe.matmul(bank[4 + u][:, 0:LAT], hTs[:, k, u * P:(u + 1) * P], w_lat[:, k, :], start=(k == 0), stop=(k == KD - 1))
                    ins.then_inc(lat, 1)
            with pe.Fori(0, PAIRS // 2) as i:
                for u in range(2):
                    pe.wait_ge(wp_in[u], 16 * i + 16)
                    pe.wait_ge(wp_me, 2 * i + u + 1)
                    pe.wait_ge(wp_ve, 2 * i + u + 1)
                    w = wprep[:, u, :]
                    wn, wk = w[:, 0:2 * QL], w[:, 2 * QL:2 * QL + 2 * KVL]
                    wv, wo = w[:, 2 * QL + 2 * KVL:2 * QL + 4 * KVL], w[:, 2 * QL + 4 * KVL:]
                    for e in range(2):
                        ins = pe.matmul(bank[u][0:QL, e * KVL:(e + 1) * KVL], wn[:, e * QL:(e + 1) * QL], wk[:, e * KVL:(e + 1) * KVL], start=True, stop=True)
                    ins.then_inc(wp_m, 1)
                    for e in range(2):
                        ins = pe.matmul(bank[2 + u][e * 64:e * 64 + 64, 0:D], wv[:, e * KVL:(e + 1) * KVL], wo[:, e * D:(e + 1) * D], start=True, stop=True)
                    ins.then_inc(wp_v, 1)
            pe.wait_ge(wp_me, PAIRS + 2)
            pe.wait_ge(wp_ve, PAIRS + 2)
            pe.wait_ge(lat_ok, TILES)
            with pe.Fori(0, QN // 2) as i:
                for v in range(2):
                    q = 2 * i + v
                    pe.wait_ge(kT_ok, 2 * i)
                    pe.wait_ge(qk_ready, q + 1)
                    bq_, ba, bb = latent_banks[v]
                    for u in range(QT):
                        at = slice(u * P, (u + 1) * P)
                        pe.transpose(bank[bq_][0:QL, at], qn[:, v, u, :], ident[:, :])
                        pe.transpose(bank[ba][:, at], kst[:, v, u, 0:2, :].rearrange("p a n -> p (a n)"), ident[:, :])
                        ins = pe.transpose(bank[bb][:, at], kst[:, v, u, 1:3, :].rearrange("p a n -> p (a n)"), ident[:, :])
                    ins.then_inc(qk_tr, 1)
            pe.wait_ge(kT_ok, QN)
            pe.wait_ge(ckv_ok, QN)

            def q_rope_mm(g, b, u, first=False):
                pe.wait_ge(wst_ok, g + 1)
                if not first:
                    pe.wait_ge(rmul_ok, g)
                for k in (1, 2):
                    ins = pe.matmul(bank[3][:, (k - 1) * SEQ:k * SEQ], wst[:, u, k, :], qlatT[:, bass.ds(SEQ * b, SEQ)], start=True, stop=True)
                ins.then_inc(q_rr, 1)

            def q_abs_mm(g, b, u, first=False):
                if not first:
                    pe.wait_ge(q_abs, g)
                pe.matmul(bank[2][:, 0:SEQ], wst[:, u, 0, :], qlatT[:, bass.ds(SEQ * b, SEQ)], start=True, stop=True).then_inc(q_ab, 1)

            def scores(g, b, u, e, first=False):
                pe.wait_ge(q_rope, g + 1)
                pe.wait_ge(q_abs, g + 1)
                if not first:
                    pe.wait_ge(exp_ok[e], g)
                kT = (kTa, kTb)[e]
                for lo, n in ((0, P), (P, SEQ)):
                    pe.matmul(bank[e][:, lo:lo + n], qT[:, u, e, lo:lo + P], kT[:, bass.ds(SEQ * b, n)], start=True, stop=False)
                    ins = pe.matmul(bank[e][:, lo + n - P:lo + n], ident_bf, causal_bf, start=False, stop=True)
                ins.then_inc(s_mm[e], 1)

            def pt(g, u, e):
                pe.wait_ge(exp_ok[e], g + 1)
                for c in range(3):
                    ins = pe.transpose(bank[4 + e][:, c * P:(c + 1) * P], Pr[:, u, e, c * P:(c + 1) * P], ident[:, :])
                ins.then_inc(pt_mm[e], 1)

            def pv(g, b):
                for e in range(2):
                    pe.wait_ge(pt_ok[e], g + 1)
                    o0 = bank[6][:, e * KVL:(e + 1) * KVL]
                    o1 = bank[6][:, P + e * KVL:P + (e + 1) * KVL]
                    v0 = ckv[:, bass.ds(2 * b, 1), :].rearrange("p a n -> p (a n)")
                    v1 = ckv[:, bass.ds(2 * b + 1, 1), :].rearrange("p a n -> p (a n)")
                    pe.matmul(o0, PTs[:, e, 0:P], v0, start=True, stop=True)
                    pe.matmul(o1, PTs[:, e, P:2 * P], v0, start=True, stop=False)
                    ins = pe.matmul(o1, PTs[:, e, 2 * P:3 * P], v1, start=False, stop=True)
                ins.then_inc(pv_mm, 1)

            def oT(g):
                pe.wait_ge(o_ok, g + 1)
                for t in range(2):
                    ins = pe.transpose(bank[6][:, SEQ + t * P:SEQ + (t + 1) * P], o_sb[:, t, :], ident[:, :])
                ins.then_inc(oT_mm, 1)

            def proj(g, pair, done=False):
                pe.wait_ge(oT_ok, g + 1)
                for t in range(2):
                    ins = pe.matmul(bank[7][:, t * D:(t + 1) * D], oT_sb[:, t * P:(t + 1) * P], Wvo[:, bass.ds(pair, 1), :].rearrange("p a n -> p (a n)"),
                                    start=False, stop=done, skip_group_check=True)
                if done:
                    ins.then_inc(y_mm, 1)

            pe.wait_ge(z_ok, 1)
            for g in range(2):
                q_rope_mm(g, 0, g, g == 0)
                q_abs_mm(g, 0, g, g == 0)
            scores(0, 0, 0, 0, True)
            scores(0, 0, 0, 1, True)

            def start_sum(b):
                pe.wait_ge(y_ok, b)
                pe.matmul(bank[7][:, :], zbf[:, 0:P], zbf[:, :], start=True, stop=False, skip_group_check=True)

            def step(b, pair, u, at=None, last=False, first=False):
                g = 8 * b + pair
                nb = b + 1 if at == 7 else b
                nq = b + 1 if at in (6, 7) else b
                s_next, q_next = not (last and at == 7), not (last and at in (6, 7))
                if s_next:
                    scores(g + 1, nb, 1 - u, 0)
                if not first:
                    oT(g - 1)
                pt(g, u, 0)
                pt(g, u, 1)
                if q_next:
                    q_rope_mm(g + 2, nq, u)
                    q_abs_mm(g + 2, nq, u)
                if at == 0:
                    if not first:
                        proj(g - 1, PAIRS - 1, done=True)
                else:
                    if at == 1:
                        start_sum(b)
                    proj(g - 1, pair - 1)
                if s_next:
                    scores(g + 1, nb, 1 - u, 1)
                pv(g, b)

            def batch(b, first=False, last=False):
                step(b, 0, 0, 0, first=first)
                step(b, 1, 1, 1)
                with pe.Fori(1, 3) as i:
                    for u in range(2):
                        step(b, 2 * i + u, u)
                step(b, 6, 0, 6, last=last)
                step(b, 7, 1, 7, last=last)

            batch(0, first=True)
            with pe.Fori(1, BATCH - 1) as b:
                batch(b)
            batch(BATCH - 1, last=True)
            oT(PAIRS * BATCH - 1)
            proj(PAIRS * BATCH - 1, PAIRS - 1, done=True)
            if phases >= 2:
                pe.wait_ge(b_in, 96)
                with pe.Fori(0, QN) as q:
                    transposes(1, q)
                    pe.wait_ge(lg_ok, q)
                    for u in range(QT):
                        pe.wait_ge(hT_n, 2 * QN + 2 * q + u // 2 + 1)
                        for k in range(KD):
                            ins = pe.matmul(bank[4][:, u * (E0 + 1):(u + 1) * (E0 + 1)], hTs[:, k, u * P:(u + 1) * P], w_rt[:, k, :], start=(k == 0), stop=(k == KD - 1))
                    ins.then_inc(lg_mm, 1)
                pe.wait_ge(mask_ok, 1)
                rank = bank[0]
                pe.matmul(rank[:, :], upper_bf, MBF[:, :, :].rearrange("p t e -> p (t e)"), start=True, stop=False)
                for t in range(TILES - 1):
                    n = TILES - 1 - t
                    ins = pe.matmul(rank[:, (t + 1) * E0:].rearrange("p (a e) -> p a e", a=n), ones_bf, MBF[:, t, None, :].to_broadcast([P, n, E0]),
                                    start=False, stop=(t == TILES - 2))
                ins.then_inc(rank_mm, 1)
                pe.wait_ge(slots_ok, 1)
                with pe.Fori(0, 4) as c:
                    for f in range(FSC):
                        pe.wait_ge(hf_ok, FSC * c + f + 1)
                        for j in range(2):
                            for k in range(KD):
                                ins = pe.matmul(bank[2 * (f % 2) + j][:, :], sw_gu[:, k, j * FSP + f * P:j * FSP + (f + 1) * P], xnT[:, k, bass.ds(512 * c, 512)],
                                                start=(k == 0), stop=(k == KD - 1))
                        ins.then_inc(gu_mm, 1)
                    pe.wait_ge(hf_ok, FSC * c + FSC + 2)
                    for t in range(4):
                        if t >= 2:
                            pe.wait_ge(dn_ok, 4 * c + t - 1)
                        for f in range(FSC):
                            ins = pe.matmul(bank[4 + t % 2][:, 0:D], hF[:, f, t * P:(t + 1) * P], sw_d[:, f, :], start=(f == 0), stop=(f == FSC - 1))
                        ins.then_inc(dn_mm, 1)
                    pe.wait_ge(dn_ok, 4 * c + 4)
                def rows_T(e, u, first=False):
                    pe.wait_ge(xe_in[u % 4], placed(e, u))
                    if not first:
                        pe.wait_ge(xe_ok, e - 1)
                    for k in range(KD):
                        ins = pe.transpose(bank[u % 2][:, k * P:(k + 1) * P], Xe[:, u % 4, k * P:(k + 1) * P], ident[:, :])
                    ins.then_inc(xe_tr, 1)

                def gate_up(e, u, first=False):
                    wg = wexp[:, u % 4, 0:2 * KD * FE].rearrange("p (k n) -> p k n", k=KD)
                    pe.wait_ge(xe_ok, e + 1)
                    pe.wait_ge(we_in[u % 4], placed(e, u))
                    if not first:
                        pe.wait_ge(he_ok, e - 1)
                    for k in range(KD):
                        ins = pe.matmul(bank[2 + u % 2][:, 0:2 * FE], XeT[:, u % 2, k, :], wg[:, k, :], start=(k == 0), stop=(k == KD - 1))
                    ins.then_inc(ge_mm, 1)

                def placed(e, u):
                    return 4 * (e - u % 4) + 16

                def step(e, u, j, more=True):
                    if more or u < 3:
                        gate_up(e + 1, u + 1)
                    pe.wait_ge(he_ok, e + 1)
                    for f in range(FEC):
                        ins = pe.transpose(bank[4 + u % 2][0:FEK, f * P:(f + 1) * P], hE[:, u % 2, f * FEK:(f + 1) * FEK], ident[:, :])
                    if u < 3:
                        if u == 0:
                            pe.wait_ge(nat_in, 48 * j + 48)
                        for k in range(KD):
                            ins = pe.transpose(bank[4 + u % 2][:, D + k * P:D + (k + 1) * P], wnat[:, u, k * P:(k + 1) * P], ident[:, :])
                    ins.then_inc(he_tr, 1)
                    if more or u < 2:
                        rows_T(e + 2, u + 2)
                    wd = wexp[:, u, 2 * KD * FE:].rearrange("p (f n) -> p f n", f=FEC)
                    pe.wait_ge(heT_ok, e + 1)
                    for f in range(FEC):
                        ins = pe.matmul(bank[6 + u % 2][:, 0:D], hET[0:FEK, u % 2, f * P:(f + 1) * P], wd[0:FEK, f, :], start=(f == 0), stop=(f == FEC - 1))
                    ins.then_inc(ye_mm, 1)

                rows_T(0, 0, True)
                rows_T(1, 1, True)
                gate_up(0, 0, True)
                with pe.Fori(0, E0 // 4 - 1) as i:
                    for u in range(4):
                        step(4 * i + u, u, i)
                for u in range(4):
                    step(E0 - 4 + u, u, E0 // 4 - 1, False)
            if phases >= 3:
                pe.wait_ge(cp_in, 64)
                with pe.Fori(0, QN) as q:
                    transposes(2, q)
                    pe.wait_ge(hT_n, 4 * QN + 2 * q + 2)
                    pe.wait_ge(qk1_ok, q)
                    pe.wait_ge(v1_ok, q)
                    for c in range(KD):
                        for k in range(KD):
                            pe.matmul(bank[4 + c][:, :], WqT[:, k, c * P:(c + 1) * P], hTs[:, k, :], start=(k == 0), stop=(k == KD - 1))
                    for k in range(KD):
                        pe.matmul(bank[6][:, :], WkT[:, k, :], hTs[:, k, :], start=(k == 0), stop=(k == KD - 1))
                    for u in range(QT):
                        for k in range(KD):
                            ins = pe.matmul(bank[7][:, u * HD1:(u + 1) * HD1], hTs[:, k, u * P:(u + 1) * P], WvT[:, k, :], start=(k == 0), stop=(k == KD - 1))
                    ins.then_inc(qkv_mm, 1)
                pe.wait_ge(qk1_ok, QN)
                pe.wait_ge(v1_ok, QN)

                def scores1(g, b, p, e, first=False):
                    if e == 0 and p % 4 == 0:
                        pe.wait_ge(kbd_ok, b + 1)
                        pe.wait_ge(qst_ok, 2 * b + p // 4 + 1)
                    if not first:
                        pe.wait_ge(exp1_ok[e], g - 1)
                    sc = bank[2 * (p % 2) + e]
                    for lo, n in ((0, P), (P, SEQ)):
                        pe.matmul(sc[:, lo:lo + n], qst[:, p // 4, lo:lo + P], Kbd[:, bass.ds(b % 2, 1), 2 * (p % 4) + e, 0:n].rearrange("p a s -> p (a s)"), start=True, stop=False)
                        ins = pe.matmul(sc[:, lo + n - P:lo + n], ident_bf, strict_bf, start=False, stop=True)
                    ins.then_inc(s1_mm[e], 1)

                def pt1(g, p, e):
                    pe.wait_ge(exp1_ok[e], g + 1)
                    pe.wait_ge(pt1_ok[e], g)
                    for c in range(3):
                        ins = pe.transpose(bank[4 + e][:, c * P:(c + 1) * P], Pr[:, p % 2, e, c * P:(c + 1) * P], ident[:, :])
                    ins.then_inc(pt1_mm[e], 1)

                def pv1(g, b, p):
                    v0, v1 = (vall[:, bass.ds(2 * b + t, 1), :].rearrange("p a n -> p (a n)") for t in range(2))
                    for e in range(2):
                        pe.wait_ge(pt1_ok[e], g + 1)
                        at = (2 * p + e) * HD1
                        o0, o1 = bank[6][:, at:at + HD1], bank[6][:, D + at:D + at + HD1]
                        PT = PTc[p % 2][:, e, :]
                        pe.matmul(o0, PT[:, 0:P], v0, start=True, stop=True)
                        pe.matmul(o1, PT[:, P:2 * P], v0, start=True, stop=False)
                        ins = pe.matmul(o1, PT[:, 2 * P:3 * P], v1, start=False, stop=True)
                    ins.then_inc(pv1_mm, 1)

                def outputs_T(b):
                    pe.wait_ge(o1_ok, b + 1)
                    pe.wait_ge(y1_ok, b)
                    for c in range(KD):
                        for t in range(2):
                            ins = pe.transpose(bank[7][:, c * SEQ + t * P:c * SEQ + (t + 1) * P], oC_sb[:, t, c * P:(c + 1) * P], ident[:, :])
                    ins.then_inc(oT1_mm, 1)

                def proj1(b):
                    pe.wait_ge(oT1_ok, b + 1)
                    for t in range(2):
                        for c in range(KD):
                            ins = pe.matmul(bank[7][:, t * D:(t + 1) * D], oTC_sb[:, c, t * P:(t + 1) * P], WoT[:, c, :], start=(c == 0), stop=(c == KD - 1))
                    ins.then_inc(y1_mm, 1)

                def step(b, p, more=True, before=True):
                    g = 8 * b + p
                    if more:
                        for e in range(2):
                            scores1(g + 1, b + 1 if p == 7 else b, (p + 1) % 8, e)
                    for e in range(2):
                        pt1(g, p, e)
                    if before and p == 2:
                        outputs_T(b - 1)
                    if before and p == 4:
                        proj1(b - 1)
                    if before and p == 0:
                        pv1(g - 1, b - 1, 7)
                    elif p > 0:
                        if before and p == 1:
                            pe.wait_ge(o1_ok, b)
                        pv1(g - 1, b, p - 1)

                scores1(0, 0, 0, 0, True)
                scores1(0, 0, 0, 1, True)
                for p in range(8):
                    step(0, p, before=False)
                with pe.Fori(1, BATCH - 1) as b:
                    for p in range(8):
                        step(b, p)
                for p in range(8):
                    step(BATCH - 1, p, more=p < 7)
                pv1(8 * BATCH - 1, BATCH - 1, 7)
                outputs_T(BATCH - 1)
                proj1(BATCH - 1)
            if phases >= 4:
                with pe.Fori(0, QN) as q:
                    transposes(3, q)
                pe.wait_ge(hT_n, 6 * QN + 2 * QN)
                with pe.Fori(0, 4) as c:
                    for f in range(IC):
                        pe.wait_ge(hf1_ok, IC * c + f + 1)
                        for j, wT in enumerate((gateT, upT)):
                            for k in range(KD):
                                ins = pe.matmul(bank[2 * (f % 2) + j][:, :], wT[:, k, f * P:(f + 1) * P], hTall[:, k, bass.ds(512 * c, 512)], start=(k == 0), stop=(k == KD - 1))
                        ins.then_inc(gu1_mm, 1)
                    pe.wait_ge(hf1_ok, IC * c + IC + 2)
                    for t in range(4):
                        if t >= 2:
                            pe.wait_ge(dn1_ok, 4 * c + t - 1)
                        for f in range(IC):
                            ins = pe.matmul(bank[4 + t % 2][:, 0:D], hFD[:, f, t * P:(t + 1) * P], downT[:, f, :], start=(f == 0), stop=(f == IC - 1))
                        ins.then_inc(dn1_mm, 1)
                    pe.wait_ge(dn1_ok, 4 * c + 4)


def layouts(inputs):
    a = {k: np.ascontiguousarray(v) for k, v in inputs.items()}
    f = np.float32
    d = {}
    d["x"] = a["L0_attn_x"].reshape(TILES, P, D).transpose(1, 0, 2)
    r = np.arange(P)
    tri = r[:, None] - r[None, :]
    d["cst"] = np.stack([np.eye(P), np.where(tri >= 0, 0.0, NEG), np.where(tri > 0, 0.0, NEG), np.where(tri < 0, 1.0, 0.0), np.ones((P, P))], 1).astype(f)
    inv = (1.0 / np.float32(10000.0) ** (np.arange(0, ROPE, 2, dtype=f) / f(ROPE))).astype(f)
    ang = np.outer(np.arange(SEQ, dtype=f), inv).astype(f)
    ang = np.concatenate([ang, ang], -1)
    cos, sin = np.cos(ang).astype(f), np.sin(ang).astype(f)
    sin = sin * np.where(np.arange(ROPE) % 2 == 0, -1, 1).astype(f)
    d["rope_q"] = np.stack([np.tile(cos.T, (2, 1)), np.tile(sin.T, (2, 1))], 1)
    d["rope_k"] = np.stack([cos, sin], 1).reshape(KD, P, 2, ROPE).transpose(1, 0, 2, 3)
    swap = np.arange(ROPE) ^ 1
    kva = a["L0_attn_w_kva"]
    d["w_lat"] = np.concatenate([a["L0_attn_w_qa"], kva, kva[:, KVL:][:, swap]], 1).reshape(KD, P, LAT).transpose(1, 0, 2)
    vecs = np.zeros((P, KVL + 2), f)
    vecs[:, 0:KVL] = a["L0_attn_kv_a_norm_w"][None]
    vecs[:, KVL] = np.tile(a["L0_attn_kv_a_norm_w"], 2)
    vecs[:QL, KVL + 1] = a["L0_attn_q_a_norm_w"]
    d["vecs"] = vecs
    wqb = a["L0_attn_w_qb"].reshape(QL, PAIRS, 2, NOPE + ROPE)
    rp = wqb[:, :, ::-1, NOPE:]
    d["w_rope"] = np.stack([rp, rp[..., swap]], 2).reshape(QL, PAIRS, 2, P)
    wkvb = a["L0_attn_w_kvb"].reshape(KVL, PAIRS, 2, NOPE + DV)
    wo = a["L0_attn_w_o"].reshape(PAIRS, 2, DV, D)
    d["wprep"] = np.concatenate([
        wqb[..., :NOPE].transpose(1, 3, 2, 0).reshape(PAIRS, P, 2 * QL),
        wkvb[..., :NOPE].transpose(1, 3, 2, 0).reshape(PAIRS, P, 2 * KVL),
        wkvb[..., NOPE:].transpose(1, 3, 2, 0).reshape(PAIRS, P, 2 * KVL),
        wo.transpose(0, 2, 1, 3).reshape(PAIRS, P, 2 * D)], 2)
    d["w_rt"] = np.concatenate([a["L0_ffn_w_router"], a["L0_ffn_w_shared_gate"]], 1).reshape(KD, P, E0 + 1).transpose(1, 0, 2)
    d["wn_bc"] = np.tile(a["L0_ffn_w_norm"][None], (P, 1))
    swg = np.zeros((D, 2, FSP), f)
    swg[:, 0, :FS], swg[:, 1, :FS] = a["L0_ffn_sw_gate"], a["L0_ffn_sw_up"]
    d["sw_gu"] = swg.reshape(KD, P, 2 * FSP).transpose(1, 0, 2)
    swd = np.zeros((FSC * P, D), f)
    swd[:FS] = a["L0_ffn_sw_down"]
    d["sw_d"] = swd.reshape(FSC, P, D).transpose(1, 0, 2)
    t, e, p = np.arange(TILES), np.arange(E0), np.arange(P)
    spare = SLOTS + (t[None, :, None] * E0 + e[None, None, :]) * P + p[:, None, None]
    d["slot_c"] = np.stack([np.broadcast_to(e[None, None] + 1, spare.shape), spare + 1], 1).astype(f)
    d["tok_i"] = (t[None, :] * P + p[:, None]).astype(np.int32)
    d["spare"] = np.tile((TOK + p)[:, None], (1, E0)).astype(np.int32)
    gu = np.stack([a["L0_ffn_w_gate"], a["L0_ffn_w_up"]], 1).reshape(E0, 2, KD, P, FE).transpose(0, 3, 2, 1, 4).reshape(E0, P, 2 * KD * FE)
    dn = np.zeros((E0, P, FEC, D), f)
    dn[:, :FEK] = a["L0_ffn_w_down"].reshape(E0, FEC, FEK, D).transpose(0, 2, 1, 3)
    d["wexp"] = np.concatenate([gu, dn.reshape(E0, P, FEC * D)], 2)
    n = np.arange(P * ROWS * SPAN).reshape(P * ROWS, SPAN)
    pos = np.linspace(0.0, NCTRL - 1.0, INTER * D, dtype=np.float64)
    pos = np.concatenate([pos, np.full(n.size - pos.size, pos[-1])])[n]
    cell = np.clip(np.floor(pos).astype(np.int64), 0, NCTRL - 2)
    row = np.arange(P * ROWS)[:, None]
    real = n < INTER * D
    assert np.all((cell == row) | (cell == row - 1) | ~real) and np.all((cell == row)[:, ALT:] | ~real[:, ALT:])
    own = np.where(cell == row, pos - row, 0.0).astype(f)
    was = np.where((cell == row - 1) & real, pos - (row - 1), 0.0).astype(f)[:, :ALT]
    d["frac"] = own.reshape(P, ROWS, SPAN)
    d["fracb"] = np.stack([was.reshape(P, ROWS, ALT), ((cell == row - 1) & real)[:, :ALT].astype(f).reshape(P, ROWS, ALT)], 1)
    at = np.clip(ROWS * p[:, None] - 2 + np.arange(ROWS + 4)[None], 0, NCTRL - 1)
    d["cpw"] = np.stack([a[k][at] for k in ("L1_ffn_gate_cp", "L1_ffn_up_cp", "L1_ffn_down_cp")], 1)
    split = lambda w: w.T.reshape(KD, P, -1).transpose(1, 0, 2).reshape(P, -1)
    bc = lambda v: np.tile(v[None], (P, 1))
    d["wC"] = np.concatenate([
        split(a["L1_attn_Wq"]), split(a["L1_attn_Wo"]), split(np.tile(a["L1_attn_Wk"], (8, 1))), split(a["L1_attn_Wv"]), bc(a["L1_attn_bo"]), bc(a["L1_attn_bv"]),
        a["L1_attn_bq"].reshape(KD, P).T, np.tile(a["L1_attn_bk"], 8)[:, None], (p[:, None] > 0).astype(f), (p[:, None] // HD1 == np.arange(8)[None]).astype(f)], 1)
    return {k: np.ascontiguousarray(v) for k, v in d.items()}


def kernel(**inputs):
    import concourse.bacc as bacc
    from concourse.bass_utils import run_bass_kernel_spmd

    nc = bacc.Bacc("TRN2", target_bir_lowering=False, num_devices=1)
    arrays = layouts(inputs)
    T = {k: nc.dram_tensor(f"in_{k}", v.shape, mybir.dt.from_np(v.dtype), kind="ExternalInput").ap() for k, v in arrays.items()}
    out = nc.dram_tensor("out_x", (P, TILES, D), F32, kind="ExternalOutput").ap()
    build_program(nc, T, out, 4)
    r = run_bass_kernel_spmd(nc, [{f"in_{k}": v for k, v in arrays.items()}], core_ids=[0])
    return r.results[0]["out_x"].transpose(1, 0, 2).reshape(BATCH, SEQ, D)
```

```python
from contextlib import ExitStack

import numpy as np
import concourse.bass as bass
from concourse import mybir

F32 = mybir.dt.float32
F32R = mybir.dt.float32r
BF16 = mybir.dt.bfloat16
I32 = mybir.dt.int32
U32 = mybir.dt.uint32
ALU = mybir.AluOpType
ACT = mybir.ActivationFunctionType
AX = mybir.AxisListType

P = 128
BATCH, SEQ, D = 8, 256, 256
TOK = BATCH * SEQ
TILES = TOK // P
QT = 4
QN = TILES // QT
KD = D // P
LN_EPS = 1e-5
RMS_EPS = 1e-6
NEG = -1e30

PAIRS = 16 // 2
QL, KVL = 96, 64
NOPE, ROPE, DV = 128, 64, 128
SCALE0 = 1.0 / float(np.sqrt(NOPE + ROPE))
LAT = QL + KVL + 2 * ROPE
CAUSAL = P + SEQ

E0, TOPK, FE, FS, CAP = 32, 4, 176, 704, 128
FEC, FEK = 2, FE // 2
FSC = -(-FS // P)
FSP = FSC * P
ROW = D + E0
SLOTS = E0 * CAP
TABLE = SLOTS + TILES * E0 * P
WEXP = 2 * KD * FE + FEC * D
PREP = 2 * QL + 4 * KVL + 2 * D

H1, HD1 = 16, 16
SCALE1 = 1.0 / float(np.sqrt(HD1))
WC = 1596
IC = 8

INTER = 1024
NCTRL = 2033
SPAN = 129
ROWS = 16
ALT = 16
SPLINE = P * ROWS * SPAN


class Tally:

    def __init__(self, eng, sem):
        self.eng, self.sem, self.base, self.k, self.outer = eng, sem, 0, 0, []

    def mark(self, ins):
        ins.then_inc(self.sem, 1)
        self.k += 1

    def wait(self):
        self.eng.wait_ge(self.sem, self.base + self.k)

    def link(self, ins):
        self.mark(ins)
        self.wait()

    def enter(self, i, per):
        self.outer.append((self.base, self.k, per))
        self.base, self.k = self.base + self.k + i * per, 0

    def leave(self, n):
        base, k, per = self.outer.pop()
        assert self.k == per, (self.k, per)
        self.base, self.k = base, k + n * per


def build_program(nc, T, out):
    ctx = ExitStack()
    with ctx:
        def sb(name, shape, dt=F32):
            return ctx.enter_context(nc.sbuf_tensor(name, list(shape), dt))

        def sem(name):
            return ctx.enter_context(nc.semaphore(name))

        ident = sb("ident", [P, P])
        cst = sb("cst", [P, 5, P])
        cbf = sb("cbf", [P, 5, P], BF16)
        zbf = sb("zbf", [P, 512], BF16)
        ident_bf, causal_bf, strict_bf, upper_bf, ones_bf = (cbf[:, i, :] for i in range(5))
        mhalf = sb("mhalf", [P, 4])
        vecs = sb("vecs", [P, KVL + 2])
        SP_N, AL_N = ROWS * SPAN, ROWS * ALT
        X = sb("X", [P, TILES, D])
        oF = 2 * KD * FSP + FSC * D
        sizes = (("R0", KD * TOK), ("R2", TILES * ROW), ("R3", PAIRS * (3 * P + D)), ("R4", 3 * KD * INTER), ("R5", 2 * PREP), ("R7", oF + FSC * 512), ("R8", KD * QT * P))
        with ExitStack() as first:
            R0, R2, R3, R4, R5, R7, R8 = (first.enter_context(nc.sbuf_tensor(n, [P, size], F32)) for n, size in sizes)
        S0, S2, S3, S4, S5, S7, S8 = (sb(f"S{n[1:]}", [P, size], F32R) for n, size in sizes)
        R1 = sb("R1", [P, TILES * D])
        Y = R1[:, :].rearrange("p (t n) -> p t n", t=TILES)
        stats = sb("stats", [P, 2, 2, QT, 6])
        mv = sb("mv", [P, 2, TILES, 2])
        norm = sb("norm", [P, 2, TILES, 2])
        rms = sb("rms", [P, TILES])
        sil = sb("sil", [P, 2, 512])
        R6 = sb("R6", [P, 2176])
        rope_q = R6[:, 0:512].rearrange("p (a t) -> p a t", a=2)
        rope_k = R6[:, 512:768].rearrange("p (t a n) -> p t a n", t=KD, a=2)
        w_lat = R6[:, 768:1344].rearrange("p (k n) -> p k n", k=KD)
        Wq = R3[0:QL, 0:PAIRS * 3 * P].rearrange("p (a k m) -> p a k m", a=PAIRS, k=3)
        Wvo = R3[:, PAIRS * 3 * P:].rearrange("p (a n) -> p a n", a=PAIRS)
        wprep = R7[:, 0:PAIRS * PREP].rearrange("p (a n) -> p a n", a=PAIRS)
        ms = sb("ms", [P, TILES, 2])
        LATS = R4[:, 0:TILES * LAT].rearrange("p (t n) -> p t n", t=TILES)
        H = R1[:, :].rearrange("p (t n) -> p t n", t=TILES)
        sq_q = R1[:, 0:TILES * QL].rearrange("p (t n) -> p t n", t=TILES)
        sq_kv = R1[:, TILES * QL:TILES * (QL + KVL)].rearrange("p (t n) -> p t n", t=TILES)
        qn = R1[:, 0:2 * QT * QL].rearrange("p (v u n) -> p v u n", v=2, u=QT)
        oK = 2 * QT * QL
        kst = R1[:, oK:oK + 2 * QT * 3 * KVL].rearrange("p (v u a n) -> p v u a n", v=2, u=QT, a=3)
        oK2 = oK + 2 * QT * 3 * KVL
        kr2 = R1[:, oK2:oK2 + 2 * QT * 2 * ROPE].rearrange("p (v u a n) -> p v u a n", v=2, u=QT, a=2)
        kTa = R0[:, 0:TOK]
        kTb = R0[:, TOK:2 * TOK]
        qlatT = [S2[0:QL, 0:TOK], S7[0:QL, 2 * PAIRS * D:2 * PAIRS * D + TOK]]
        ckv = R2[:, TOK:TOK + TILES * KVL].rearrange("p (t n) -> p t n", t=TILES)
        oW = 2 * SP_N + 3 * AL_N
        wst = [sb("wst", [QL, 2, 3, P], F32R), S4[0:QL, oW:oW + 2 * 3 * P].rearrange("p (u k m) -> p u k m", u=2, k=3)]
        rmul = sb("rmul", [P, 2, 2, SEQ])
        qT = sb("qT", [P, 2, 2, SEQ])
        hTs = [w.rearrange("p (k t) -> p k t", k=KD) for w in (rmul[:, :, :, :].rearrange("p a b n -> p (a b n)"), R8[:, :])]
        nmax = sb("nmax", [P, 2, 2, 2])
        Pr = sb("Pr", [P, 2, 2, CAUSAL])
        sums = sb("sums", [P, 2, 2, 2])
        rsum = sb("rsum", [P, 2, 2])
        PTs = sb("PTs", [P, 2, CAUSAL])
        o_sb = sb("o_sb", [P, 2, P])
        Wvo2 = [S7[:, i * PAIRS * D:(i + 1) * PAIRS * D].rearrange("p (a n) -> p a n", a=PAIRS) for i in range(2)]
        oT2 = [S8[:, i * SEQ:(i + 1) * SEQ] for i in range(2)]
        w_rt = sb("w_rt", [P, KD, E0 + 1])
        wn_bc = sb("wn_bc", [P, D])
        sw_gu = R7[:, 0:2 * KD * FSP].rearrange("p (k n) -> p k n", k=KD)
        sw_d = R7[:, 2 * KD * FSP:oF].rearrange("p (f n) -> p f n", f=FSC)
        INP = Y
        xnT = R0[:, :].rearrange("p (k t) -> p k t", k=KD)
        XNP = R2[:, :].rearrange("p (t n) -> p t n", t=TILES)
        ROUTE = TILES * E0
        rt = R3[:, 0:6 * ROUTE].rearrange("p (a t e) -> p a t e", a=6, t=TILES)
        LG, EXPL, MSK, SLOT, INV = rt[:, 0], rt[:, 1], rt[:, 2], rt[:, 3], rt[:, 4]
        slot_c = sb("slot_c", [P, 2, TILES, E0])
        o5 = 6 * ROUTE
        PP = R3[:, o5:o5 + TILES * 40].rearrange("p (t e) -> p t e", t=TILES)
        RP = R3[:, o5 + TILES * 40:o5 + TILES * 80].rearrange("p (t e) -> p t e", t=TILES)
        MBF = sb("MBF", [P, TILES, E0], BF16)
        top8 = sb("top8", [P, TILES, 8])
        slot8 = sb("slot8", [P, TILES, 8])
        slot_i = sb("slot_i", [P, TILES, 4], I32)
        tok_i = sb("tok_i", [P, TILES], I32)
        slot_st = sb("slot_st", [P, 2, 4], I32)
        tok_st = sb("tok_st", [P, 2], I32)
        table_sb = sb("table_sb", [P, E0], I32)
        idx_st = sb("idx_st", [P, 4], I32)
        add_idx = sb("add_idx", [P, 2], I32)
        rmx = sb("rmx", [P, TILES])
        rsm = sb("rsm", [P, TILES])
        gate = sb("gate", [P, TILES])
        zer = sb("zer", [P, ROW])
        hF = R7[:, oF:].rearrange("p (f t) -> p f t", f=FSC)
        wexp = R3[:, 0:4 * WEXP].rearrange("p (u n) -> p u n", u=4)
        Xe = Pr[:, :, :, :].rearrange("p a b n -> p (a b n)")[:, 0:4 * ROW].rearrange("p (u n) -> p u n", u=4)
        XeT = rmul[:, 0, :, :].rearrange("p k (u t) -> p u k t", u=2)
        gE = sil[:, :, 0:FE]
        hE = sil[:, :, FE:2 * FE]
        hET = qT[:, 0, :, :]
        yE = qT[:, 1, :, :]
        cpw = sb("cpw", [P, 3, ROWS + 4])
        coef = sb("coef", [P, 3, 4, ROWS + 1])
        ctmp = sb("ctmp", [P, 3, ROWS + 1])
        frac = R4[:, 0:SP_N].rearrange("p (r n) -> p r n", r=ROWS)
        samp = R4[:, SP_N:2 * SP_N].rearrange("p (r n) -> p r n", r=ROWS)
        fracb = R4[:, 2 * SP_N:2 * SP_N + AL_N].rearrange("p (r n) -> p r n", r=ROWS)
        before = R4[:, 2 * SP_N + AL_N:2 * SP_N + 2 * AL_N].rearrange("p (r n) -> p r n", r=ROWS)
        sampb = R4[:, 2 * SP_N + 2 * AL_N:2 * SP_N + 3 * AL_N].rearrange("p (r n) -> p r n", r=ROWS)
        wC = R6[:, 0:WC]
        WqT = wC[:, 0:512].rearrange("p (k n) -> p k n", k=KD)
        WoT = wC[:, 512:1024].rearrange("p (k n) -> p k n", k=KD)
        WkT = wC[:, 1024:1280].rearrange("p (k n) -> p k n", k=KD)
        WvT = wC[:, 1280:1312].rearrange("p (k n) -> p k n", k=KD)
        bo_bc = wC[:, 1312:1568]
        bv_bc = wC[:, 1568:1584]
        bq, bk, row_valid = wC[:, 1584:1586], wC[:, 1586:1587], wC[:, 1587:1588]
        head_row = wC[:, 1588:1596]
        qTall = R0[:, :].rearrange("p (c t) -> p c t", c=KD)
        Kbd = R2[:, 0:2 * 8 * SEQ].rearrange("p (u j s) -> p u j s", u=2, j=8)
        kTr = R3[:, 0:TOK]
        vall = R3[:, TOK:TOK + TILES * HD1].rearrange("p (t n) -> p t n", t=TILES)
        oC = TOK + TILES * HD1
        qst = R3[:, oC:oC + 512].rearrange("p (c t) -> p c t", c=KD)
        oC_sb = R3[:, oC + 512:oC + 1024].rearrange("p (t n) -> p t n", t=2)
        oTC_sb = R3[:, oC + 1024:oC + 1536].rearrange("p (c t) -> p c t", c=KD)
        PTc = (PTs, R5[:, 0:2 * CAUSAL].rearrange("p (e n) -> p e n", e=2))
        sumC = sb("sumC", [P, 2, H1])
        rsumC = sb("rsumC", [P, 2, H1])
        def spline_weights(region):
            n, w = KD * INTER, region
            return [w[:, i * n:(i + 1) * n].rearrange("p (k i) -> p k i", k=KD) for i in range(2)] + [w[:, 2 * n:3 * n].rearrange("p (f n) -> p f n", f=IC)]

        gateT, upT, downT = zip(spline_weights(S4), spline_weights(S7))
        o7 = 3 * KD * INTER
        wnat = R5[:, 0:3 * D].rearrange("p (m n) -> p m n", m=3)
        hTall = [S[:, 0:KD * TOK].rearrange("p (k t) -> p k t", k=KD) for S in (S0, S2)]
        blocks = lambda S, at, n: [S[:, at + f * 512:at + (f + 1) * 512] for f in range(n)]
        hFD = (blocks(S3, 0, IC), blocks(S5, 0, 3) + blocks(S7, o7, 3) + blocks(S3, KD * TOK, 2))

        bank = [ctx.enter_context(nc.psum_tensor(f"bank{i}", [P, 512], F32)) for i in range(8)]
        rows_d = nc.dram_tensor("rows_d", (TOK + CAP, ROW), F32).ap()
        acc_d = nc.dram_tensor("acc_d", (TOK + CAP, D), F32).ap()
        spline_d = nc.dram_tensor("spline_d", (3, SPLINE), F32).ap()
        table_d = nc.dram_tensor("table_d", (TABLE, 1), I32).ap()

        c_in = sem("c_in"); x_in = [sem(f"x_in{i}") for i in range(2)]; w_in = sem("w_in"); fin_out = sem("fin_out")
        cbf_ok = sem("cbf_ok"); z_ok = sem("z_ok")
        wp_in = [sem(f"wp_in{u}") for u in range(2)]
        wp_m = sem("wp_m"); wp_v = sem("wp_v"); wp_me = sem("wp_me"); wp_ve = sem("wp_ve"); wr_ok = sem("wr_ok")
        dch = sem("dch"); pch = sem("pch")
        lat = sem("lat"); lat_ok = sem("lat_ok")
        ms_ok = sem("ms_ok"); msr_ok = sem("msr_ok"); rs_ok = sem("rs_ok"); ckv_ok = sem("ckv_ok"); qk_ready = sem("qk_ready"); qk_tr = sem("qk_tr"); kT_ok = sem("kT_ok")
        wst_ok = sem("wst_ok"); wlo_ok = sem("wlo_ok"); qlo_ok = sem("qlo_ok"); q_rr = sem("q_rr"); q_ab = sem("q_ab"); rmul_ok = sem("rmul_ok")
        q_rope = sem("q_rope"); q_abs = sem("q_abs")
        s_mm = [sem("s_mm_e"), sem("s_mm_o")]; max_ok = [sem("max_e"), sem("max_o")]; exp_ok = [sem("exp_e"), sem("exp_o")]
        pt_mm = [sem("pt_e"), sem("pt_o")]; pt_ok = [sem("ptc_e"), sem("ptc_o")]
        pv_mm = sem("pv_mm"); o_ok = sem("o_ok"); oT_mm = sem("oT_mm"); oT_ok = sem("oT_ok")
        y_mm = sem("y_mm"); y_ok = sem("y_ok")
        mvy, ny, lny, mvx, nx, h_n, tr_n, hT_n = (sem(n) for n in ("mvy", "ny", "lny", "mvx", "nx", "h_n", "tr_n", "hT_n"))
        b_in = sem("b_in"); sw_in = sem("sw_in"); wvo_ok = sem("wvo_ok"); b_pool = sem("b_pool"); inp_ok = sem("inp_ok"); rms_ok = sem("rms_ok"); row_ok = sem("row_ok"); xnT_ok = sem("xnT_ok")
        lg_mm = sem("lg_mm"); lg_ok = sem("lg_ok"); lgs_ok = sem("lgs_ok"); lge_ok = sem("lge_ok"); mask_ok = sem("mask_ok"); rank_mm = sem("rank_mm")
        probs_ok = sem("probs_ok"); slots_ok = sem("slots_ok"); rows_out = sem("rows_out"); sc_st = sem("sc_st"); sc_out = [sem(f"sc_out{u}") for u in range(2)]
        table_in = sem("table_in"); init_out = sem("init_out")
        gu_mm = sem("gu_mm"); sil_ok = sem("sil_ok"); hf_ok = sem("hf_ok"); dn_mm = sem("dn_mm"); dn_ok = sem("dn_ok"); acc_out = sem("acc_out"); added = sem("added")
        we_in = [sem(f"we_in{u}") for u in range(4)]; idx_ok = sem("idx_ok"); adx_ok = sem("adx_ok"); xe_in = [sem(f"xe_in{u}") for u in range(4)]
        xe_tr = sem("xe_tr"); xe_ok = sem("xe_ok"); ge_mm = sem("ge_mm"); se_ok = sem("se_ok"); he_ok = sem("he_ok"); he_tr = sem("he_tr"); heT_ok = sem("heT_ok"); ye_mm = sem("ye_mm"); ye_ok = sem("ye_ok")
        cp_in = sem("cp_in"); samp_ok = sem("samp_ok"); spl_out = sem("spl_out"); nat_in = sem("nat_in")
        qkv_mm = sem("qkv_mm"); bq_ok = sem("bq_ok"); rs1_ok = sem("rs1_ok"); qk1_ok = sem("qk1_ok"); v1_ok = sem("v1_ok"); qst_ok = sem("qst_ok"); kbd_ok = sem("kbd_ok")
        s1_mm = [sem("s1_mm_e"), sem("s1_mm_o")]; max1_ok = [sem("max1_e"), sem("max1_o")]; exp1_ok = [sem("exp1_e"), sem("exp1_o")]
        pt1_mm = [sem("pt1_e"), sem("pt1_o")]; pt1_ok = [sem("ptc1_e"), sem("ptc1_o")]
        pv1_mm = sem("pv1_mm"); o1_ok = sem("o1_ok"); oT1_mm = sem("oT1_mm"); oT1_ok = sem("oT1_ok"); y1_mm = sem("y1_mm"); y1_ok = sem("y1_ok")
        gu1_mm = sem("gu1_mm"); sil1_ok = sem("sil1_ok"); hf1_ok = sem("hf1_ok"); up1_ok = sem("up1_ok"); dn1_mm = sem("dn1_mm"); dn1_ok = sem("dn1_ok")
        add_out = sem("add_out"); back_in = [sem(f"back_in{i}") for i in range(QN)]; xb_ok = sem("xb_ok")

        EARLY = {0: (0, 0), 1: (0, 1), 2: (0, 2), 3: (1, 0), 4: (1, 1), 5: (1, 2)}
        LATE = ((0, 3), (1, 3))
        PASS = ((0, 0), (0, 1), (0, 2), (1, 0), (0, 3), (1, 1), (1, 2), (1, 3))

        def first_bank(i, q):
            return 6 if (i, q) == (3, QN - 1) else 2 * (q % 2)

        latent_banks = ((4, 5, 6), (7, 0, 1))

        block = ctx.enter_context(nc.Block())

        @block.sync
        def _(sp):
            sp.dma_start(cst[:, :, :], T["cst"]).then_inc(c_in, 16)
            sp.dma_start(vecs[:, :], T["vecs"]).then_inc(c_in, 16)
            sp.dma_start(Wq[:, :, 1:3, :], T["w_rope"]).then_inc(c_in, 16)
            sp.dma_start(rope_k, T["rope_k"]).then_inc(w_in, 16)
            sp.dma_start(rope_q, T["rope_q"]).then_inc(w_in, 16)
            for i in range(2):
                half = slice(i * PAIRS // 2, (i + 1) * PAIRS // 2)
                sp.dma_start(wprep[:, half, :], T["wprep"][:, half, :]).then_inc(wp_in[i], 16)

            for name, dst in (("w_rt", w_rt), ("wn_bc", wn_bc), ("slot_c", slot_c), ("tok_i", tok_i)):
                sp.dma_start(dst[...], T[name]).then_inc(b_in, 16)
            sp.dma_start(table_d[0:SLOTS, :].rearrange("(p a) b -> p (a b)", p=P), T["spare"]).then_inc(init_out, 16)
            sp.wait_ge(z_ok, 1)
            sp.dma_start(rows_d[TOK:, :], zer[:, :]).then_inc(init_out, 16)
            sp.dma_start(acc_d[TOK:, :], zer[:, 0:D]).then_inc(init_out, 16)
            sp.wait_ge(qk_ready, QN)
            sp.wait_ge(ckv_ok, QN)
            sp.dma_start(frac, T["frac"]).then_inc(cp_in, 16)
            sp.dma_start(R4[:, 2 * SP_N:2 * SP_N + 2 * AL_N].rearrange("p (a r n) -> p a r n", a=2, r=ROWS), T["fracb"]).then_inc(cp_in, 16)
            sp.dma_start(cpw[:, :, :], T["cpw"]).then_inc(cp_in, 16)
            sp.wait_ge(y_ok, BATCH)
            sp.dma_start(sw_gu, T["sw_gu"]).then_inc(sw_in, 16)
            sp.dma_start(sw_d, T["sw_d"]).then_inc(sw_in, 16)
            sp.dma_start(wC, T["wC"]).then_inc(cp_in, 16)
            sp.wait_ge(probs_ok, 1)
            sp.wait_ge(row_ok, QN)
            sp.dma_start(rows_d[0:TOK, :].rearrange("(t p) n -> p t n", p=P), XNP).then_inc(rows_out, 16)
            sp.wait_ge(slots_ok, 1)
            for u in range(4):
                sp.dma_start(wexp[:, u, :], T["wexp"][u, :, :]).then_inc(we_in[u], 16)
            def acc_store(c):
                sp.wait_ge(dn_ok, 4 * c + 4)
                sp.dma_start(acc_d[bass.ds(4 * P * c, 4 * P), :].rearrange("(t p) n -> p t n", p=P), INP[:, bass.ds(4 * c, 4), :]).then_inc(acc_out, 16)

            acc_store(0)
            with sp.Fori(0, 3) as m:
                sp.wait_ge(samp_ok, m + 1)
                sp.dma_start(spline_d[bass.ds(m, 1), :].rearrange("a (p n) -> (a p) n", p=P), samp.rearrange("p r n -> p (r n)")).then_inc(spl_out, 16)
                acc_store(m + 1)

            def natural(j):
                for m in range(2):
                    sp.dma_start(wnat[:, m, :], spline_d[m, bass.ds(P * D * j, P * D)].rearrange("(p n) -> p n", p=P)).then_inc(nat_in, 16)
                sp.dma_start(wnat[:, 2, :].rearrange("p (k i) -> p k i", k=KD),
                             spline_d[2, 0:D * INTER].rearrange("(k p j i) -> p j k i", k=KD, p=P, j=IC)[:, bass.ds(j, 1), :, :].rearrange("p a k i -> p (a k) i")).then_inc(nat_in, 16)

            sp.wait_ge(spl_out, 48)
            natural(0)
            with sp.Fori(1, E0 // 4) as i:
                for u in range(4):
                    sp.wait_ge(ye_mm, 4 * i + u - 3)
                    sp.dma_start(wexp[:, u, :], T["wexp"][bass.ds(4 * i + u, 1), :, :].rearrange("a p n -> (a p) n")).then_inc(we_in[u], 16)
                    if u == 2:
                        natural(i)
            sp.wait_ge(add_out, 16 * E0)
            for q in range(QN):
                sp.dma_start(Y[:, QT * q:QT * (q + 1), :], acc_d[QT * P * q:QT * P * (q + 1), :].rearrange("(t p) n -> p t n", p=P)).then_inc(back_in[q], 16)
        @block.gpsimd
        def _(pool):
            ch = Tally(pool, pch)
            ch.mark(pool.memset(zbf[:, :], 0.0))
            ch.mark(pool.memset(mhalf[:, :], -0.5))
            ch.mark(pool.memset(zer[:, :], 0.0))
            ch.wait()
            pool.nop().then_inc(z_ok, 1)

            def roots(k, i, q, after=None):
                src_sem, done = ((mvy, ny), (mvx, nx))[k]
                quarter = bass.ds(QT * q, QT)
                inv, off = norm[:, k, quarter, 0], norm[:, k, quarter, 1]
                pool.wait_ge(src_sem, QN * (i if k else i - 1) + q + 1)
                ch.mark(pool.nop())
                ch.mark(pool.tensor_scalar(off, mv[:, k, quarter, 0], -1.0, None, ALU.mult))
                ch.link(pool.tensor_scalar(inv, mv[:, k, quarter, 1], LN_EPS, None, ALU.add))
                ch.link(pool.tensor_tensor(inv, inv, mhalf[:, :], ALU.pow))
                pool.tensor_tensor(off, off, inv, ALU.mult).then_inc(done, 1)
                if after is not None:
                    after(quarter, inv)

            def ln_roots(i, order, after=None):
                for k, q in order:
                    roots(k, i, q, after if k else None)

            def rms_root(quarter, inv):
                w = rms[:, quarter]
                ch.wait()
                ch.link(pool.tensor_tensor(w, mv[:, 1, quarter, 1], inv, ALU.mult))
                ch.link(pool.tensor_tensor(w, w, inv, ALU.mult))
                ch.link(pool.tensor_scalar(w, w, RMS_EPS, None, ALU.add))
                pool.tensor_tensor(w, w, mhalf[:, :], ALU.pow).then_inc(rms_ok, 1)

            for q in range(QN):
                roots(1, 0, q)
            pool.wait_ge(msr_ok, 1)
            ch.link(pool.tensor_scalar(ms[:, :, :], ms[:, :, :], RMS_EPS, None, ALU.add))
            pool.tensor_tensor(ms[:, :, :], ms[:, :, :], mhalf[:, None, 0:2].to_broadcast([P, TILES, 2]), ALU.pow).then_inc(rs_ok, 1)
            with pool.Fori(0, QN) as q:
                quarter = bass.ds(QT * q, QT)
                pool.wait_ge(rs_ok, 1)
                pool.tensor_tensor(ckv[:, quarter, :], LATS[:, quarter, QL:QL + KVL], ms[:, quarter, 1, None].to_broadcast([P, QT, KVL]), ALU.mult).then_inc(ckv_ok, 1)
            pool.wait_ge(wr_ok, 1)
            pool.wait_ge(wp_me, PAIRS + 2)

            def rope_sum(g, u):
                pool.wait_ge(rmul_ok, g + 1)
                ch.link(pool.tensor_tensor(qT[64:128, u, 0, :], rmul[64:128, u, 0, :], rmul[64:128, u, 1, :], ALU.add))
                pool.tensor_tensor(qT[0:64, u, 1, :], rmul[0:64, u, 0, :], rmul[0:64, u, 1, :], ALU.add).then_inc(q_rope, 1)
                pool.wait_ge(q_rope, g + 1)
                ch.mark(pool.nop())

            rope_sum(0, 0)
            rope_sum(1, 1)

            STEP = 2
            with pool.Fori(0, BATCH - 1) as b:
                ch.enter(b, 8 * STEP)
                with pool.Fori(0, 3) as i:
                    ch.enter(i, 2 * STEP)
                    for u in range(2):
                        g = 8 * b + 2 * i + u
                        rope_sum(g + 2, u)
                ch.leave(3)
                for u in range(2):
                    g = 8 * b + 6 + u
                    rope_sum(g + 2, u)
            ch.leave(BATCH - 1)
            for p in range(6):
                g = 8 * (BATCH - 1) + p
                if p >= 1:
                    k, q = EARLY[p - 1]
                    ln_roots(1, ((k, q),), rms_root)
                    pool.wait_ge(rms_ok if k else ny, q + 1)
                    ch.mark(pool.nop())
                rope_sum(g + 2, p % 2)
            ln_roots(1, (EARLY[5],), rms_root)
            ln_roots(1, LATE, rms_root)
            pool.wait_ge(slots_ok, 1)
            pool.wait_ge(b_in, 64)
            pool.wait_ge(init_out, 48)
            ch.mark(pool.nop())
            with pool.Fori(0, BATCH) as b:
                ch.enter(b, 2)
                for u in range(2):
                    ch.mark(pool.nop())
                    pool.tensor_copy(slot_st[:, u, :], slot_i[:, bass.ds(2 * b + u, 1), :].rearrange("p a k -> p (a k)")).then_inc(sc_st, 1)
                    pool.tensor_copy(tok_st[:, u:u + 1], tok_i[:, bass.ds(2 * b + u, 1)]).then_inc(sc_st, 1)
                pool.wait_ge(sc_st, 4 * b + 4)
                pool.nop().then_inc(b_pool, 1)
                for u in range(2):
                    for k in range(TOPK):
                        pool.indirect_dma_start(out=table_d, out_offset=bass.IndirectOffsetOnAxis(ap=slot_st[:, u, k:k + 1], axis=0),
                                                in_=tok_st[:, u:u + 1], in_offset=None).then_inc(sc_out[u], 16)
                for u in range(2):
                    pool.wait_ge(sc_out[u], 64 * b + 64)
                pool.nop().then_inc(b_pool, 1)
            ch.leave(BATCH)
            pool.dma_start(table_sb[:, :], table_d[0:SLOTS, :].rearrange("(p a) b -> p (a b)", p=P)).then_inc(table_in, 16)
            pool.wait_ge(table_in, 16)
            pool.wait_ge(rows_out, 16)
            ch.mark(pool.nop())

            def gather(e, u):
                pool.tensor_copy(idx_st[:, u:u + 1], table_sb[:, bass.ds(e, 1)]).then_inc(idx_ok, 1)
                pool.wait_ge(idx_ok, e + 1)
                ch.mark(pool.nop())
                pool.indirect_dma_start(out=Xe[:, u, :], out_offset=None, in_=rows_d, in_offset=bass.IndirectOffsetOnAxis(ap=idx_st[:, u:u + 1], axis=0))\
                    .then_inc(xe_in[u], 16)

            def step(e, u, more):
                pool.tensor_copy(add_idx[:, u % 2:u % 2 + 1], table_sb[:, bass.ds(e, 1)]).then_inc(adx_ok, 1)
                pool.wait_ge(adx_ok, e + 1)
                pool.wait_ge(add_out, 16 * e)
                pool.nop().then_inc(added, 1)
                pool.wait_ge(ye_ok, e + 1)
                ch.mark(pool.nop())
                pool.indirect_dma_start(out=acc_d, out_offset=bass.IndirectOffsetOnAxis(ap=add_idx[:, u % 2:u % 2 + 1], axis=0), in_=yE[:, u % 2, :], in_offset=None,
                                        compute_op=ALU.add).then_inc(add_out, 16)
                if more:
                    ch.mark(pool.nop())
                    gather(e + 4, u)

            for e in range(4):
                gather(e, e)
            pool.wait_ge(acc_out, 64)
            ch.mark(pool.nop())
            with pool.Fori(0, E0 // 4 - 1) as i:
                ch.enter(i, 12)
                for u in range(4):
                    step(4 * i + u, u, True)
            ch.leave(E0 // 4 - 1)
            for u in range(4):
                step(E0 - 4 + u, u, False)
            ln_roots(2, PASS)
            pool.wait_ge(qk1_ok, 3 * QN)
            ch.mark(pool.nop())

            def key_blocks(b):
                pool.tensor_tensor(Kbd[:, bass.ds(b % 2, 1), :, :].rearrange("p a j s -> p (a j) s"), kTr[:, None, bass.ds(SEQ * b, SEQ)].to_broadcast([P, 8, SEQ]),
                                   head_row[:, :, None].to_broadcast([P, 8, SEQ]), ALU.mult).then_inc(kbd_ok, 1)
                pool.wait_ge(kbd_ok, b + 1)
                ch.mark(pool.nop())

            def queries(b, c):
                pool.tensor_copy(qst[:, c, :], qTall[:, c, bass.ds(SEQ * b, SEQ)]).then_inc(qst_ok, 1)
                pool.wait_ge(qst_ok, 2 * b + c + 1)
                ch.mark(pool.nop())

            key_blocks(0)
            queries(0, 0)
            queries(0, 1)
            key_blocks(1)

            def batch(b, more):
                for c in range(2):
                    pool.wait_ge(s1_mm[1], 8 * b + 4 * c + 4)
                    ch.mark(pool.nop())
                    queries(b + 1, c)
                if more:
                    key_blocks(b + 2)

            with pool.Fori(0, BATCH - 2) as b:
                ch.enter(b, 5)
                batch(b, True)
            ch.leave(BATCH - 2)
            batch(BATCH - 2, False)
            ln_roots(3, [EARLY[p] for p in range(6)])
            ln_roots(3, LATE)
            for q in range(QN):
                roots(0, 4, q)

        @block.scalar
        def _(act):
            act.dma_start(X[:, 0:8, :], T["x"][:, 0:8, :]).then_inc(x_in[0], 16)
            act.dma_start(X[:, 8:16, :], T["x"][:, 8:16, :]).then_inc(x_in[1], 16)
            act.dma_start(w_lat, T["w_lat"]).then_inc(w_in, 16)

            def tile(buf, t):
                return buf[:, bass.ds(t, 1), :].rearrange("p a n -> p (a n)")

            def scaled(k, t, dst, src):
                return act.activation(dst, src, ACT.Identity, scale=norm[:, k, bass.ds(t, 1), 0], bias=norm[:, k, bass.ds(t, 1), 1])

            def output_norm(i, q):
                act.wait_ge(ny, QN * (i - 1) + q + 1)
                for u in range(QT):
                    ins = scaled(0, QT * q + u, tile(Y, QT * q + u), tile(Y, QT * q + u))
                ins.then_inc(lny, 1)

            def x_norm(i, q):
                act.wait_ge(nx, QN * i + q + 1)
                for u in range(QT):
                    ins = scaled(1, QT * q + u, tile(H, QT * q + u), tile(X, QT * q + u))
                ins.then_inc(h_n, 1)

            def norms(i, order):
                for k, q in order:
                    (output_norm, x_norm)[k](i, q)

            for q in range(QN):
                x_norm(0, q)
            with act.Fori(0, QN) as q:
                for u in range(QT):
                    act.wait_ge(lat, QT * q + u + 1)
                    act.activation(tile(LATS, QT * q + u), bank[4 + u][:, 0:LAT], ACT.Identity).then_inc(lat_ok, 1)
            act.wait_ge(lat_ok, TILES)
            act.activation(sq_q, LATS[:, :, 0:QL], ACT.Square, scale=float(QL ** -0.5)).then_inc(ms_ok, 1)
            act.activation(sq_kv, LATS[:, :, QL:QL + KVL], ACT.Square, scale=float(KVL ** -0.5)).then_inc(ms_ok, 1)
            act.wait_ge(c_in, 48)
            with act.Fori(0, PAIRS // 2) as i:
                for u in range(2):
                    act.wait_ge(wp_v, 2 * i + u + 1)
                    act.activation(Wvo[:, bass.ds(2 * i + u, 1), :].rearrange("p a n -> p (a n)"), bank[2 + u][:, 0:D], ACT.Copy, scale=vecs[:, KVL:KVL + 1]).then_inc(wp_ve, 1)
            with act.Fori(0, QN // 2) as i:
                for v in range(2):
                    q = 2 * i + v
                    act.wait_ge(qk_tr, q + 1)
                    for dst, src in zip((qlatT[0], kTa, kTb), latent_banks[v]):
                        ins = act.activation(dst[:, bass.ds(QT * P * q, QT * P)], bank[src][0:dst.shape[0], :], ACT.Copy)
                    ins.then_inc(kT_ok, 1)

            def abs_copy(g, u):
                act.wait_ge(q_ab, g + 1)
                act.activation(qT[0:64, u, 0, :], bank[2][0:64, 0:SEQ], ACT.Copy)
                act.activation(qT[64:128, u, 1, :], bank[2][64:128, 0:SEQ], ACT.Copy).then_inc(q_abs, 1)

            def exps(g, u, e):
                act.wait_ge(max_ok[e], g + 1)
                for t, (lo, n) in enumerate(((0, P), (P, SEQ))):
                    ins = act.activation(Pr[:, u, e, lo:lo + n], bank[e][:, lo:lo + n], ACT.Exp, bias=nmax[:, u, t, e:e + 1],
                                         accum_out=sums[:, u, t, e:e + 1])
                ins.then_inc(exp_ok[e], 1)

            def stage(g, u, first=False):
                if not first:
                    act.wait_ge(q_ab, g - 1)
                act.activation(wst[0][:, u, :, :], Wq[:, bass.ds(g % PAIRS, 1), :, :].rearrange("p a k m -> p (a k) m"), ACT.Copy).then_inc(wst_ok, 1)

            def pt_copy(g):
                act.wait_ge(pt_mm[0], g + 1)
                act.activation(PTs[:, 0, :], bank[4][:, 0:CAUSAL], ACT.Copy).then_inc(pt_ok[0], 1)

            act.wait_ge(wr_ok, 1)
            act.wait_ge(wp_me, PAIRS + 2)
            stage(0, 0, True)
            stage(1, 1, True)
            abs_copy(0, 0)
            stage(2, 0)
            exps(0, 0, 0)
            exps(0, 0, 1)
            abs_copy(1, 1)

            def y_copy(b):
                act.wait_ge(y_mm, b + 1)
                act.activation(Y[:, bass.ds(2 * b, 2), :], bank[7][:, :].rearrange("p (t n) -> p t n", t=2), ACT.Copy).then_inc(y_ok, 1)

            def step(g, u, q_next=True, s_next=True, w_next=True, y_of=None):
                pt_copy(g)
                if s_next:
                    exps(g + 1, 1 - u, 0)
                if q_next:
                    abs_copy(g + 2, u)
                if w_next:
                    stage(g + 3, 1 - u)
                if y_of is not None:
                    y_copy(y_of)
                if s_next:
                    exps(g + 1, 1 - u, 1)

            def batch(b, first=False):
                step(8 * b, 0, y_of=None if first else b - 1)
                step(8 * b + 1, 1)
                with act.Fori(1, PAIRS // 2) as i:
                    for u in range(2):
                        step(8 * b + 2 * i + u, u)

            batch(0, first=True)
            with act.Fori(1, BATCH - 1) as b:
                batch(b)
            for p in range(PAIRS):
                step(8 * (BATCH - 1) + p, p % 2, p < 6, p < 7, p < 5, y_of=BATCH - 2 if p == 0 else None)
                if p - 2 in EARLY:
                    norms(1, (EARLY[p - 2],))
            y_copy(BATCH - 1)
            norms(1, LATE)
            with act.Fori(0, QN // 2) as i:
                for v in range(2):
                    q = 2 * i + v
                    act.wait_ge(hT_n, 2 * QN + 2 * q + 2)
                    act.activation(xnT[:, :, bass.ds(QT * P * q, QT * P)], hTs[v], ACT.Identity).then_inc(xnT_ok, 1)
                    act.wait_ge(lg_mm, q + 1)
                    lg = bank[4][:, 0:QT * (E0 + 1)].rearrange("p (u n) -> p u n", u=QT)
                    act.activation(LG[:, bass.ds(QT * q, QT), :], lg[:, :, 0:E0], ACT.Identity)
                    act.activation(gate[:, bass.ds(QT * q, QT)], lg[:, :, E0], ACT.Identity).then_inc(lg_ok, 1)
            act.wait_ge(lgs_ok, 1)
            act.activation(EXPL, EXPL, ACT.Exp).then_inc(lge_ok, 1)
            act.activation(gate[:, :], gate[:, :], ACT.Exp, scale=-1.0).then_inc(lge_ok, 1)
            with act.Fori(0, 4) as c:
                for f in range(FSC):
                    act.wait_ge(gu_mm, FSC * c + f + 1)
                    act.wait_ge(hf_ok, FSC * c + f + 1)
                    act.activation(sil[:, f % 2, :], bank[2 * (f % 2)][:, :], ACT.Silu).then_inc(sil_ok, 1)
            def xe_copy(e, u):
                act.wait_ge(xe_tr, e + 1)
                act.activation(XeT[:, u % 2, :, :], bank[u % 2][:, 0:D].rearrange("p (k t) -> p k t", k=KD), ACT.Copy).then_inc(xe_ok, 1)

            def gate_silu(e, u):
                act.wait_ge(ge_mm, e + 1)
                act.activation(gE[:, u % 2, :], bank[2 + u % 2][:, 0:FE], ACT.Silu).then_inc(se_ok, 1)

            def step(e, u, more=True):
                if more or u < 3:
                    gate_silu(e + 1, u + 1)
                if more or u < 2:
                    xe_copy(e + 2, u)

            xe_copy(0, 0)
            xe_copy(1, 1)
            gate_silu(0, 0)
            with act.Fori(0, E0 // 4 - 1) as i:
                for u in range(4):
                    step(4 * i + u, u)
            for u in range(4):
                step(E0 - 4 + u, u, False)
            norms(2, PASS)
            act.wait_ge(bq_ok, 1)
            with act.Fori(0, QN) as q:
                for c in range(KD):
                    act.wait_ge(qkv_mm, 4 * q + c + 1)
                    act.activation(qTall[:, c, bass.ds(QT * P * q, QT * P)], bank[4 + c][:, :], ACT.Identity, bias=bq[:, c:c + 1], scale=SCALE1).then_inc(qk1_ok, 1)
                act.wait_ge(qkv_mm, 4 * q + 3)
                act.activation(kTr[:, bass.ds(QT * P * q, QT * P)], bank[6][:, :], ACT.Identity, bias=bk, scale=1.0).then_inc(qk1_ok, 1)

            def exps1(g, p, e):
                act.wait_ge(max1_ok[e], g + 1)
                for t, (lo, n) in enumerate(((0, P), (P, SEQ))):
                    ins = act.activation(Pr[:, p % 2, e, lo:lo + n], bank[2 * (p % 2) + e][:, lo:lo + n], ACT.Exp, bias=nmax[:, p % 2, t, e:e + 1],
                                         accum_out=sumC[:, t, 2 * p + e:2 * p + e + 1])
                ins.then_inc(exp1_ok[e], 1)

            def step(b, p, more=True, before=True):
                g = 8 * b + p
                if before and p == 3:
                    act.wait_ge(oT1_mm, b)
                    act.activation(oTC_sb, bank[7][:, :].rearrange("p (c t) -> p c t", c=KD), ACT.Copy).then_inc(oT1_ok, 1)
                if more:
                    if p == 7:
                        act.wait_ge(rs1_ok, b + 1)
                    exps1(g + 1, (p + 1) % 8, 0)
                act.wait_ge(pt1_mm[0], g + 1)
                act.activation(PTc[p % 2][:, 0, :], bank[4][:, 0:CAUSAL], ACT.Copy).then_inc(pt1_ok[0], 1)
                if more:
                    exps1(g + 1, (p + 1) % 8, 1)

            exps1(0, 0, 0)
            exps1(0, 0, 1)
            for p in range(8):
                step(0, p, before=False)
            with act.Fori(1, BATCH - 1) as b:
                for p in range(8):
                    step(b, p)
            for p in range(8):
                step(BATCH - 1, p, more=p < 7)
                if p - 1 in EARLY:
                    norms(3, (EARLY[p - 1],))
            act.wait_ge(oT1_mm, BATCH)
            act.activation(oTC_sb, bank[7][:, :].rearrange("p (c t) -> p c t", c=KD), ACT.Copy).then_inc(oT1_ok, 1)
            norms(3, LATE)
            with act.Fori(0, 4) as c:
                for f in range(IC):
                    act.wait_ge(gu1_mm, IC * c + f + 1)
                    act.wait_ge(hf1_ok, IC * c + f + 1)
                    act.activation(sil[:, f % 2, :], bank[2 * (f % 2)][:, :], ACT.Silu).then_inc(sil1_ok, 1)
            for q in range(QN):
                output_norm(4, q)
            with act.Fori(0, QN) as q:
                act.wait_ge(xb_ok, q + 1)
                act.dma_start(out[:, bass.ds(QT * q, QT), :], X[:, bass.ds(QT * q, QT), :]).then_inc(fin_out, 16)
            act.wait_ge(fin_out, 16 * QN)

        @block.vector
        def _(dve):
            ch = Tally(dve, dch)
            dve.sem_inc(hf_ok, 2)
            dve.sem_inc(wp_me, 2)
            dve.sem_inc(wp_ve, 2)

            def tile(buf, t):
                return buf[:, bass.ds(t, 1), :].rearrange("p a n -> p (a n)")

            def moments(k, i, q, src):
                done, n = (mvy, QN * (i - 1) + q) if k == 0 else (mvx, QN * i + q)
                if n >= 2:
                    dve.wait_ge(done, n - 1)
                st = stats[:, k, n % 2]
                for u in range(QT):
                    ch.mark(dve.bn_stats(st[:, u, :], src[:, QT * q + u, :]))
                ch.wait()
                for u in range(QT):
                    ins = dve.bn_aggr(mv[:, k, QT * q + u, :], st[:, u, :])
                ins.then_inc(done, 1)

            def add_quarter(i, q):
                dve.wait_ge(lny, QN * (i - 1) + q + 1)
                quarter = bass.ds(QT * q, QT)
                ch.mark(dve.tensor_tensor(X[:, quarter, :], X[:, quarter, :], Y[:, quarter, :], ALU.add))

            def ln_part(i, k, q):
                if k == 0:
                    moments(0, i, q, Y)
                else:
                    add_quarter(i, q)
                    ch.wait()
                    moments(1, i, q, X)

            def hT_copies(i, q):
                for v in range(2):
                    dve.wait_ge(tr_n, TILES * i + QT * q + 2 * v + 2)
                    dst = hTs[q % 2][:, :, v * SEQ:(v + 1) * SEQ]
                    dve.tensor_copy(dst.rearrange("p k (u t) -> p k u t", u=2), bank[first_bank(i, q) + v][:, :].rearrange("p (u k t) -> p k u t", u=2, k=KD)).then_inc(hT_n, 1)

            for q in range(QN):
                dve.wait_ge(x_in[q // 2], 16)
                moments(1, 0, q, X)
                if q == 0:
                    dve.wait_ge(c_in, 48)
                    dve.tensor_copy(cbf[:, :, :], cst[:, :, :]).then_inc(cbf_ok, 1)
                    dve.tensor_copy(ident[:, :], cst[:, 0, :]).then_inc(cbf_ok, 1)
            ch.link(dve.tensor_scalar(vecs[:, KVL + 1:KVL + 2], vecs[:, KVL + 1:KVL + 2], SCALE0, None, ALU.mult))
            for q in range(QN):
                if q >= 2:
                    dve.wait_ge(lat, QT * (q - 1))
                hT_copies(0, q)
                if q == 0:
                    dve.tensor_scalar(Wq[:, :, 1:3, :].rearrange("p a k m -> p a (k m)"), Wq[:, :, 1:3, :].rearrange("p a k m -> p a (k m)"),
                                      vecs[0:QL, KVL + 1:KVL + 2], None, ALU.mult).then_inc(wr_ok, 1)
            dve.wait_ge(ms_ok, 1)
            dve.tensor_reduce(ms[:, :, 0], sq_q, AX.X, ALU.add)
            dve.wait_ge(ms_ok, 2)
            dve.tensor_reduce(ms[:, :, 1], sq_kv, AX.X, ALU.add).then_inc(msr_ok, 1)
            with dve.Fori(0, PAIRS // 2) as i:
                for u in range(2):
                    dve.wait_ge(wp_m, 2 * i + u + 1)
                    dve.scalar_tensor_tensor(Wq[:, bass.ds(2 * i + u, 1), 0, :].rearrange("p a (e m) -> p (a e) m", e=2),
                                             bank[u][0:QL, 0:P].rearrange("p (e m) -> p e m", e=2), vecs[0:QL, KVL + 1:KVL + 2],
                                             vecs[0:QL, None, 0:KVL].to_broadcast([QL, 2, KVL]), ALU.mult, ALU.mult).then_inc(wp_me, 1)
            dve.wait_ge(w_in, 48)
            dve.wait_ge(rs_ok, 1)
            def latent_quarter(q):
                v, quarter = q % 2, slice(QT * q, QT * (q + 1))
                if q >= 2:
                    dve.wait_ge(qk_tr, q - 1)
                lats = LATS[:, quarter, :]
                ch.mark(dve.tensor_tensor(qn[:, v], lats[:, :, 0:QL], ms[:, quarter, 0, None].to_broadcast([P, QT, QL]), ALU.mult))
                for t in range(2):
                    ins = dve.tensor_tensor(kr2[:, v, 2 * t:2 * t + 2], lats[:, 2 * t:2 * t + 2, QL + KVL:LAT].rearrange("p u (a n) -> p u a n", a=2), rope_k, ALU.mult)
                ch.mark(ins)
                for a in (0, 2):
                    ins = dve.tensor_tensor(kst[:, v, :, a, :], lats[:, :, QL:QL + KVL], ms[:, quarter, 1, None].to_broadcast([P, QT, KVL]), ALU.mult)
                ch.mark(ins)
                ch.wait()
                dve.tensor_tensor(kst[:, v, :, 1, :], kr2[:, v, :, 0, :], kr2[:, v, :, 1, :], ALU.add).then_inc(qk_ready, 1)

            def latent_low(q):
                dve.wait_ge(kT_ok, q + 1)
                at = slice(QT * P * q, QT * P * (q + 1))
                dve.tensor_tensor(qlatT[1][:, at], bank[latent_banks[q % 2][0]][0:QL, :], qlatT[0][:, at].bitcast(F32), ALU.subtract).then_inc(qlo_ok, 1)

            latent_quarter(0)
            for q in range(1, QN):
                latent_quarter(q)
                latent_low(q - 1)
            latent_low(QN - 1)

            def split(high, low, x):
                ch.mark(dve.tensor_copy(high, x))
                ch.wait()
                return dve.tensor_tensor(low, x, high.bitcast(F32), ALU.subtract)

            def rope_mul(g, u, first=False):
                dve.wait_ge(q_rr, g + 1)
                if not first:
                    dve.wait_ge(q_rope, g - 1)
                dve.tensor_tensor(rmul[:, u, :, :], bank[3][:, :].rearrange("p (k t) -> p k t", k=2), rope_q[:, :, :], ALU.mult).then_inc(rmul_ok, 1)

            def stage_low(g, u):
                dve.wait_ge(wst_ok, g + 1)
                dve.tensor_tensor(wst[1][:, u, :, :], Wq[:, bass.ds(g % PAIRS, 1), :, :].rearrange("p a k m -> p (a k) m"), wst[0][:, u, :, :].bitcast(F32), ALU.subtract)\
                    .then_inc(wlo_ok, 1)

            def maxes(g, u, e):
                dve.wait_ge(s_mm[e], g + 1)
                for t, (lo, n) in enumerate(((0, P), (P, SEQ))):
                    ins = dve.tensor_reduce(nmax[:, u, t, e:e + 1], bank[e][:, lo:lo + n], AX.X, ALU.max, negate=True)
                ins.then_inc(max_ok[e], 1)

            def pt_copy(g):
                dve.wait_ge(pt_mm[1], g + 1)
                dve.tensor_copy(PTs[:, 1, :], bank[5][:, 0:CAUSAL]).then_inc(pt_ok[1], 1)

            def o_norm(g, u):
                dve.wait_ge(exp_ok[1], g + 1)
                ch.link(dve.reciprocal(rsum[:, :, :], sums[:, u, :, :]))
                dve.wait_ge(pv_mm, g + 1)
                dve.tensor_tensor(o_sb[:, :, :].rearrange("p t (e n) -> p (t e) n", e=2), bank[6][:, 0:SEQ].rearrange("p (c n) -> p c n", c=4),
                                  rsum[:, :, :].rearrange("p t e -> p (t e)")[:, :, None].to_broadcast([P, 4, KVL]), ALU.mult).then_inc(o_ok, 1)

            def oT_copy(g):
                dve.wait_ge(oT_mm, g + 1)
                split(*oT2, bank[6][:, SEQ:2 * SEQ]).then_inc(oT_ok, 1)

            stage_low(0, 0)
            stage_low(1, 1)
            rope_mul(0, 0, True)
            rope_mul(1, 1, True)
            stage_low(2, 0)
            maxes(0, 0, 0)
            maxes(0, 0, 1)
            dve.wait_ge(wp_ve, PAIRS + 2)
            split(*Wvo2, Wvo).then_inc(wvo_ok, 1)

            def step(g, u, q_next=True, s_next=True, w_next=True, first=False):
                if s_next:
                    maxes(g + 1, 1 - u, 0)
                if not first:
                    oT_copy(g - 1)
                pt_copy(g)
                if q_next:
                    rope_mul(g + 2, u)
                if w_next:
                    stage_low(g + 3, 1 - u)
                if s_next:
                    maxes(g + 1, 1 - u, 1)
                o_norm(g, u)

            step(0, 0, first=True)
            step(1, 1)
            with dve.Fori(1, PAIRS * (BATCH - 1) // 2) as i:
                ch.enter(i - 1, 4)
                for u in range(2):
                    step(2 * i + u, u)
            ch.leave(PAIRS * (BATCH - 1) // 2 - 1)
            for p in range(PAIRS):
                step(PAIRS * (BATCH - 1) + p, p % 2, p < 6, p < 7, p < 5)
                if p == 0:
                    dve.wait_ge(y_ok, BATCH - 2)
                if p in EARLY:
                    ln_part(1, *EARLY[p])
            oT_copy(PAIRS * BATCH - 1)
            dve.wait_ge(y_ok, BATCH)
            dve.wait_ge(b_in, 64)
            def xn_quarter(q):
                dve.wait_ge(rms_ok, q + 1)
                dve.wait_ge(h_n, QN * 1 + q + 1)
                for u in range(QT):
                    t = QT * q + u
                    ins = dve.scalar_tensor_tensor(XNP[:, t, 0:D], INP[:, t, :], rms[:, t:t + 1], wn_bc[:, :], ALU.mult, ALU.mult)
                ins.then_inc(row_ok, 1)

            def xnT_quarter(q):
                if q >= 2:
                    dve.wait_ge(lg_mm, q - 1)
                    dve.wait_ge(xnT_ok, q - 1)
                hT_copies(1, q)

            xn_quarter(0)
            ln_part(1, *LATE[0])
            xn_quarter(1)
            xnT_quarter(0)
            ln_part(1, *LATE[1])
            xn_quarter(2)
            xnT_quarter(1)
            xn_quarter(3)
            xnT_quarter(2)
            xnT_quarter(3)
            def shared_hidden(c, f):
                dve.wait_ge(sil_ok, FSC * c + f + 1)
                dve.tensor_tensor(hF[:, f, :], sil[:, f % 2, :], bank[2 * (f % 2) + 1][:, :], ALU.mult).then_inc(hf_ok, 1)

            def shared_out(c, t):
                dve.wait_ge(dn_mm, 4 * c + t + 1)
                dve.scalar_tensor_tensor(tile(INP, 4 * c + t), bank[4 + t % 2][:, 0:D], gate[:, bass.ds(4 * c + t, 1)], tile(INP, 4 * c + t),
                                         ALU.mult, ALU.add).then_inc(dn_ok, 1)

            dve.wait_ge(lg_ok, QN)
            bc = lambda v: v[:, :, None].to_broadcast([P, TILES, E0])
            ch.link(dve.tensor_reduce(rmx[:, :], LG, AX.X, ALU.max))
            dve.tensor_tensor(EXPL, LG, bc(rmx), ALU.subtract).then_inc(lgs_ok, 1)
            ch.mark(dve.memset(PP[:, :, E0:], -1.0))
            dve.wait_ge(lge_ok, 2)
            ch.link(dve.tensor_reduce(rsm[:, :], EXPL, AX.X, ALU.add))
            ch.mark(dve.reciprocal(rsm[:, :], rsm[:, :]))
            ch.link(dve.tensor_scalar(gate[:, :], gate[:, :], 1.0, None, ALU.add))
            ch.mark(dve.reciprocal(gate[:, :], gate[:, :]))
            ch.link(dve.tensor_tensor(PP[:, :, 0:E0], EXPL, bc(rsm), ALU.mult))
            dve.tensor_copy(XNP[:, :, D:], PP[:, :, 0:E0]).then_inc(probs_ok, 1)
            shared_hidden(0, 0)
            for t in range(TILES):
                ch.mark(dve.max(top8[:, t, :], PP[:, t, 0:E0]))
            ch.wait()
            ch.link(dve.memset(top8[:, :, TOPK:], -1.0))
            shared_hidden(0, 1)
            for t in range(TILES):
                ch.mark(dve.match_replace(RP[:, t, :], top8[:, t, :], PP[:, t, :], -2.0))
            ch.wait()
            dve.tensor_scalar(MBF[:, :, :], RP[:, :, 0:E0], -2.0, None, ALU.is_equal).then_inc(mask_ok, 1)
            ch.mark(dve.tensor_scalar(MSK, RP[:, :, 0:E0], -2.0, None, ALU.is_equal))
            for f in range(2, FSC):
                shared_hidden(0, f)
            dve.wait_ge(rank_mm, 1)
            rank = bank[7][:, :].rearrange("p (t e) -> p t e", t=TILES)
            ch.mark(dve.scalar_tensor_tensor(SLOT, rank, float(E0), slot_c[:, 0], ALU.mult, ALU.add))
            ch.link(dve.tensor_scalar(INV, rank, float(CAP), None, ALU.is_ge))
            for t in range(2):
                shared_out(0, t)
            ch.link(dve.copy_predicated(SLOT, INV.bitcast(U32), slot_c[:, 1]))
            ch.link(dve.tensor_tensor(SLOT, SLOT, MSK, ALU.mult))
            for t in range(TILES):
                ch.mark(dve.max(slot8[:, t, :], SLOT[:, t, :]))
            ch.wait()
            dve.tensor_scalar(slot_i[:, :, :], slot8[:, :, 0:TOPK], -1.0, None, ALU.add).then_inc(slots_ok, 1)
            for t in range(2, QT):
                shared_out(0, t)
            dve.wait_ge(cp_in, 64)
            dve.tensor_scalar(bq, bq, SCALE1, None, ALU.mult).then_inc(bq_ok, 1)
            p0, p1, p2, p3 = (cpw[:, :, k:k + ROWS + 1] for k in range(4))
            c0, c1, c2, c3 = (coef[:, :, k, :] for k in range(4))
            ch.mark(dve.tensor_copy(c0, p1))
            ch.link(dve.tensor_tensor(ctmp[:, :, :], p2, p0, ALU.subtract))
            ch.mark(dve.tensor_scalar(c1, ctmp[:, :, :], 0.5, None, ALU.mult))
            ch.mark(dve.scalar_tensor_tensor(c3, p2, -3.0, p3, ALU.mult, ALU.add))
            ch.link(dve.scalar_tensor_tensor(c2, p2, 4.0, p3, ALU.mult, ALU.subtract))
            ch.mark(dve.scalar_tensor_tensor(c3, p1, 3.0, c3, ALU.mult, ALU.add))
            ch.link(dve.scalar_tensor_tensor(c2, p1, -5.0, c2, ALU.mult, ALU.add))
            ch.mark(dve.tensor_tensor(c3, c3, p0, ALU.subtract))
            ch.link(dve.scalar_tensor_tensor(c2, p0, 2.0, c2, ALU.mult, ALU.add))
            ch.mark(dve.tensor_scalar(c3, c3, 0.5, None, ALU.mult))
            ch.link(dve.tensor_scalar(c2, c2, 0.5, None, ALU.mult))

            def spline_op(m, f):
                for out_, t_, row, n in ((samp, frac, 1, SPAN), (sampb, fracb, 0, ALT)):
                    c = coef[:, bass.ds(m, 1), 3 - (f + 1) // 2, row:row + ROWS].rearrange("p a r -> p (a r)")[:, :, None].to_broadcast([P, ROWS, n])
                    if f == 0:
                        ch.mark(dve.tensor_tensor(out_, t_, c, ALU.mult))
                    elif f % 2:
                        ch.mark(dve.tensor_tensor(out_, out_, c, ALU.add))
                    else:
                        ch.mark(dve.tensor_tensor(out_, out_, t_, ALU.mult))
                ch.wait()

            with dve.Fori(0, 3) as m:
                ch.enter(m, 2 * FSC)
                for f in range(FSC):
                    spline_op(m, f)
                    shared_hidden(m + 1, f)
                dve.copy_predicated(samp[:, :, 0:ALT], before.bitcast(U32), sampb).then_inc(samp_ok, 1)
                for t in range(QT):
                    shared_out(m + 1, t)
                dve.wait_ge(spl_out, 16 * m + 16)
            ch.leave(3)

            def hidden(e, u):
                dve.wait_ge(se_ok, e + 1)
                dve.tensor_tensor(hE[:, u % 2, :], gE[:, u % 2, :], bank[2 + u % 2][:, FE:2 * FE], ALU.mult).then_inc(he_ok, 1)

            def step(e, u, j, more=True):
                if more or u < 3:
                    hidden(e + 1, u + 1)
                dve.wait_ge(he_tr, e + 1)
                b = bank[4 + u % 2]
                dve.tensor_copy(hET[0:FEK, u % 2, :], b[0:FEK, 0:FEC * P]).then_inc(heT_ok, 1)
                if u < 2:
                    split(*(w[:, :, bass.ds(P * j, P)] for w in (gateT, upT)[u]), b[:, D:2 * D].rearrange("p (k i) -> p k i", k=KD))
                elif u == 2:
                    split(*(tile(w, j) for w in downT), b[:, D:2 * D])
                dve.wait_ge(ye_mm, e + 1)
                dve.wait_ge(added, e)
                dve.tensor_scalar(yE[:, u % 2, :], bank[6 + u % 2][:, 0:D], Xe[:, u, bass.ds(D + e, 1)], None, ALU.mult).then_inc(ye_ok, 1)

            hidden(0, 0)
            with dve.Fori(0, E0 // 4 - 1) as i:
                ch.enter(i, 3)
                for u in range(4):
                    step(4 * i + u, u, i)
            ch.leave(E0 // 4 - 1)
            for u in range(4):
                step(E0 - 4 + u, u, E0 // 4 - 1, False)
            def hT_quarter(q):
                if q >= 2:
                    dve.wait_ge(qkv_mm, 4 * (q - 1))
                hT_copies(2, q)

            def values(q):
                dve.wait_ge(qkv_mm, 4 * q + 4)
                dve.tensor_tensor(vall[:, QT * q:QT * (q + 1), :], bank[7][:, 0:QT * HD1].rearrange("p (u n) -> p u n", u=QT), bv_bc[:, None, :].to_broadcast([P, QT, HD1]),
                                  ALU.add).then_inc(v1_ok, 1)

            for k, q in PASS:
                if k == 0:
                    dve.wait_ge(back_in[q], 16)
                ln_part(2, k, q)
                if k == 1 and q >= 1 and q < QN - 1:
                    hT_quarter(q - 1)
            values(0)
            for q in range(2, QN):
                hT_quarter(q)
                values(q - 1)
            values(QN - 1)

            def maxes1(g, p, e):
                dve.wait_ge(s1_mm[e], g + 1)
                for t, (lo, n) in enumerate(((0, P), (P, SEQ))):
                    ins = dve.tensor_reduce(nmax[:, p % 2, t, e:e + 1], bank[2 * (p % 2) + e][:, lo:lo + n], AX.X, ALU.max, negate=True)
                ins.then_inc(max1_ok[e], 1)

            def hT_split(q):
                for v in range(2):
                    dve.wait_ge(tr_n, TILES * 3 + QT * q + 2 * v + 2)
                    split(*(w[:, :, QT * P * q + v * SEQ:QT * P * q + (v + 1) * SEQ].rearrange("p k (u t) -> p k u t", u=2) for w in hTall),
                          bank[first_bank(3, q) + v][:, :].rearrange("p (u k t) -> p k u t", u=2, k=KD)).then_inc(hT_n, 1)

            def o_norm1(b):
                dve.wait_ge(pv1_mm, 8 * b + 8)
                dve.tensor_tensor(oC_sb.rearrange("p t (h n) -> p (t h) n", n=HD1), bank[6][:, :].rearrange("p (c n) -> p c n", n=HD1),
                                  rsumC[:, :, :].rearrange("p t h -> p (t h)")[:, :, None].to_broadcast([P, 2 * H1, HD1]), ALU.mult).then_inc(o1_ok, 1)

            def y_add(b):
                dve.wait_ge(y1_mm, b + 1)
                dve.tensor_tensor(Y[:, bass.ds(2 * b, 2), :], bank[7][:, :].rearrange("p (t n) -> p t n", t=2), bo_bc[:, None, :].to_broadcast([P, 2, D]), ALU.add)\
                    .then_inc(y1_ok, 1)

            def step(b, p, more=True, before=True):
                g = 8 * b + p
                if before and p == 1:
                    o_norm1(b - 1)
                if before and p == 5:
                    y_add(b - 1)
                if p == 7:
                    dve.wait_ge(exp1_ok[1], g + 1)
                    ch.link(dve.reciprocal(rsumC[:, :, :], sumC[:, :, :]))
                    ch.link(dve.tensor_scalar(rsumC[:, 0, :], rsumC[:, 0, :], row_valid, None, ALU.mult))
                    dve.nop().then_inc(rs1_ok, 1)
                if more:
                    maxes1(g + 1, (p + 1) % 8, 0)
                    maxes1(g + 1, (p + 1) % 8, 1)
                dve.wait_ge(pt1_mm[1], g + 1)
                dve.tensor_copy(PTc[p % 2][:, 1, :], bank[5][:, 0:CAUSAL]).then_inc(pt1_ok[1], 1)

            maxes1(0, 0, 0)
            maxes1(0, 0, 1)
            for p in range(8):
                step(0, p, before=False)
            with dve.Fori(1, BATCH - 1) as b:
                ch.enter(b - 1, 2)
                for p in range(8):
                    step(b, p)
            ch.leave(BATCH - 2)
            for p in range(8):
                step(BATCH - 1, p, more=p < 7)
                if p == 0:
                    dve.wait_ge(y1_ok, BATCH - 2)
                if p in EARLY:
                    ln_part(3, *EARLY[p])
            hT_split(0)
            o_norm1(BATCH - 1)
            hT_split(1)
            y_add(BATCH - 1)
            dve.wait_ge(y1_ok, BATCH)
            dve.sem_inc(hf1_ok, 2)
            dve.sem_inc(up1_ok, 2)
            def hidden1(c, f):
                dve.wait_ge(sil1_ok, IC * c + f + 1)
                dve.tensor_tensor(sil[:, f % 2, :], sil[:, f % 2, :], bank[2 * (f % 2) + 1][:, :], ALU.mult).then_inc(up1_ok, 1)
                dve.wait_ge(up1_ok, IC * c + f + 3)
                split(hFD[0][f], hFD[1][f], sil[:, f % 2, :]).then_inc(hf1_ok, 1)

            def out1(c, t):
                dve.wait_ge(dn1_mm, 4 * c + t + 1)
                dve.tensor_copy(tile(Y, 4 * c + t), bank[4 + t % 2][:, 0:D]).then_inc(dn1_ok, 1)

            ln_part(3, *LATE[0])
            hT_split(2)
            ln_part(3, *LATE[1])
            for f in range(IC):
                if f == 3:
                    hT_split(3)
                hidden1(0, f)
            for t in range(QT):
                out1(0, t)
            with dve.Fori(1, QN - 1) as c:
                ch.enter(c - 1, IC)
                for f in range(IC):
                    hidden1(c, f)
                for t in range(QT):
                    out1(c, t)
            ch.leave(QN - 2)
            for f in range(IC):
                hidden1(QN - 1, f)

            def add_last(q):
                add_quarter(4, q)
                ch.wait()
                dve.nop().then_inc(xb_ok, 1)

            dve.wait_ge(dn1_ok, QT * (QN - 1))
            moments(0, 4, 0, Y)
            moments(0, 4, 1, Y)
            out1(QN - 1, 0)
            moments(0, 4, 2, Y)
            out1(QN - 1, 1)
            add_last(0)
            add_last(1)
            out1(QN - 1, 2)
            add_last(2)
            out1(QN - 1, 3)
            dve.wait_ge(dn1_ok, TILES)
            moments(0, 4, 3, Y)
            add_last(3)

        @block.tensor
        def _(pe):
            def transposes(i, q, src=H):
                sem_in, n = (row_ok, q + 1) if i == 1 else (h_n, QN * i + q + 1)
                pe.wait_ge(sem_in, n)
                if q >= 2:
                    pe.wait_ge(hT_n, 2 * QN * i + 2 * q - 2)
                for u in range(QT):
                    for k in range(KD):
                        at = (u % 2) * D + k * P
                        ins = pe.transpose(bank[first_bank(i, q) + u // 2][:, at:at + P], src[:, QT * q + u, k * P:(k + 1) * P], ident[:, :])
                    ins.then_inc(tr_n, 1)

            def ln_quarters(i, work, src=H):
                transposes(i, 0, src)
                for q in range(QN):
                    if q + 1 < QN:
                        transposes(i, q + 1, src)
                    work(q)

            def product(dst, lhs, rhs, start, stop, **more):
                pe.matmul(dst, lhs[0], rhs[0], start=start, stop=False, **more)
                pe.matmul(dst, lhs[0], rhs[1], start=False, stop=False, **more)
                return pe.matmul(dst, lhs[1], rhs[0], start=False, stop=stop, **more)

            pe.wait_ge(cbf_ok, 2)

            def latents(q):
                pe.wait_ge(w_in, 48)
                for u in range(QT):
                    if q >= 1:
                        pe.wait_ge(lat_ok, QT * (q - 1) + u + 1)
                    pe.wait_ge(hT_n, 2 * q + u // 2 + 1)
                    for k in range(KD):
                        ins = pe.matmul(bank[4 + u][:, 0:LAT], hTs[q % 2][:, k, u * P:(u + 1) * P], w_lat[:, k, :], start=(k == 0), stop=(k == KD - 1))
                    ins.then_inc(lat, 1)

            ln_quarters(0, latents)
            pe.wait_ge(hT_n, 2 * QN)
            for a in range(PAIRS):
                u = a % 2
                pe.wait_ge(wp_in[a // (PAIRS // 2)], 16)
                pe.wait_ge(wp_me, a + 1)
                pe.wait_ge(wp_ve, a + 1)
                w = wprep[:, a, :]
                wn, wk = w[:, 0:2 * QL], w[:, 2 * QL:2 * QL + 2 * KVL]
                wv, wo = w[:, 2 * QL + 2 * KVL:2 * QL + 4 * KVL], w[:, 2 * QL + 4 * KVL:]
                for e in range(2):
                    ins = pe.matmul(bank[u][0:QL, e * KVL:(e + 1) * KVL], wn[:, e * QL:(e + 1) * QL], wk[:, e * KVL:(e + 1) * KVL], start=True, stop=True)
                ins.then_inc(wp_m, 1)
                for e in range(2):
                    ins = pe.matmul(bank[2 + u][e * 64:e * 64 + 64, 0:D], wv[:, e * KVL:(e + 1) * KVL], wo[:, e * D:(e + 1) * D], start=True, stop=True)
                ins.then_inc(wp_v, 1)
            pe.wait_ge(wp_me, PAIRS + 2)
            pe.wait_ge(wp_ve, PAIRS + 2)
            pe.wait_ge(lat_ok, TILES)
            for q in range(QN):
                v = q % 2
                if q >= 2:
                    pe.wait_ge(kT_ok, q - 1)
                    pe.wait_ge(qlo_ok, q - 1)
                pe.wait_ge(qk_ready, q + 1)
                bq_, ba, bb = latent_banks[v]
                for u in range(QT):
                    at = slice(u * P, (u + 1) * P)
                    pe.transpose(bank[bq_][0:QL, at], qn[:, v, u, :], ident[:, :])
                    pe.transpose(bank[ba][:, at], kst[:, v, u, 0:2, :].rearrange("p a n -> p (a n)"), ident[:, :])
                    ins = pe.transpose(bank[bb][:, at], kst[:, v, u, 1:3, :].rearrange("p a n -> p (a n)"), ident[:, :])
                ins.then_inc(qk_tr, 1)
            pe.wait_ge(kT_ok, QN)
            pe.wait_ge(qlo_ok, QN)
            pe.wait_ge(ckv_ok, QN)

            def q_rope_mm(g, b, u, first=False):
                pe.wait_ge(wlo_ok, g + 1)
                if not first:
                    pe.wait_ge(rmul_ok, g)
                for k in (1, 2):
                    ins = product(bank[3][:, (k - 1) * SEQ:k * SEQ], [w[:, u, k, :] for w in wst], [x[:, bass.ds(SEQ * b, SEQ)] for x in qlatT], True, True)
                ins.then_inc(q_rr, 1)

            def q_abs_mm(g, b, u, first=False):
                if not first:
                    pe.wait_ge(q_abs, g)
                product(bank[2][:, 0:SEQ], [w[:, u, 0, :] for w in wst], [x[:, bass.ds(SEQ * b, SEQ)] for x in qlatT], True, True).then_inc(q_ab, 1)

            def scores(g, b, u, e, first=False):
                pe.wait_ge(q_rope, g + 1)
                pe.wait_ge(q_abs, g + 1)
                if not first:
                    pe.wait_ge(exp_ok[e], g)
                kT = (kTa, kTb)[e]
                for lo, n in ((0, P), (P, SEQ)):
                    pe.matmul(bank[e][:, lo:lo + n], qT[:, u, e, lo:lo + P], kT[:, bass.ds(SEQ * b, n)], start=True, stop=False)
                    ins = pe.matmul(bank[e][:, lo + n - P:lo + n], ident_bf, causal_bf, start=False, stop=True)
                ins.then_inc(s_mm[e], 1)

            def pt(g, u, e):
                pe.wait_ge(exp_ok[e], g + 1)
                for c in range(3):
                    ins = pe.transpose(bank[4 + e][:, c * P:(c + 1) * P], Pr[:, u, e, c * P:(c + 1) * P], ident[:, :])
                ins.then_inc(pt_mm[e], 1)

            def pv(g, b):
                for e in range(2):
                    pe.wait_ge(pt_ok[e], g + 1)
                    o0 = bank[6][:, e * KVL:(e + 1) * KVL]
                    o1 = bank[6][:, P + e * KVL:P + (e + 1) * KVL]
                    v0 = ckv[:, bass.ds(2 * b, 1), :].rearrange("p a n -> p (a n)")
                    v1 = ckv[:, bass.ds(2 * b + 1, 1), :].rearrange("p a n -> p (a n)")
                    pe.matmul(o0, PTs[:, e, 0:P], v0, start=True, stop=True)
                    pe.matmul(o1, PTs[:, e, P:2 * P], v0, start=True, stop=False)
                    ins = pe.matmul(o1, PTs[:, e, 2 * P:3 * P], v1, start=False, stop=True)
                ins.then_inc(pv_mm, 1)

            def oT(g):
                pe.wait_ge(o_ok, g + 1)
                for t in range(2):
                    ins = pe.transpose(bank[6][:, SEQ + t * P:SEQ + (t + 1) * P], o_sb[:, t, :], ident[:, :])
                ins.then_inc(oT_mm, 1)

            def proj(g, pair, done=False):
                pe.wait_ge(oT_ok, g + 1)
                w = [w[:, bass.ds(pair, 1), :].rearrange("p a n -> p (a n)") for w in Wvo2]
                for t in range(2):
                    ins = product(bank[7][:, t * D:(t + 1) * D], [o[:, t * P:(t + 1) * P] for o in oT2], w, False, done, skip_group_check=True)
                if done:
                    ins.then_inc(y_mm, 1)

            pe.wait_ge(z_ok, 1)
            for g in range(2):
                q_rope_mm(g, 0, g, g == 0)
                q_abs_mm(g, 0, g, g == 0)
            scores(0, 0, 0, 0, True)
            scores(0, 0, 0, 1, True)

            def start_sum(b):
                pe.wait_ge(y_ok, b)
                pe.matmul(bank[7][:, :], zbf[:, 0:P], zbf[:, :], start=True, stop=False, skip_group_check=True)

            def step(b, pair, u, at=None, last=False, first=False):
                g = 8 * b + pair
                nb = b + 1 if at == 7 else b
                nq = b + 1 if at in (6, 7) else b
                s_next, q_next = not (last and at == 7), not (last and at in (6, 7))
                if s_next:
                    scores(g + 1, nb, 1 - u, 0)
                if not first:
                    oT(g - 1)
                pt(g, u, 0)
                pt(g, u, 1)
                if q_next:
                    q_rope_mm(g + 2, nq, u)
                    q_abs_mm(g + 2, nq, u)
                if at == 0:
                    if not first:
                        proj(g - 1, PAIRS - 1, done=True)
                else:
                    if at == 1:
                        start_sum(b)
                    proj(g - 1, pair - 1)
                if s_next:
                    scores(g + 1, nb, 1 - u, 1)
                pv(g, b)

            def batch(b, first=False, last=False):
                step(b, 0, 0, 0, first=first)
                step(b, 1, 1, 1)
                with pe.Fori(1, 3) as i:
                    for u in range(2):
                        step(b, 2 * i + u, u)
                step(b, 6, 0, 6, last=last)
                step(b, 7, 1, 7, last=last)

            pe.wait_ge(wvo_ok, 1)
            batch(0, first=True)
            with pe.Fori(1, BATCH - 1) as b:
                batch(b)
            batch(BATCH - 1, last=True)
            oT(PAIRS * BATCH - 1)
            proj(PAIRS * BATCH - 1, PAIRS - 1, done=True)
            pe.wait_ge(b_in, 64)
            def logits(q):
                pe.wait_ge(lg_ok, q)
                for u in range(QT):
                    pe.wait_ge(hT_n, 2 * QN + 2 * q + u // 2 + 1)
                    for k in range(KD):
                        ins = pe.matmul(bank[4][:, u * (E0 + 1):(u + 1) * (E0 + 1)], hTs[q % 2][:, k, u * P:(u + 1) * P], w_rt[:, k, :], start=(k == 0), stop=(k == KD - 1))
                ins.then_inc(lg_mm, 1)

            ln_quarters(1, logits, XNP)
            pe.wait_ge(xnT_ok, QN)
            def gate_up(c, f):
                pe.wait_ge(hf_ok, FSC * c + f + 1)
                for j in range(2):
                    for k in range(KD):
                        ins = pe.matmul(bank[2 * (f % 2) + j][:, :], sw_gu[:, k, j * FSP + f * P:j * FSP + (f + 1) * P], xnT[:, k, bass.ds(512 * c, 512)],
                                        start=(k == 0), stop=(k == KD - 1))
                ins.then_inc(gu_mm, 1)

            def downs(c, first=False):
                pe.wait_ge(hf_ok, FSC * c + FSC + 2)
                for t in range(QT):
                    if not first or t >= 2:
                        pe.wait_ge(dn_ok, QT * c + t - 1)
                    for f in range(FSC):
                        ins = pe.matmul(bank[4 + t % 2][:, 0:D], hF[:, f, t * P:(t + 1) * P], sw_d[:, f, :], start=(f == 0), stop=(f == FSC - 1))
                    ins.then_inc(dn_mm, 1)

            pe.wait_ge(sw_in, 32)
            for f in range(FSC):
                gate_up(0, f)
            pe.wait_ge(mask_ok, 1)
            rank = bank[7]
            pe.matmul(rank[:, :], upper_bf, MBF[:, :, :].rearrange("p t e -> p (t e)"), start=True, stop=False)
            for t in range(TILES - 1):
                n = TILES - 1 - t
                ins = pe.matmul(rank[:, (t + 1) * E0:].rearrange("p (a e) -> p a e", a=n), ones_bf, MBF[:, t, None, :].to_broadcast([P, n, E0]),
                                start=False, stop=(t == TILES - 2))
            ins.then_inc(rank_mm, 1)
            gate_up(1, 0)
            downs(0, True)
            with pe.Fori(1, QN - 1) as c:
                for f in range(1, FSC):
                    gate_up(c, f)
                gate_up(c + 1, 0)
                downs(c)
            for f in range(1, FSC):
                gate_up(QN - 1, f)
            downs(QN - 1)
            pe.wait_ge(dn_ok, TILES)
            def rows_T(e, u, first=False):
                pe.wait_ge(xe_in[u % 4], placed(e, u))
                if not first:
                    pe.wait_ge(xe_ok, e - 1)
                for k in range(KD):
                    ins = pe.transpose(bank[u % 2][:, k * P:(k + 1) * P], Xe[:, u % 4, k * P:(k + 1) * P], ident[:, :])
                ins.then_inc(xe_tr, 1)

            def gate_up_e(e, u, first=False):
                wg = wexp[:, u % 4, 0:2 * KD * FE].rearrange("p (k n) -> p k n", k=KD)
                pe.wait_ge(xe_ok, e + 1)
                pe.wait_ge(we_in[u % 4], placed(e, u))
                if not first:
                    pe.wait_ge(he_ok, e - 1)
                for k in range(KD):
                    ins = pe.matmul(bank[2 + u % 2][:, 0:2 * FE], XeT[:, u % 2, k, :], wg[:, k, :], start=(k == 0), stop=(k == KD - 1))
                ins.then_inc(ge_mm, 1)

            def placed(e, u):
                return 4 * (e - u % 4) + 16

            def step(e, u, j, more=True):
                if more or u < 3:
                    gate_up_e(e + 1, u + 1)
                pe.wait_ge(he_ok, e + 1)
                for f in range(FEC):
                    ins = pe.transpose(bank[4 + u % 2][0:FEK, f * P:(f + 1) * P], hE[:, u % 2, f * FEK:(f + 1) * FEK], ident[:, :])
                if u < 3:
                    if u == 0:
                        pe.wait_ge(nat_in, 48 * j + 48)
                    for k in range(KD):
                        ins = pe.transpose(bank[4 + u % 2][:, D + k * P:D + (k + 1) * P], wnat[:, u, k * P:(k + 1) * P], ident[:, :])
                ins.then_inc(he_tr, 1)
                if more or u < 2:
                    rows_T(e + 2, u + 2)
                wd = wexp[:, u, 2 * KD * FE:].rearrange("p (f n) -> p f n", f=FEC)
                pe.wait_ge(heT_ok, e + 1)
                for f in range(FEC):
                    ins = pe.matmul(bank[6 + u % 2][:, 0:D], hET[0:FEK, u % 2, f * P:(f + 1) * P], wd[0:FEK, f, :], start=(f == 0), stop=(f == FEC - 1))
                ins.then_inc(ye_mm, 1)

            rows_T(0, 0, True)
            rows_T(1, 1, True)
            gate_up_e(0, 0, True)
            with pe.Fori(0, E0 // 4 - 1) as i:
                for u in range(4):
                    step(4 * i + u, u, i)
            for u in range(4):
                step(E0 - 4 + u, u, E0 // 4 - 1, False)
            pe.wait_ge(cp_in, 64)
            def qkv(q):
                pe.wait_ge(hT_n, 4 * QN + 2 * q + 2)
                h = hTs[q % 2]
                for c in range(KD):
                    if q >= 1:
                        pe.wait_ge(qk1_ok, 3 * (q - 1) + c + 1)
                    for k in range(KD):
                        ins = pe.matmul(bank[4 + c][:, :], WqT[:, k, c * P:(c + 1) * P], h[:, k, :], start=(k == 0), stop=(k == KD - 1))
                    ins.then_inc(qkv_mm, 1)
                if q >= 1:
                    pe.wait_ge(qk1_ok, 3 * q)
                for k in range(KD):
                    ins = pe.matmul(bank[6][:, :], WkT[:, k, :], h[:, k, :], start=(k == 0), stop=(k == KD - 1))
                ins.then_inc(qkv_mm, 1)
                if q >= 1:
                    pe.wait_ge(v1_ok, q)
                for u in range(QT):
                    for k in range(KD):
                        ins = pe.matmul(bank[7][:, u * HD1:(u + 1) * HD1], h[:, k, u * P:(u + 1) * P], WvT[:, k, :], start=(k == 0), stop=(k == KD - 1))
                ins.then_inc(qkv_mm, 1)

            ln_quarters(2, qkv)
            pe.wait_ge(qk1_ok, 3 * QN)
            pe.wait_ge(v1_ok, QN)

            def scores1(g, b, p, e, first=False):
                if e == 0 and p % 4 == 0:
                    pe.wait_ge(kbd_ok, b + 1)
                    pe.wait_ge(qst_ok, 2 * b + p // 4 + 1)
                if not first:
                    pe.wait_ge(exp1_ok[e], g - 1)
                sc = bank[2 * (p % 2) + e]
                for lo, n in ((0, P), (P, SEQ)):
                    pe.matmul(sc[:, lo:lo + n], qst[:, p // 4, lo:lo + P], Kbd[:, bass.ds(b % 2, 1), 2 * (p % 4) + e, 0:n].rearrange("p a s -> p (a s)"), start=True, stop=False)
                    ins = pe.matmul(sc[:, lo + n - P:lo + n], ident_bf, strict_bf, start=False, stop=True)
                ins.then_inc(s1_mm[e], 1)

            def pt1(g, p, e):
                pe.wait_ge(exp1_ok[e], g + 1)
                pe.wait_ge(pt1_ok[e], g)
                for c in range(3):
                    ins = pe.transpose(bank[4 + e][:, c * P:(c + 1) * P], Pr[:, p % 2, e, c * P:(c + 1) * P], ident[:, :])
                ins.then_inc(pt1_mm[e], 1)

            def pv1(g, b, p):
                v0, v1 = (vall[:, bass.ds(2 * b + t, 1), :].rearrange("p a n -> p (a n)") for t in range(2))
                for e in range(2):
                    pe.wait_ge(pt1_ok[e], g + 1)
                    at = (2 * p + e) * HD1
                    o0, o1 = bank[6][:, at:at + HD1], bank[6][:, D + at:D + at + HD1]
                    PT = PTc[p % 2][:, e, :]
                    pe.matmul(o0, PT[:, 0:P], v0, start=True, stop=True)
                    pe.matmul(o1, PT[:, P:2 * P], v0, start=True, stop=False)
                    ins = pe.matmul(o1, PT[:, 2 * P:3 * P], v1, start=False, stop=True)
                ins.then_inc(pv1_mm, 1)

            def outputs_T(b):
                pe.wait_ge(o1_ok, b + 1)
                pe.wait_ge(y1_ok, b)
                for c in range(KD):
                    for t in range(2):
                        ins = pe.transpose(bank[7][:, c * SEQ + t * P:c * SEQ + (t + 1) * P], oC_sb[:, t, c * P:(c + 1) * P], ident[:, :])
                ins.then_inc(oT1_mm, 1)

            def proj1(b):
                pe.wait_ge(oT1_ok, b + 1)
                for t in range(2):
                    for c in range(KD):
                        ins = pe.matmul(bank[7][:, t * D:(t + 1) * D], oTC_sb[:, c, t * P:(t + 1) * P], WoT[:, c, :], start=(c == 0), stop=(c == KD - 1))
                ins.then_inc(y1_mm, 1)

            def step(b, p, more=True, before=True):
                g = 8 * b + p
                if more:
                    for e in range(2):
                        scores1(g + 1, b + 1 if p == 7 else b, (p + 1) % 8, e)
                for e in range(2):
                    pt1(g, p, e)
                if not more:
                    transposes(3, 0)
                    transposes(3, 1)
                if before and p == 2:
                    outputs_T(b - 1)
                if before and p == 4:
                    proj1(b - 1)
                if before and p == 0:
                    pv1(g - 1, b - 1, 7)
                elif p > 0:
                    if before and p == 1:
                        pe.wait_ge(o1_ok, b)
                    pv1(g - 1, b, p - 1)

            scores1(0, 0, 0, 0, True)
            scores1(0, 0, 0, 1, True)
            for p in range(8):
                step(0, p, before=False)
            with pe.Fori(1, BATCH - 1) as b:
                for p in range(8):
                    step(b, p)
            for p in range(8):
                step(BATCH - 1, p, more=p < 7)
            pv1(8 * BATCH - 1, BATCH - 1, 7)
            outputs_T(BATCH - 1)
            proj1(BATCH - 1)
            transposes(3, 2)
            def gate_up1(c, f):
                pe.wait_ge(up1_ok, IC * c + f + 1)
                for j, wT in enumerate((gateT, upT)):
                    for k in range(KD):
                        ins = product(bank[2 * (f % 2) + j][:, :], [w[:, k, f * P:(f + 1) * P] for w in wT], [h[:, k, bass.ds(512 * c, 512)] for h in hTall], k == 0, k == KD - 1)
                ins.then_inc(gu1_mm, 1)

            def downs1(c, first=False):
                pe.wait_ge(hf1_ok, IC * c + IC + 2)
                for t in range(QT):
                    if not first or t >= 2:
                        pe.wait_ge(dn1_ok, QT * c + t - 1)
                    for f in range(IC):
                        ins = product(bank[4 + t % 2][:, 0:D], [h[f][:, t * P:(t + 1) * P] for h in hFD], [w[:, f, :] for w in downT], f == 0, f == IC - 1)
                    ins.then_inc(dn1_mm, 1)

            pe.wait_ge(hT_n, 6 * QN + 2 * 3)
            for f in range(IC):
                if f == 2:
                    transposes(3, 3)
                gate_up1(0, f)
            gate_up1(1, 0)
            downs1(0, True)
            pe.wait_ge(hT_n, 8 * QN)
            with pe.Fori(1, QN - 1) as c:
                for f in range(1, IC):
                    gate_up1(c, f)
                gate_up1(c + 1, 0)
                downs1(c)
            for f in range(1, IC):
                gate_up1(QN - 1, f)
            downs1(QN - 1)


def layouts(inputs):
    a = {k: np.ascontiguousarray(v) for k, v in inputs.items()}
    f = np.float32
    d = {}
    d["x"] = a["L0_attn_x"].reshape(TILES, P, D).transpose(1, 0, 2)
    r = np.arange(P)
    tri = r[:, None] - r[None, :]
    d["cst"] = np.stack([np.eye(P), np.where(tri >= 0, 0.0, NEG), np.where(tri > 0, 0.0, NEG), np.where(tri < 0, 1.0, 0.0), np.ones((P, P))], 1).astype(f)
    inv = (1.0 / np.float32(10000.0) ** (np.arange(0, ROPE, 2, dtype=f) / f(ROPE))).astype(f)
    ang = np.outer(np.arange(SEQ, dtype=f), inv).astype(f)
    ang = np.concatenate([ang, ang], -1)
    cos, sin = np.cos(ang).astype(f), np.sin(ang).astype(f)
    sin = sin * np.where(np.arange(ROPE) % 2 == 0, -1, 1).astype(f)
    d["rope_q"] = np.stack([np.tile(cos.T, (2, 1)), np.tile(sin.T, (2, 1))], 1)
    d["rope_k"] = np.stack([cos, sin], 1).reshape(KD, P, 2, ROPE).transpose(1, 0, 2, 3)
    swap = np.arange(ROPE) ^ 1
    kva = a["L0_attn_w_kva"]
    d["w_lat"] = np.concatenate([a["L0_attn_w_qa"], kva, kva[:, KVL:][:, swap]], 1).reshape(KD, P, LAT).transpose(1, 0, 2)
    vecs = np.zeros((P, KVL + 2), f)
    vecs[:, 0:KVL] = a["L0_attn_kv_a_norm_w"][None]
    vecs[:, KVL] = np.tile(a["L0_attn_kv_a_norm_w"], 2)
    vecs[:QL, KVL + 1] = a["L0_attn_q_a_norm_w"]
    d["vecs"] = vecs
    wqb = a["L0_attn_w_qb"].reshape(QL, PAIRS, 2, NOPE + ROPE)
    rp = wqb[:, :, ::-1, NOPE:]
    d["w_rope"] = np.stack([rp, rp[..., swap]], 2).reshape(QL, PAIRS, 2, P)
    wkvb = a["L0_attn_w_kvb"].reshape(KVL, PAIRS, 2, NOPE + DV)
    wo = a["L0_attn_w_o"].reshape(PAIRS, 2, DV, D)
    d["wprep"] = np.concatenate([
        wqb[..., :NOPE].transpose(1, 3, 2, 0).reshape(PAIRS, P, 2 * QL),
        wkvb[..., :NOPE].transpose(1, 3, 2, 0).reshape(PAIRS, P, 2 * KVL),
        wkvb[..., NOPE:].transpose(1, 3, 2, 0).reshape(PAIRS, P, 2 * KVL),
        wo.transpose(0, 2, 1, 3).reshape(PAIRS, P, 2 * D)], 2).transpose(1, 0, 2)
    d["w_rt"] = np.concatenate([a["L0_ffn_w_router"], a["L0_ffn_w_shared_gate"]], 1).reshape(KD, P, E0 + 1).transpose(1, 0, 2)
    d["wn_bc"] = np.tile(a["L0_ffn_w_norm"][None], (P, 1))
    swg = np.zeros((D, 2, FSP), f)
    swg[:, 0, :FS], swg[:, 1, :FS] = a["L0_ffn_sw_gate"], a["L0_ffn_sw_up"]
    d["sw_gu"] = swg.reshape(KD, P, 2 * FSP).transpose(1, 0, 2)
    swd = np.zeros((FSC * P, D), f)
    swd[:FS] = a["L0_ffn_sw_down"]
    d["sw_d"] = swd.reshape(FSC, P, D).transpose(1, 0, 2)
    t, e, p = np.arange(TILES), np.arange(E0), np.arange(P)
    spare = SLOTS + (t[None, :, None] * E0 + e[None, None, :]) * P + p[:, None, None]
    d["slot_c"] = np.stack([np.broadcast_to(e[None, None] + 1, spare.shape), spare + 1], 1).astype(f)
    d["tok_i"] = (t[None, :] * P + p[:, None]).astype(np.int32)
    d["spare"] = np.tile((TOK + p)[:, None], (1, E0)).astype(np.int32)
    gu = np.stack([a["L0_ffn_w_gate"], a["L0_ffn_w_up"]], 1).reshape(E0, 2, KD, P, FE).transpose(0, 3, 2, 1, 4).reshape(E0, P, 2 * KD * FE)
    dn = np.zeros((E0, P, FEC, D), f)
    dn[:, :FEK] = a["L0_ffn_w_down"].reshape(E0, FEC, FEK, D).transpose(0, 2, 1, 3)
    d["wexp"] = np.concatenate([gu, dn.reshape(E0, P, FEC * D)], 2)
    n = np.arange(P * ROWS * SPAN).reshape(P * ROWS, SPAN)
    pos = np.linspace(0.0, NCTRL - 1.0, INTER * D, dtype=np.float64)
    pos = np.concatenate([pos, np.full(n.size - pos.size, pos[-1])])[n]
    cell = np.clip(np.floor(pos).astype(np.int64), 0, NCTRL - 2)
    row = np.arange(P * ROWS)[:, None]
    real = n < INTER * D
    assert np.all((cell == row) | (cell == row - 1) | ~real) and np.all((cell == row)[:, ALT:] | ~real[:, ALT:])
    own = np.where(cell == row, pos - row, 0.0).astype(f)
    was = np.where((cell == row - 1) & real, pos - (row - 1), 0.0).astype(f)[:, :ALT]
    d["frac"] = own.reshape(P, ROWS, SPAN)
    d["fracb"] = np.stack([was.reshape(P, ROWS, ALT), ((cell == row - 1) & real)[:, :ALT].astype(f).reshape(P, ROWS, ALT)], 1)
    at = np.clip(ROWS * p[:, None] - 2 + np.arange(ROWS + 4)[None], 0, NCTRL - 1)
    d["cpw"] = np.stack([a[k][at] for k in ("L1_ffn_gate_cp", "L1_ffn_up_cp", "L1_ffn_down_cp")], 1)
    split = lambda w: w.T.reshape(KD, P, -1).transpose(1, 0, 2).reshape(P, -1)
    bc = lambda v: np.tile(v[None], (P, 1))
    d["wC"] = np.concatenate([
        split(a["L1_attn_Wq"]), split(a["L1_attn_Wo"]), split(np.tile(a["L1_attn_Wk"], (8, 1))), split(a["L1_attn_Wv"]), bc(a["L1_attn_bo"]), bc(a["L1_attn_bv"]),
        a["L1_attn_bq"].reshape(KD, P).T, np.tile(a["L1_attn_bk"], 8)[:, None], (p[:, None] > 0).astype(f), (p[:, None] // HD1 == np.arange(8)[None]).astype(f)], 1)
    return {k: np.ascontiguousarray(v) for k, v in d.items()}


def kernel(**inputs):
    import concourse.bacc as bacc
    from concourse.bass_utils import run_bass_kernel_spmd

    nc = bacc.Bacc("TRN2", target_bir_lowering=False, num_devices=1)
    arrays = layouts(inputs)
    T = {k: nc.dram_tensor(f"in_{k}", v.shape, mybir.dt.from_np(v.dtype), kind="ExternalInput").ap() for k, v in arrays.items()}
    out = nc.dram_tensor("out_x", (P, TILES, D), F32, kind="ExternalOutput").ap()
    build_program(nc, T, out)
    r = run_bass_kernel_spmd(nc, [{f"in_{k}": v for k, v in arrays.items()}], core_ids=[0])
    return r.results[0]["out_x"].transpose(1, 0, 2).reshape(BATCH, SEQ, D)
```
